# Optimizing a Trainium2 kernel written in Bass

```python
import numpy as np
import jax
import jax.numpy as jnp

def _softmax(x, axis=-1):
    return jax.nn.softmax(x, axis=axis)

def _gelu(x):
    return jax.nn.gelu(x, approximate=True)

def _silu(x):
    return jax.nn.silu(x)

def _sigmoid(x):
    return jax.nn.sigmoid(x)

def _layernorm(x, axis=-1, eps=1e-05):
    m = jnp.mean(x, axis=axis, keepdims=True)
    v = jnp.var(x, axis=axis, keepdims=True)
    return (x - m) / jnp.sqrt(v + eps)

def _scatter_add(tgt, idx, src, axis=0):
    return tgt.at[idx].add(src)

def _segment_sum(src, seg, n):
    return jax.ops.segment_sum(src, seg, n)
kernel_name = 'mk_flamingo_gated_d1_seqx_r4_231fa4'

def setup_inputs(seed: int=0):
    np.random.seed(seed)
    _w = jnp.asarray

    def _rec_inputs():
        import jax
        import jax.numpy as jnp
        _rk = jax.random.key(seed)
        x = -0.0002928 + 1 * jax.random.normal(jax.random.fold_in(_rk, 1), (8, 512, 256), jnp.float32)
        _lenS = 512 - jax.random.randint(jax.random.fold_in(_rk, 7), (8,), 0, max(1, 512 // 4) + 1, jnp.int32)
        _lenS2 = 512 - jax.random.randint(jax.random.fold_in(_rk, 8), (8,), 0, max(1, 512 // 4) + 1, jnp.int32)
        _ctx_1024P = jax.random.normal(jax.random.fold_in(_rk, 11), (8, 16, 256), jnp.float32)
        _ctx_1024c = jax.random.dirichlet(jax.random.fold_in(_rk, 511), 0.3 * jnp.ones((16,), jnp.float32), (8, 512))
        _ctx_1024t = jnp.einsum('bsk,bkd->bsd', _ctx_1024c, _ctx_1024P)
        _ctx_1024t = _ctx_1024t * jax.lax.rsqrt(jnp.mean(jnp.square(_ctx_1024t)) + 1e-12) * 0.953939
        ctx_1024 = 0.000227908 + 0.99994 * (_ctx_1024t + 0.3 * jax.random.normal(jax.random.fold_in(_rk, 611), (8, 512, 256), jnp.float32))
        _g = jax.random.normal(jax.random.fold_in(_rk, 9001), (2, 1), jnp.float32)
        _g = jnp.sign(_g) * jnp.maximum(jnp.abs(_g), 1.0) + (_g == 0) * 1.0
        g_xattn = _g[0]
        g_ffn = _g[1]
        return (x, ctx_1024, g_xattn, g_ffn)
    x, ctx_1024, g_xattn, g_ffn = _rec_inputs()

    def _L0_xattn_setup():
        import jax, jax.numpy as jnp
        import numpy as np
        HEADS = 16
        key = jax.random.key(seed)
        ks = jax.random.split(key, 6)
        b, n, m, dim = (2, 512, 128, 256)
        s = dim ** (-0.5)
        return {'x': jax.random.normal(ks[0], (b, n, dim), jnp.float32), 'mem': jax.random.normal(ks[1], (b, m, dim), jnp.float32), 'Wq': jax.random.normal(ks[2], (dim, dim), jnp.float32) * s, 'Wkv': jax.random.normal(ks[3], (dim, 2 * dim), jnp.float32) * s, 'Wout': jax.random.normal(ks[4], (dim, dim), jnp.float32) * s, 'bout': jnp.zeros((dim,), jnp.float32)}
    _L0_xattn_all = _L0_xattn_setup()
    _L0_xattn_in = {k: v for k, v in _L0_xattn_all.items() if k in ('Wq', 'Wkv', 'Wout', 'bout')}
    del _L0_xattn_all

    def _L0_ffn_setup():
        import jax, jax.numpy as jnp
        import numpy as np
        E, D, F, GATE_DIM = (8, 256, 1024, 16)
        B, T = (2, 512)
        key = jax.random.key(seed)
        ks = jax.random.split(key, 7)
        s = 0.02
        return {'hidden_states': jax.random.normal(ks[0], (B, T, D), dtype=jnp.float32), 'w_red': jax.random.normal(ks[1], (D, GATE_DIM), dtype=jnp.float32) * s, 'wg': jax.random.normal(ks[2], (E, GATE_DIM), dtype=jnp.float32), 'w1': jax.random.normal(ks[3], (E, D, F), dtype=jnp.float32) * s, 'b1': jax.random.normal(ks[4], (E, F), dtype=jnp.float32) * s, 'w2': jax.random.normal(ks[5], (E, F, D), dtype=jnp.float32) * s, 'b2': jax.random.normal(ks[6], (E, D), dtype=jnp.float32) * s}
    _L0_ffn_all = _L0_ffn_setup()
    _L0_ffn_in = {k: v for k, v in _L0_ffn_all.items() if k in ('w_red', 'wg', 'w1', 'b1', 'w2', 'b2')}
    del _L0_ffn_all
    return {'x': x, 'ctx_1024': ctx_1024, 'g_xattn': g_xattn, 'g_ffn': g_ffn, 'L0_xattn_Wq': _L0_xattn_in['Wq'], 'L0_xattn_Wkv': _L0_xattn_in['Wkv'], 'L0_xattn_Wout': _L0_xattn_in['Wout'], 'L0_xattn_bout': _L0_xattn_in['bout'], 'L0_ffn_w_red': _L0_ffn_in['w_red'], 'L0_ffn_wg': _L0_ffn_in['wg'], 'L0_ffn_w1': _L0_ffn_in['w1'], 'L0_ffn_b1': _L0_ffn_in['b1'], 'L0_ffn_w2': _L0_ffn_in['w2'], 'L0_ffn_b2': _L0_ffn_in['b2']}

def reference(x, ctx_1024, g_xattn, g_ffn, L0_xattn_Wq, L0_xattn_Wkv, L0_xattn_Wout, L0_xattn_bout, L0_ffn_w_red, L0_ffn_wg, L0_ffn_w1, L0_ffn_b1, L0_ffn_w2, L0_ffn_b2):
    import jax
    import jax.numpy as jnp

    def _L0_xattn_ref(x, mem, Wq, Wkv, Wout, bout):
        import jax, jax.numpy as jnp
        import numpy as np
        HEADS = 16
        b, n, dim = x.shape
        h = HEADS
        d = dim // h
        scale = d ** (-0.5)
        mem_len = mem.shape[1]
        q = x @ Wq
        xc = jnp.concatenate((mem, x), axis=1)
        kv = xc @ Wkv
        k, v = jnp.split(kv, 2, axis=-1)

        def to_heads(t):
            bb, nn, _ = t.shape
            return t.reshape(bb, nn, h, d).transpose(0, 2, 1, 3)
        q, k, v = (to_heads(q), to_heads(k), to_heads(v))
        dots = jnp.einsum('bhid,bhjd->bhij', q, k) * scale
        j = dots.shape[-1]
        i_idx = jnp.arange(n)[:, None]
        j_idx = jnp.arange(j)[None, :]
        mask = j_idx > i_idx + mem_len
        dots = jnp.where(mask[None, None], -jnp.inf, dots)
        attn = jax.nn.softmax(dots, axis=-1)
        out = jnp.einsum('bhij,bhjd->bhid', attn, v)
        out = out.transpose(0, 2, 1, 3).reshape(b, n, dim)
        return out @ Wout + bout

    def _L0_ffn_ref(hidden_states, w_red, wg, w1, b1, w2, b2):
        import jax, jax.numpy as jnp
        import numpy as np
        E, D, F, GATE_DIM = (8, 256, 1024, 16)
        B, T = (2, 512)
        b, t, c = hidden_states.shape
        x = hidden_states.reshape(-1, c)
        red = x @ w_red
        wg_n = wg / jnp.maximum(jnp.linalg.norm(wg, axis=1, keepdims=True), 0.0001)
        logits = red @ wg_n.T
        gates = jax.nn.softmax(logits, axis=1)
        idx = jnp.argmax(gates, axis=1)
        scores = jnp.take_along_axis(gates, idx[:, None], axis=1)
        h = jax.nn.gelu(jnp.einsum('td,edf->etf', x, w1) + b1[:, None, :], approximate=False)
        y = jnp.einsum('etf,efd->etd', h, w2) + b2[:, None, :]
        out = jnp.take_along_axis(y, idx[None, :, None], axis=0)[0]
        out = out * scores
        return out.reshape(b, t, c)
    x = x + jnp.tanh(g_xattn[0]) * _L0_xattn_ref(_layernorm(x, axis=-1), ctx_1024, L0_xattn_Wq, L0_xattn_Wkv, L0_xattn_Wout, L0_xattn_bout)
    x = x + jnp.tanh(g_ffn[0]) * _L0_ffn_ref(_layernorm(x, axis=-1), L0_ffn_w_red, L0_ffn_wg, L0_ffn_w1, L0_ffn_b1, L0_ffn_w2, L0_ffn_b2)
    return x

_drawn_inputs = setup_inputs


def setup_inputs(seed=0):
    import zlib

    import numpy as np

    out = dict(_drawn_inputs(seed))
    spreads = {'L0_xattn_bout': (0.0, 0.1)}
    factors = {'L0_ffn_w_red': 3.105,
     'L0_ffn_wg': 3.104,
     'L0_ffn_w1': 3.033,
     'L0_ffn_b1': 8.0,
     'L0_ffn_w2': 2.951,
     'L0_ffn_b2': 8.0}
    for name, (base, spread) in spreads.items():
        noise = np.random.default_rng([zlib.crc32(name.encode()), seed]).standard_normal(out[name].shape)
        drawn = base * np.exp(spread * noise) if base else spread * noise
        out[name] = jnp.asarray(drawn.astype(out[name].dtype))
    for name, factor in factors.items():
        out[name] = (out[name] * factor).astype(out[name].dtype)
    return out
```

```python
from contextlib import ExitStack

import concourse.bass as bass
from concourse import mybir

F32 = mybir.dt.float32
BF16 = mybir.dt.bfloat16
I32 = mybir.dt.int32
U32 = mybir.dt.uint32
ALU = mybir.AluOpType
ACT = mybir.ActivationFunctionType
AX = mybir.AxisListType

P = 128
B, T, D = 8, 512, 256
TM = 512
KEYS = TM + T
HEADS, DH = 16, 16
QUADS = 4
HQ = HEADS // QUADS
NB = T // P
KB = KEYS // P
KC = D // P
HALVES = 2
COLS = T + KEYS
EPS = 1e-5
SCALE = DH ** -0.5
Q_PART = (0, 0, 1, 1, 0, 2)
K_PART = (0, 1, 0, 1, 2, 0)
TERMS = len(Q_PART)
SROWS = TERMS * DH
MROWS = 2 * HQ
E, FF, GD = 8, 1024, 16
FC = FF // P
TOK = B * T
CAP = TOK + P
DUMMY = E * CAP
ROW = D + 4
TILES = 40
NOTOK = 1 << 20
MASKED = -1e30


class Count:

    def __init__(self, sem, base=0):
        self.sem, self.base, self.n = sem, base, 0

    def add(self, ins, k=1):
        ins.then_inc(self.sem, k)
        self.n += k
        return ins

    def wait(self, eng):
        eng.wait_ge(self.sem, self.base + self.n)


def peel(count, body):
    for p in range(count):
        body(p)


def wait(eng, sem, value):
    if not isinstance(value, int) or value > 0:
        eng.wait_ge(sem, value)


def project(nc, c, x, ctx, wq, wkv, parts_d, v_d):
    with ExitStack() as s:
        def sb(name, shape, dt):
            return s.enter_context(nc.sbuf_tensor(name, shape, dt))

        def sem(name):
            return s.enter_context(nc.semaphore(name))

        wq_s = sb("wq_s", [P, KC, D], F32)
        wkv_s = sb("wkv_s", [P, KC, 2 * D], F32)
        xc = [sb(f"xc{p}", [P, KB, D], F32) for p in range(2)]
        st = sb("st1", [P, NB, 6], F32)
        mv = sb("mv1", [P, NB, 2], F32)
        ve = sb("ve1", [P, NB], F32)
        rs = sb("rs1", [P, NB], F32)
        xcT = sb("xcT", [P, KC, KEYS], F32)
        part = [sb(f"part{p}", [P, 3, COLS], BF16) for p in range(HALVES)]
        rest = [sb(f"rest{p}", [P, T], F32) for p in range(2)]
        vs = sb("vs", [P, QUADS, KB, HQ, 32], F32)
        psT = [s.enter_context(nc.psum_tensor(f"psT{p}", [P, 512], F32)) for p in range(2)]
        psQ = [s.enter_context(nc.psum_tensor(f"psQ{p}", [P, 512], F32)) for p in range(3)]
        psV = [s.enter_context(nc.psum_tensor(f"psV{p}", [P, 2, D], F32)) for p in range(2)]

        w_in = sem("w_in")
        x_in = [sem(f"x_in{p}") for p in range(2)]
        stat_done, mean_done, var_done, rstd_done, norm_done = (
            sem(n) for n in ("stat_done", "mean_done", "var_done", "rstd_done", "norm_done"))
        tr_done, tr_out = sem("tr_done"), sem("tr_out")
        qk_done, first_out, rest_out, second_out, third_out = (
            sem(n) for n in ("qk_done", "first_out", "rest_out", "second_out", "third_out"))
        v_done, v_out = sem("v_done"), sem("v_out")
        ones_set = sem("ones_set")
        passed_pool, passed_dve = sem("passed_pool1"), sem("passed_dve1")
        part_st = [sem(f"part_st{h}") for h in range(HALVES)]
        v_st = sem("v_st")
        UN = 3 * HALVES

        with nc.Block() as block:
            @block.sync
            def _(sp):
                sp.dma_start(wq_s[:], wq.rearrange("(c p) n -> p c n", p=P)).then_inc(w_in, 16)
                sp.dma_start(wkv_s[:], wkv.rearrange("(c p) n -> p c n", p=P)).then_inc(w_in, 16)

                def load(b, p):
                    sp.dma_start(xc[p][:, 0:NB, :], ctx[bass.ds(b, 1)].rearrange("a (n p) d -> p (a n) d", p=P)).then_inc(x_in[p], 16)
                    sp.dma_start(xc[p][:, NB:KB, :], x[bass.ds(b, 1)].rearrange("a (n p) d -> p (a n) d", p=P)).then_inc(x_in[p], 16)

                load(0, 0)
                load(1, 1)

                def store(b):
                    for hf in range(HALVES):
                        wait(sp, third_out, UN * b + 3 * (hf + 1))
                        sp.wait_ge(first_out, UN * b + 3 * (hf + 1))
                        sp.dma_start(parts_d[bass.ds(b, 1), hf].rearrange("a c p n -> p (a c) n"), part[hf][:]).then_inc(part_st[hf], 16)
                    wait(sp, v_out, 4 * b + 4)
                    sp.dma_start(v_d[bass.ds(b, 1)].rearrange("a p n -> p (a n)"),
                                 vs[:].rearrange("p a b c d -> p (a b c d)")).then_inc(v_st, 16)

                with sp.Fori(0, B // 2 - 1) as i:
                    for p in range(2):
                        b = 2 * i + p
                        sp.wait_ge(tr_done, 4 * b + 4)
                        load(b + 2, p)
                        store(b)
                for p in range(2):
                    store(B - 2 + p)
                for hf in range(HALVES):
                    wait(sp, part_st[hf], 16 * B)
                wait(sp, v_st, 16 * B)

            @block.gpsimd
            def _(pool):
                pool.memset(vs[:], 1.0).then_inc(ones_set, 1)

                def body(b, p):
                    pool.wait_ge(mean_done, b + 1)
                    pool.sem_inc(passed_pool, 1)
                    pool.tensor_scalar(ve[:], mv[:, :, 1], EPS, None, ALU.add).then_inc(var_done, 1)
                    pool.wait_ge(var_done, b + 1)
                    pool.tensor_tensor(rs[:], ve[:], c["mhalf"][:, 0:NB], ALU.pow).then_inc(rstd_done, 1)
                    for u in range(UN):
                        hf, k = divmod(u, 3)
                        r = rest[u % 2]
                        wait(pool, rest_out, UN * b + u + 1)
                        pool.sem_inc(passed_pool, 1)
                        pool.tensor_copy(part[hf][:, 1, k * 512:(k + 1) * 512], r[:]).then_inc(second_out, 1)
                        pool.wait_ge(second_out, UN * b + u + 1)
                        pool.tensor_tensor(part[hf][:, 2, k * 512:(k + 1) * 512], r[:],
                                           part[hf][:, 1, k * 512:(k + 1) * 512], ALU.subtract).then_inc(third_out, 1)

                peel(2, lambda p: body(p, p))
                with pool.Fori(1, B // 2) as i:
                    for p in range(2):
                        body(2 * i + p, p)

            @block.vector
            def _(dve):
                def body(i, p):
                    b = 2 * i + p
                    X = xc[p][:, NB:KB, :]
                    dve.wait_ge(x_in[p], 32 * i + 32)
                    for n in range(NB):
                        dve.bn_stats(st[:, n, :], X[:, n, :]).then_inc(stat_done, 1)
                    dve.wait_ge(stat_done, NB * b + NB)
                    dve.sem_inc(passed_dve, 1)
                    for n in range(NB):
                        ins = dve.bn_aggr(mv[:, n, :], st[:, n, :])
                    ins.then_inc(mean_done, 1)
                    dve.wait_ge(mean_done, b + 1)
                    dve.wait_ge(rstd_done, b + 1)
                    for n in range(NB):
                        ins = dve.tensor_scalar(X[:, n, :], X[:, n, :], mv[:, n, 0:1], rs[:, n:n + 1], ALU.subtract, ALU.mult)
                    ins.then_inc(norm_done, 1)
                    for u in range(UN):
                        hf, k = divmod(u, 3)
                        dve.wait_ge(first_out, UN * b + u + 1)
                        wait(dve, third_out, UN * b + max(u - 1, 0))
                        dve.scalar_tensor_tensor(rest[u % 2][:], psQ[u % 3][:], SCALE if k == 0 else 1.0,
                                                 part[hf][:, 0, k * 512:(k + 1) * 512], ALU.mult, ALU.subtract).then_inc(rest_out, 1)

                peel(2, lambda p: body(0, p))
                with dve.Fori(1, B // 2) as i:
                    for p in range(2):
                        body(i, p)

            @block.scalar
            def _(act):
                def body(i, p):
                    b = 2 * i + p
                    for t in range(4):
                        act.wait_ge(tr_done, 4 * b + t + 1)
                        k, half = t // 2, t % 2
                        act.activation(xcT[:, k, half * 512:(half + 1) * 512], psT[t % 2][:], ACT.Copy).then_inc(tr_out, 1)
                    for u in range(UN):
                        hf, k = divmod(u, 3)
                        act.wait_ge(qk_done, UN * b + u + 1)
                        if k == 0:
                            wait(act, part_st[hf], 16 * b)
                        act.activation(part[hf][:, 0, k * 512:(k + 1) * 512], psQ[u % 3][:], ACT.Copy,
                                       scale=SCALE if k == 0 else 1.0).then_inc(first_out, 1)
                    wait(act, v_st, 16 * b)
                    for t in range(4):
                        act.wait_ge(v_done, 4 * b + t + 1)
                        for n in range(2):
                            ins = act.activation(vs[:, :, 2 * t + n, :, 0:DH],
                                                 psV[t % 2][:, n, :].rearrange("p (q h d) -> p q h d", q=QUADS, h=HQ), ACT.Copy)
                        ins.then_inc(v_out, 1)
                act.wait_ge(ones_set, 1)
                peel(2, lambda p: body(0, p))
                with act.Fori(1, B // 2) as i:
                    for p in range(2):
                        body(i, p)

            @block.tensor
            def _(pe):
                pe.wait_ge(w_in, 32)

                def body(i, p):
                    b = 2 * i + p
                    for t in range(4):
                        k, half = t // 2, t % 2
                        if t == 0:
                            pe.wait_ge(x_in[p], 32 * i + 32)
                        if t == 1:
                            pe.wait_ge(norm_done, b + 1)
                        wait(pe, tr_out, 4 * b + max(t - 1, 0))
                        for n in range(NB):
                            ins = pe.transpose(psT[t % 2][:, n * P:(n + 1) * P],
                                               xc[p][:, NB * half + n, k * P:(k + 1) * P], c["ident"][:])
                        ins.then_inc(tr_done, 1)
                    wait(pe, tr_out, 4 * b + 4)
                    for u in range(UN):
                        hf, k = divmod(u, 3)
                        wait(pe, rest_out, UN * b + max(u - 2, 0))
                        for kc in range(KC):
                            w = wq_s[:, kc, hf * P:(hf + 1) * P] if k == 0 else wkv_s[:, kc, hf * P:(hf + 1) * P]
                            cols = slice(TM, KEYS) if k == 0 else slice((k - 1) * 512, k * 512)
                            ins = pe.matmul(psQ[u % 3][:], w, xcT[:, kc, cols], start=kc == 0, stop=kc == KC - 1)
                        ins.then_inc(qk_done, 1)
                    for t in range(4):
                        wait(pe, v_out, 4 * b + max(t - 1, 0))
                        for n in range(2):
                            for kc in range(KC):
                                ins = pe.matmul(psV[t % 2][:, n, :], xcT[:, kc, (2 * t + n) * P:(2 * t + n + 1) * P],
                                                wkv_s[:, kc, D:2 * D], start=kc == 0, stop=kc == KC - 1)
                        ins.then_inc(v_done, 1)

                peel(2, lambda p: body(0, p))
                with pe.Fori(1, B // 2) as i:
                    for p in range(2):
                        body(i, p)


def attend(nc, c, x, parts_d, v_d, rows_d):
    N_M = 3
    N_T = 18
    N_TL = 7
    with ExitStack() as s:
        def sb(name, shape, dt):
            return s.enter_context(nc.sbuf_tensor(name, shape, dt))

        def sem(name):
            return s.enter_context(nc.semaphore(name))

        qs = [sb(f"qs{q}", [P, HQ, T], BF16) for q in range(QUADS)]
        ks = [sb(f"ks{q}", [P, HQ, KEYS], BF16) for q in range(QUADS)]
        vq = [sb(f"vq{q}", [P, KB, HQ, 32], F32) for q in range(QUADS)]
        pr = [sb(f"pr{p}", [P, HQ, 1024], F32) for p in range(2)]
        mx = sb("mx", [P, NB, HQ, 2], F32)
        nm = sb("nm", [P, NB, HQ], F32)
        mp = sb("mp", [P, NB, 2, HQ], BF16)
        mT = [sb(f"mT{p}", [MROWS, T], BF16) for p in range(2)]
        osb = sb("osb", [P, T], F32)
        lsum = sb("lsum", [P, T], F32)
        linv = sb("linv", [P, T], F32)
        ot = [sb(f"ot{q}", [P, T], F32) for q in range(QUADS)]
        xres = sb("xres", [P, NB, D], F32)
        row = sb("row", [P, NB, ROW], F32)
        st = sb("st2", [P, NB, 6], F32)
        mv = sb("mv2", [P, NB, 2], F32)
        ve = sb("ve2", [P, NB], F32)
        rs = sb("rs2", [P, NB], F32)
        hn = sb("hn", [P, NB, D], F32)
        hT = sb("hT", [P, KC, T], F32)
        redT = sb("redT", [GD, T], F32)
        lg = sb("lg", [P, NB, E], F32)
        lmax = sb("lmax", [P, NB], F32)
        dif = sb("dif", [P, NB, E], F32)
        ex = sb("ex", [P, NB, E], F32)
        esum = sb("esum", [P, NB], F32)
        einv = sb("einv", [P, NB], F32)
        eq = sb("eq", [P, NB, E], F32)
        cand = sb("cand", [P, NB, E], F32)
        cmin = sb("cmin", [P, NB], F32)
        oh = sb("oh", [P, NB, E], BF16)
        cumr = sb("cumr", [P, NB, E], F32)
        pick = sb("pick", [P, NB, E], F32)
        slot = sb("slot", [P, NB], F32)
        slots = [sb(f"slots{n}", [P, 1], U32) for n in range(NB)]

        psS = [s.enter_context(nc.psum_tensor(f"psS{p}", [P, 1024], F32)) for p in range(2)]
        psA = [s.enter_context(nc.psum_tensor(f"psA{p}", [P, 512], F32)) for p in range(2)]
        psO = s.enter_context(nc.psum_tensor("psO", [P, 512], F32))
        psM = s.enter_context(nc.psum_tensor("psM", [P, 512], F32))

        stk_in = [sem(f"stk_in{q}") for q in range(QUADS)]
        v_in = [sem(f"v_in{q}") for q in range(QUADS)]
        sel_set, sel_fix = sem("sel_set"), sem("sel_fix")
        s_done, exp_done, pv_done = sem("s_done"), sem("exp_done"), sem("pv_done")
        a_done, max_done = sem("a_done"), sem("max_done")
        shift_made, shift_tr, shift_out, shift_in = (sem(n) for n in ("shift_made", "shift_tr", "shift_out", "shift_in"))
        o_out, l_out, r_out, ot_done = (sem(n) for n in ("o_out", "l_out", "r_out", "ot_done"))
        x_in = sem("xres_in")
        tl_done, tl_out = sem("tl_done"), sem("tl_out")
        chain = sem("chain")
        ve_done, rstd_done = sem("ve_done"), sem("rstd2_done")
        ex_done = sem("ex_done")
        idx_ready, row_out = sem("idx_ready"), sem("row_out")
        passed_pool, passed_dve = sem("passed_pool2"), sem("passed_dve2")
        C_MEAN, C_HN, C_DIF, C_OH = 4, 6, 8, 12

        def spans(g):
            if g < 2:
                return [(2 * g, 0, 0), (2 * g + 1, 0, 512)]
            if g == 2:
                return [(NB, 0, 0), (NB + 1, P, 512)]
            return [(NB + 2, 2 * P, 0), (NB + 3, 3 * P, 2 * P)]

        def width(g):
            kb, q0, at = spans(g)[1]
            return at + T - q0

        def row_units(quad_h):
            for i in range(NB):
                yield i, 0, TM
                yield i, TM, (i + 1) * P

        def ahead(q, u, last):
            k = 2 * u
            d = 1 if k < 16 else 2
            if last and q + d >= QUADS:
                return None
            return d, (2 + k // 8) % HQ, k % 8

        def iterate(eng, body):
            body(0, True, False)
            with eng.Fori(1, B - 1) as b:
                body(b, False, False)
            body(B - 1, False, True)

        with nc.Block() as block:
            @block.sync
            def _(sp):
                def load_stack(b, q):
                    hf, o = divmod(q * HQ * DH, P)
                    for t in range(TERMS):
                        for dst, part, lo, hi in ((qs[q], Q_PART[t], 0, T), (ks[q], K_PART[t], T, COLS)):
                            sp.dma_start(dst[DH * t:DH * (t + 1), :, :],
                                         parts_d[bass.ds(b, 1), hf, part, o:o + HQ * DH, lo:hi]
                                         .rearrange("a (h d) n -> d (a h) n", h=HQ)).then_inc(stk_in[q], 16)

                def load_v(b, q):
                    sp.dma_start(vq[q][:].rearrange("p k h d -> p (k h d)"),
                                 v_d[bass.ds(b, 1), :, q * 1024:(q + 1) * 1024].rearrange("a p n -> p (a n)")).then_inc(v_in[q], 16)

                def load_x(b):
                    sp.dma_start(xres[:], x[bass.ds(b, 1)].rearrange("a (n p) d -> p (a n) d", p=P)).then_inc(x_in, 16)

                def send_shift(n, q):
                    sp.wait_ge(shift_out, n + 1)
                    src = mT[q % 2]
                    sp.dma_start(qs[q][SROWS:SROWS + MROWS, :, :],
                                 src[:].unsqueeze(1).to_broadcast([MROWS, HQ, T])).then_inc(shift_in, 16)

                for q in range(3):
                    load_stack(0, q)
                    load_v(0, q)
                send_shift(0, 0)

                def body(b, first, last):
                    for q in range(QUADS):
                        n = b * QUADS + q
                        bn, qn = (b, q + 3) if q == 0 else (b + 1, q - 1)
                        if q == 0 or not last:
                            wait(sp, s_done, 16 * n)
                            load_stack(bn, qn)
                            wait(sp, pv_done, 4 * n)
                            load_v(bn, qn)
                        if q == 2:
                            if not first:
                                sp.wait_ge(tl_out, N_TL * (b - 1) + 2)
                            load_x(b)
                        if not (last and q == QUADS - 1):
                            send_shift(n + 1, (q + 1) % QUADS)

                iterate(sp, body)

            @block.gpsimd
            def _(pool):
                for q in range(QUADS):
                    pool.memset(ks[q][SROWS:SROWS + MROWS], 0.0).then_inc(sel_set, 1)
                for part in range(2):
                    pool.wait_ge(sel_set, QUADS * (part + 1))
                    for q in range(QUADS):
                        v = ks[q][SROWS:SROWS + MROWS]
                        pool.affine_select(out=v, in_=v, compare_op=ALU.not_equal, fill=1.0, base=-HQ * part,
                                           pattern=[[-1, HQ], [0, KEYS]], channel_multiplier=1).then_inc(sel_set, 1)

                def rstd(tb):
                    pool.wait_ge(chain, N_T * tb + C_MEAN)
                    pool.sem_inc(passed_pool, 1)
                    pool.tensor_scalar(ve[:], mv[:, :, 1], EPS, None, ALU.add).then_inc(ve_done, 1)
                    pool.wait_ge(ve_done, tb + 1)
                    pool.tensor_tensor(rs[:], ve[:], c["mhalf"][:, 0:NB], ALU.pow).then_inc(rstd_done, 1)

                def scatter(tb):
                    pool.wait_ge(idx_ready, tb + 1)
                    pool.sem_inc(passed_pool, 1)
                    for n in range(NB):
                        pool.indirect_dma_start(rows_d[:, :], bass.IndirectOffsetOnAxis(ap=slots[n][:, 0:1], axis=0),
                                                row[:, n, :], None).then_inc(row_out, 16)

                def body(b, first, last):
                    for q in range(QUADS):
                        n = b * QUADS + q
                        if not (first and q == 0):
                            pq = (q - 1) % QUADS
                            pool.wait_ge(r_out, n)
                            if pq == 0:
                                wait(pool, tl_done, 0 if first else N_TL * (b - 1) + 2)
                            pool.tensor_tensor(ot[pq][:], osb[:], linv[:], ALU.mult).then_inc(ot_done, 1)
                        if not first:
                            if q == 0:
                                rstd(b - 1)
                            if q == 2:
                                scatter(b - 1)
                                pool.wait_ge(row_out, 16 * NB * b)

                iterate(pool, body)
                pool.wait_ge(r_out, B * QUADS)
                pool.tensor_tensor(ot[QUADS - 1][:], osb[:], linv[:], ALU.mult).then_inc(ot_done, 1)
                rstd(B - 1)
                scatter(B - 1)
                pool.wait_ge(row_out, 16 * NB * B)

            @block.vector
            def _(dve):
                def maxima(w, h, unit):
                    i, lo, nk = list(row_units(h))[unit]
                    dve.wait_ge(a_done, w + 1)
                    dve.tensor_reduce(mx[:, i, h, unit % 2:unit % 2 + 1], psA[unit % 2][:, 0:nk], AX.X, ALU.max).then_inc(max_done, 1)

                def shift(n):
                    dve.wait_ge(max_done, 32 * (n + 1))
                    dve.tensor_reduce(nm[:], mx[:], AX.X, ALU.max, negate=True).then_inc(shift_made, 1)
                    dve.wait_ge(shift_made, N_M * n + 1)
                    wait(dve, shift_tr, n)
                    dve.tensor_copy(mp[:, :, 0, :], nm[:]).then_inc(shift_made, 1)
                    dve.wait_ge(shift_made, N_M * n + 2)
                    dve.tensor_tensor(mp[:, :, 1, :], nm[:], mp[:, :, 0, :], ALU.subtract).then_inc(shift_made, 1)

                def sums(n):
                    dve.wait_ge(o_out, n + 1)
                    wait(dve, ot_done, n)
                    dve.sem_inc(passed_dve, 1)
                    dve.stream_shuffle(lsum[:], osb[:], [DH + k % DH for k in range(32)]).then_inc(l_out, 1)
                    dve.wait_ge(l_out, n + 1)
                    dve.reciprocal(linv[:], lsum[:]).then_inc(r_out, 1)

                for w in range(48):
                    maxima(w, w // 8 % HQ, w % 8)
                    if w == 31:
                        shift(0)

                def tail(tb):
                    k = Count(chain, N_T * tb)
                    bc = lambda a: a.unsqueeze(2).to_broadcast([P, NB, E])

                    def x1(r):
                        if r == 0:
                            dve.wait_ge(x_in, 16 * tb + 16)
                        dve.wait_ge(tl_done, N_TL * tb + r + 1)
                        ins = dve.tensor_tensor(row[:, 2 * r:2 * r + 2, 0:D], psM[:].rearrange("p (n d) -> p n d", d=D),
                                                xres[:, 2 * r:2 * r + 2, :], ALU.add)
                        ins.then_inc(tl_out, 1)

                    def stats():
                        dve.wait_ge(tl_out, N_TL * tb + 2)
                        k.add(dve.tensor_copy(row[:, :, D + 3:D + 4].bitcast(I32), c["tokf"][:].unsqueeze(2)))
                        k.wait(dve)
                        k.add(dve.tensor_scalar(c["tokf"][:], c["tokf"][:], float(T), None, ALU.add))
                        for n in range(NB):
                            ins = dve.bn_stats(st[:, n, :], row[:, n, 0:D])
                        k.add(ins)
                        k.wait(dve)
                        dve.sem_inc(passed_dve, 1)
                        for n in range(NB):
                            ins = dve.bn_aggr(mv[:, n, :], st[:, n, :])
                        k.add(ins)
                        assert k.n == C_MEAN

                    def norm():
                        dve.wait_ge(rstd_done, tb + 1)
                        k.wait(dve)
                        dve.tensor_copy(row[:, :, D:D + 1], rs[:].unsqueeze(2))
                        k.add(dve.scalar_tensor_tensor(row[:, :, D + 1:D + 2], mv[:, :, 0:1], -1.0, rs[:].unsqueeze(2), ALU.mult, ALU.mult))
                        k.wait(dve)
                        for n in range(NB):
                            ins = dve.tensor_scalar(hn[:, n, :], row[:, n, 0:D], rs[:, n:n + 1], row[:, n, D + 1:D + 2], ALU.mult, ALU.add)
                        k.add(ins)
                        assert k.n == C_HN

                    def route():
                        dve.wait_ge(tl_done, N_TL * tb + 6)
                        dve.tensor_copy(lg[:], psM[:, 0:NB * E].rearrange("p (n e) -> p n e", e=E)).then_inc(tl_out, 1)
                        dve.wait_ge(tl_out, N_TL * tb + 6)
                        k.add(dve.tensor_reduce(lmax[:], lg[:], AX.X, ALU.max))
                        k.wait(dve)
                        k.add(dve.tensor_tensor(dif[:], lg[:], bc(lmax[:]), ALU.subtract))
                        assert k.n == C_DIF
                        k.add(dve.tensor_tensor(eq[:], lg[:], bc(lmax[:]), ALU.is_equal))
                        k.wait(dve)
                        k.add(dve.scalar_tensor_tensor(cand[:], eq[:], -float(E), c["eiota"][:], ALU.mult, ALU.add))
                        k.wait(dve)
                        k.add(dve.tensor_reduce(cmin[:], cand[:], AX.X, ALU.min))
                        k.wait(dve)
                        k.add(dve.tensor_tensor(oh[:], cand[:], bc(cmin[:]), ALU.is_equal))
                        assert k.n == C_OH
                        dve.wait_ge(ex_done, tb + 1)
                        k.add(dve.tensor_reduce(esum[:], ex[:], AX.X, ALU.add))
                        k.wait(dve)
                        k.add(dve.reciprocal(einv[:], esum[:]))
                        k.wait(dve)
                        k.add(dve.tensor_scalar(row[:, :, D + 2:D + 3], einv[:].unsqueeze(2), c["tgf"][:, 0:1], None, ALU.mult))

                    def place():
                        dve.wait_ge(tl_done, N_TL * tb + 7)
                        run = c["run"]
                        k.add(dve.tensor_tensor(cumr[:], psM[:, 0:NB * E].rearrange("p (n e) -> p n e", e=E),
                                                run[:].unsqueeze(1).to_broadcast([P, NB, E]), ALU.add))
                        k.wait(dve)
                        dve.tensor_tensor(run[:], run[:], psM[:, NB * E:NB * E + E], ALU.add).then_inc(tl_out, 1)
                        k.add(dve.tensor_tensor(pick[:], cumr[:], oh[:], ALU.mult))
                        k.wait(dve)
                        k.add(dve.tensor_reduce(slot[:], pick[:], AX.X, ALU.add))
                        k.wait(dve)
                        for n in range(NB):
                            ins = dve.tensor_copy(slots[n][:], slot[:, n:n + 1])
                        ins.then_inc(idx_ready, 1)
                        assert k.n == N_T, k.n

                    return [lambda: x1(0), lambda: x1(1), stats, norm, route, place]

                def body(b, first, last):
                    for q in range(QUADS):
                        n = b * QUADS + q
                        for u in range(16):
                            if u == 8 and not (last and q == QUADS - 1):
                                shift(n + 1)
                            a = ahead(q, u, last)
                            if a:
                                d, h, unit = a
                                for k in range(2):
                                    maxima(32 * n + 48 + 2 * u + k, h, unit + k)
                            if u == 4 and not (first and q == 0):
                                sums(n - 1)
                            if not first and (q, u) in TAIL_DVE:
                                step(b, TAIL_DVE[q, u])

                TAIL_DVE = {(0, 9): 0, (0, 15): 1, (1, 0): 2, (1, 2): 3, (2, 4): 4, (2, 10): 5}
                tails = {}

                def step(b, j):
                    if j == 0:
                        tails["now"] = tail(b - 1)
                    tails["now"][j]()

                iterate(dve, body)
                sums(B * QUADS - 1)
                for f in tail(B - 1):
                    f()

            @block.scalar
            def _(act):
                act.wait_ge(shift_tr, 1)
                act.activation(mT[0][:], psM[0:MROWS, :], ACT.Copy).then_inc(shift_out, 1)

                def tail_copy(tb, j):
                    if j == 0 or j == 1:
                        act.wait_ge(tl_done, N_TL * tb + 3 + j)
                        act.activation(hT[:, j, :], psM[:], ACT.Copy).then_inc(tl_out, 1)
                    if j == 2:
                        act.wait_ge(tl_done, N_TL * tb + 5)
                        act.activation(redT[:], psM[0:GD, :], ACT.Copy).then_inc(tl_out, 1)
                    if j == 3:
                        act.wait_ge(chain, N_T * tb + C_DIF)
                        act.activation(ex[:], dif[:], ACT.Exp).then_inc(ex_done, 1)

                TAIL_ACT = {(1, 5): 0, (1, 8): 1, (1, 14): 2, (2, 4): 3}

                def body(b, first, last):
                    for q in range(QUADS):
                        n = b * QUADS + q
                        for g in range(4):
                            for h in range(HQ):
                                u = 4 * g + h
                                act.wait_ge(s_done, 16 * n + u + 1)
                                if not (first and q == 0 and g < 2):
                                    wait(act, pv_done, 4 * n + g - 1)
                                act.activation(pr[g % 2][:, h, 0:width(g)], psS[u % 2][:, 0:width(g)], ACT.Exp).then_inc(exp_done, 1)
                                if u == 2 and not (first and q == 0):
                                    act.wait_ge(pv_done, 4 * n)
                                    wait(act, ot_done, n - 1)
                                    act.activation(osb[:], psO[:], ACT.Copy).then_inc(o_out, 1)
                                if u == 11 and not (last and q == QUADS - 1):
                                    nn, qq = n + 1, (q + 1) % QUADS
                                    act.wait_ge(shift_tr, nn + 1)
                                    wait(act, shift_in, 16 * n)
                                    act.activation(mT[qq % 2][:], psM[0:MROWS, :], ACT.Copy).then_inc(shift_out, 1)
                                if not first and (q, u) in TAIL_ACT:
                                    tail_copy(b - 1, TAIL_ACT[q, u])

                iterate(act, body)
                act.wait_ge(pv_done, 4 * B * QUADS)
                act.wait_ge(ot_done, B * QUADS - 1)
                act.activation(osb[:], psO[:], ACT.Copy).then_inc(o_out, 1)
                for j in range(4):
                    tail_copy(B - 1, j)

            @block.tensor
            def _(pe):
                def row_scores(w, q, h, unit):
                    i, lo, nk = list(row_units(h))[unit]
                    ps = psA[unit % 2]
                    wait(pe, max_done, w - 1)
                    causal = lo > 0
                    ins = pe.matmul(ps[:, 0:nk], qs[q][0:SROWS, h, i * P:(i + 1) * P], ks[q][0:SROWS, h, lo:lo + nk],
                                    start=True, stop=not causal)
                    if causal:
                        ins = pe.matmul(ps[:, nk - P:nk], c["identb"][:], c["mask_q"][:], start=False, stop=True)
                    ins.then_inc(a_done, 1)

                def shift_rows(n):
                    pe.wait_ge(shift_made, N_M * (n + 1))
                    for i in range(NB):
                        ins = pe.matmul(psM[0:MROWS, i * P:(i + 1) * P], mp[:, i].rearrange("p a h -> p (a h)"), c["identb"][:],
                                        start=True, stop=True)
                    ins.then_inc(shift_tr, 1)

                def key_scores(n, q, g, h, tile0):
                    u = 4 * g + h
                    if not (tile0 and u < 2):
                        wait(pe, exp_done, 16 * n + u - 1)
                    ps = psS[u % 2]
                    for kb, q0, at in spans(g):
                        nq = T - q0
                        causal = kb >= NB
                        ins = pe.matmul(ps[:, at:at + nq], ks[q][0:SROWS + MROWS, h, kb * P:(kb + 1) * P],
                                        qs[q][0:SROWS + MROWS, h, q0:T], start=True, stop=not causal)
                        if causal:
                            ins = pe.matmul(ps[:, at:at + P], c["identb"][:], c["mask_k"][:], start=False, stop=True)
                    ins.then_inc(s_done, 1)

                def values(n, q, g):
                    wait(pe, exp_done, 16 * n + 4 * g + 4)
                    for kb, q0, at in spans(g):
                        for h in range(HQ):
                            ins = pe.matmul(psO[32 * h:32 * h + 32, q0:T], vq[q][:, kb, h, :], pr[g % 2][:, h, at:at + T - q0],
                                            start=kb == 0, stop=kb == KB - 1)
                    ins.then_inc(pv_done, 1)

                def tail(tb, j):
                    if j > 0:
                        pe.wait_ge(tl_out, N_TL * tb + j)
                    if j < 2:
                        pe.wait_ge(ot_done, QUADS * tb + QUADS)
                        for n in range(2):
                            for q in range(QUADS):
                                ins = pe.matmul(psM[:, n * D:(n + 1) * D], ot[q][:, (2 * j + n) * P:(2 * j + n + 1) * P],
                                                c["wout"][:, q, :], start=q == 0, stop=q == QUADS - 1)
                    elif j < 4:
                        pe.wait_ge(chain, N_T * tb + C_HN)
                        for n in range(NB):
                            ins = pe.transpose(psM[:, n * P:(n + 1) * P], hn[:, n, (j - 2) * P:(j - 1) * P], c["ident"][:])
                    elif j == 4:
                        for k in range(KC):
                            ins = pe.matmul(psM[0:GD, :], c["wred"][:, k, :], hT[:, k, :], start=k == 0, stop=k == KC - 1)
                    elif j == 5:
                        for n in range(NB):
                            ins = pe.matmul(psM[:, n * E:(n + 1) * E], redT[:, n * P:(n + 1) * P], c["wgT"][:], start=True, stop=True)
                    else:
                        pe.wait_ge(chain, N_T * tb + C_OH)
                        o = oh[:].rearrange("p n e -> p (n e)")
                        pe.matmul(psM[:, 0:NB * E], c["before"][:], o, start=True, stop=False, skip_group_check=True)
                        for m in range(1, NB):
                            pe.matmul(psM[:, m * E:NB * E], c["onesb"][:], o[:, 0:(NB - m) * E], start=False, stop=False,
                                      skip_group_check=True)
                        for m in range(NB):
                            ins = pe.matmul(psM[:, NB * E:NB * E + E], c["onesb"][:], o[:, m * E:(m + 1) * E], start=False,
                                            stop=m == NB - 1, skip_group_check=True)
                    ins.then_inc(tl_done, 1)

                TAIL_PE = {(0, 7): 0, (0, 14): 1, (1, 4): 2, (1, 7): 3, (1, 13): 4, (2, 2): 5, (2, 7): 6}

                for w in range(48):
                    if w == 0:
                        pe.wait_ge(stk_in[0], 16 * 2 * TERMS)
                    if w == 32:
                        pe.wait_ge(stk_in[1], 16 * 2 * TERMS)
                    row_scores(w, w // 32, w // 8 % HQ, w % 8)
                shift_rows(0)
                pe.wait_ge(sel_set, 3 * QUADS)

                def body(b, first, last):
                    done = 0
                    for q in range(QUADS):
                        n = b * QUADS + q
                        tile0 = first and q == 0
                        pe.wait_ge(shift_in, 16 * (n + 1))
                        for g in range(4):
                            for h in range(HQ):
                                u = 4 * g + h
                                key_scores(n, q, g, h, tile0)
                                if h == 1:
                                    if g == 0 and not tile0:
                                        values(n - 1, (q - 1) % QUADS, 3)
                                    if g == 1:
                                        pe.wait_ge(v_in[q], 16 * (b + 1))
                                        wait(pe, o_out, n)
                                    if g > 0:
                                        values(n, q, g - 1)
                                a = ahead(q, u, last)
                                if a:
                                    d, hh, unit = a
                                    qq = (q + d) % QUADS
                                    if u == 8:
                                        pe.wait_ge(stk_in[qq], 16 * 2 * TERMS * (b + 1 + (q + d) // QUADS))
                                    for k in range(2):
                                        row_scores(32 * n + 48 + 2 * u + k, qq, hh, unit + k)
                                if u == 11 and not (last and q == QUADS - 1):
                                    pe.wait_ge(shift_out, n + 1)
                                    if not first:
                                        pe.wait_ge(tl_out, N_TL * (b - 1) + done)
                                    shift_rows(n + 1)
                                if not first and (q, u) in TAIL_PE:
                                    pe.wait_ge(shift_out, n + 2 if u > 11 else n + 1)
                                    tail(b - 1, TAIL_PE[q, u])
                                    done += 1

                iterate(pe, body)
                values(B * QUADS - 1, QUADS - 1, 3)
                for j in range(N_TL):
                    tail(B - 1, j)


def setup(nc, c, g_x, g_f, wout, bout, w_red, wg):
    with ExitStack() as s:
        def sb(name, shape, dt):
            return s.enter_context(nc.sbuf_tensor(name, shape, dt))

        def sem(name):
            return s.enter_context(nc.semaphore(name))

        gates = sb("gates", [P, 2], F32)
        wg_s = sb("wg_s", [E, GD], F32)
        wsq = sb("wsq", [E, GD], F32)
        wn = sb("wn", [E, 1], F32)
        wn2 = sb("wn2", [E, 1], F32)
        wn3 = sb("wn3", [E, 1], F32)
        wgn = sb("wgn", [E, GD], F32)
        ints = sb("ints", [P, 64], I32)
        tg = sb("tg", [P, 2], F32)
        ps = s.enter_context(nc.psum_tensor("ps_setup", [P, 512], F32))
        load, wload, cleared, built, ints_set, tanh_done, step, norm_done, scaled, tr = (
            sem(n) for n in ("g_load", "w_load", "cleared", "built", "ints_set", "tanh_done", "step", "wg_norm", "scaled", "wg_tr"))
        with nc.Block() as block:
            @block.sync
            def _(sp):
                sp.dma_start(gates[:, 0:1], g_x.rearrange("(a n) -> a n", a=1).to_broadcast([P, 1])).then_inc(load, 16)
                sp.dma_start(gates[:, 1:2], g_f.rearrange("(a n) -> a n", a=1).to_broadcast([P, 1])).then_inc(load, 16)
                sp.dma_start(wg_s[:], wg).then_inc(load, 16)
                sp.dma_start(c["wred"][:], w_red.rearrange("(k p) n -> p k n", p=P)).then_inc(load, 16)
                sp.wait_ge(cleared, 1)
                for h in range(HQ):
                    sp.dma_start(c["wout"][32 * h:32 * h + DH, :, :],
                                 wout.rearrange("(q h d) n -> h d q n", q=QUADS, h=HQ)[h]).then_inc(wload, 16)
                sp.dma_start(c["wout"][DH:DH + 1, 0, :], bout.rearrange("(a n) -> a n", a=1)).then_inc(wload, 16)
                sp.wait_ge(wload, 16 * (HQ + 1))
                sp.wait_ge(load, 64)

            @block.gpsimd
            def _(pool):
                pool.memset(c["ident"][:], 0.0).then_inc(built, 1)
                pool.memset(c["identb"][:], 0.0).then_inc(built, 1)
                pool.memset(c["mask_q"][:], 0.0).then_inc(built, 1)
                pool.memset(c["mask_k"][:], 0.0).then_inc(built, 1)
                pool.memset(c["before"][:], 1.0).then_inc(built, 1)
                pool.memset(c["onesb"][:], 1.0)
                pool.memset(c["mhalf"][:], -0.5).then_inc(built, 1)
                pool.wait_ge(built, 6)
                for m in (c["ident"], c["identb"]):
                    pool.affine_select(out=m[:], in_=m[:], compare_op=ALU.not_equal, fill=1.0, base=0,
                                       pattern=[[-1, P]], channel_multiplier=1).then_inc(built, 1)
                pool.affine_select(out=c["mask_q"][:], in_=c["mask_q"][:], compare_op=ALU.is_ge, fill=MASKED, base=0,
                                   pattern=[[-1, P]], channel_multiplier=1)
                pool.affine_select(out=c["mask_k"][:], in_=c["mask_k"][:], compare_op=ALU.is_ge, fill=MASKED, base=0,
                                   pattern=[[1, P]], channel_multiplier=-1)
                pool.affine_select(out=c["before"][:], in_=c["before"][:], compare_op=ALU.is_gt, fill=0.0, base=0,
                                   pattern=[[1, P]], channel_multiplier=-1)
                pool.iota(ints[:, 0:NB * E], pattern=[[0, NB], [1, E]], base=0, channel_multiplier=0).then_inc(ints_set, 1)
                pool.iota(ints[:, 32:40], pattern=[[CAP, E]], base=0, channel_multiplier=0).then_inc(ints_set, 1)
                pool.iota(ints[:, 40:40 + NB], pattern=[[P, NB]], base=0, channel_multiplier=1).then_inc(ints_set, 1)
                pool.wait_ge(norm_done, 1)
                pool.tensor_tensor(wn2[:], wn[:], c["half"][0:E, 0:1], ALU.pow).then_inc(norm_done, 1)

            @block.vector
            def _(dve):
                dve.memset(c["half"][:], 0.5)
                dve.memset(c["wout"][:], 0.0).then_inc(cleared, 1)
                dve.wait_ge(ints_set, 3)
                dve.tensor_copy(c["eiota"][:].rearrange("p n e -> p (n e)"), ints[:, 0:NB * E])
                dve.tensor_copy(c["run"][:], ints[:, 32:40])
                dve.tensor_copy(c["base"][:], ints[:, 32:40])
                dve.tensor_copy(c["tokf"][:], ints[:, 40:40 + NB])
                dve.wait_ge(load, 64)
                dve.tensor_tensor(wsq[:], wg_s[:], wg_s[:], ALU.mult).then_inc(step, 1)
                dve.wait_ge(step, 1)
                dve.tensor_reduce(wn[:], wsq[:], AX.X, ALU.add).then_inc(norm_done, 1)
                dve.wait_ge(norm_done, 2)
                dve.tensor_scalar(wn3[:], wn2[:], 1e-4, None, ALU.max).then_inc(step, 1)
                dve.wait_ge(step, 2)
                dve.reciprocal(wn[:], wn3[:]).then_inc(step, 1)
                dve.wait_ge(step, 3)
                dve.tensor_scalar(wgn[:], wg_s[:], wn[:, 0:1], None, ALU.mult).then_inc(scaled, 1)
                dve.wait_ge(tanh_done, 1)
                dve.tensor_copy(c["tgf"][:], tg[:, 1:2])
                dve.wait_ge(wload, 16 * (HQ + 1))
                dve.tensor_scalar(c["wout"][:].rearrange("p q n -> p (q n)"), c["wout"][:].rearrange("p q n -> p (q n)"),
                                  tg[:, 0:1], None, ALU.mult)
                dve.wait_ge(tr, 1)
                dve.tensor_copy(c["wgT"][:], ps[0:GD, 0:E])

            @block.scalar
            def _(act):
                act.wait_ge(load, 64)
                act.activation(tg[:], gates[:], ACT.Tanh).then_inc(tanh_done, 1)

            @block.tensor
            def _(pe):
                pe.wait_ge(scaled, 1)
                pe.wait_ge(built, 8)
                pe.transpose(ps[0:GD, 0:E], wgn[:], c["ident"][0:E, 0:E]).then_inc(tr, 1)


def close_rows(nc, c, rows_d):
    with ExitStack() as s:
        def sb(name, shape, dt):
            return s.enter_context(nc.sbuf_tensor(name, shape, dt))

        def sem(name):
            return s.enter_context(nc.semaphore(name))

        pad = sb("pad", [P, ROW], F32)
        padf = sb("padf", [P, E], F32)
        padi = [sb(f"padi{e}", [P, 1], U32) for e in range(E)]
        pi = sb("pi", [P, E], I32)
        pf = sb("pf", [P, E], F32)
        ti = sb("ti", [1, TILES], I32)
        tf = sb("tf", [1, TILES], F32)
        cf = sb("cf", [1, E], F32)
        ci = sb("ci", [1, E], I32)
        nt = sb("nt", [1, E], F32)
        ones = sb("ones8", [1, E], F32)
        end = sb("end", [1, E], F32)
        skip = sb("skip", [1, E], F32)
        ge = sb("ge", [1, TILES, E], F32)
        gs = sb("gsk", [1, TILES, E], F32)
        te = sb("te", [1, TILES], F32)
        tr = sb("tr", [1, TILES], F32)
        tr2 = sb("tr2", [1, TILES], F32)
        ints_set, step, pad_ready, pad_out, dummy_out = (sem(n) for n in ("ints2", "step2", "pad_ready", "pad_out", "dummy_out"))
        with nc.Block() as block:
            @block.gpsimd
            def _(pool):
                pool.iota(pi[:], pattern=[[0, E]], base=0, channel_multiplier=1).then_inc(ints_set, 1)
                pool.iota(ti[:], pattern=[[P, TILES]], base=0, channel_multiplier=0).then_inc(ints_set, 1)
                pool.wait_ge(pad_ready, 1)
                for e in range(E):
                    pool.indirect_dma_start(rows_d[:, :], bass.IndirectOffsetOnAxis(ap=padi[e][:, 0:1], axis=0),
                                            pad[:], None).then_inc(pad_out, 16)
                pool.wait_ge(pad_out, 16 * E)

            @block.sync
            def _(sp):
                sp.wait_ge(pad_ready, 1)
                sp.dma_start(rows_d[DUMMY:DUMMY + P, :], pad[:]).then_inc(dummy_out, 16)
                sp.wait_ge(dummy_out, 16)

            @block.vector
            def _(dve):
                k = Count(step)
                dve.memset(ones[:], 1.0)
                k.add(dve.memset(pad[:], 0.0))
                k.wait(dve)
                k.add(dve.memset(pad[:, D + 3:D + 4].bitcast(I32), NOTOK))
                dve.wait_ge(ints_set, 2)
                k.add(dve.tensor_copy(pf[:], pi[:]))
                k.add(dve.tensor_copy(tf[:], ti[:]))
                k.wait(dve)
                k.add(dve.tensor_tensor(padf[:], pf[:], c["run"][:], ALU.add))
                k.wait(dve)
                for e in range(E):
                    ins = dve.tensor_copy(padi[e][:], padf[:, e:e + 1])
                ins.then_inc(pad_ready, 1)
                k.add(dve.tensor_tensor(cf[:], c["run"][0:1, :], c["base"][0:1, :], ALU.subtract))
                k.wait(dve)
                k.add(dve.tensor_scalar(nt[:], cf[:], float(P - 1), None, ALU.add))
                k.wait(dve)
                k.add(dve.tensor_copy(ci[:], nt[:]))
                k.wait(dve)
                k.add(dve.tensor_scalar(ci[:], ci[:], 7, None, ALU.arith_shift_right))
                k.wait(dve)
                k.add(dve.tensor_copy(nt[:], ci[:]))
                k.wait(dve)
                k.add(dve.tensor_tensor_scan(end[:], ones[:], nt[:], 0.0, ALU.mult, ALU.add))
                k.add(dve.tensor_scalar(skip[:], nt[:], -float(P), float(CAP), ALU.mult, ALU.add))
                k.wait(dve)
                k.add(dve.tensor_scalar(end[:], end[:], float(P), None, ALU.mult))
                k.wait(dve)
                k.add(dve.tensor_tensor(ge[:], tf[:].unsqueeze(2).to_broadcast([1, TILES, E]),
                                        end[:].unsqueeze(1).to_broadcast([1, TILES, E]), ALU.is_ge))
                k.wait(dve)
                k.add(dve.tensor_reduce(te[:], ge[:], AX.X, ALU.add))
                k.add(dve.tensor_tensor(gs[:], ge[:], skip[:].unsqueeze(1).to_broadcast([1, TILES, E]), ALU.mult))
                k.wait(dve)
                k.add(dve.tensor_scalar(te[:], te[:], float(E - 1), None, ALU.min))
                k.add(dve.tensor_reduce(tr[:], gs[:], AX.X, ALU.add))
                k.wait(dve)
                k.add(dve.tensor_tensor(tr2[:], tr[:], tf[:], ALU.add))
                k.wait(dve)
                k.add(dve.tensor_scalar(tr2[:], tr2[:], float(DUMMY), None, ALU.min))
                k.wait(dve)
                dve.tensor_copy(c["tile_e"][:], te[:])
                dve.tensor_copy(c["tile_r"][:], tr2[:])


def experts(nc, c, w1, b1, w2, b2, rows_d, out):
    out_d = out.rearrange("b t d -> (b t) d")
    with ExitStack() as s:
        def sb(name, shape, dt):
            return s.enter_context(nc.sbuf_tensor(name, shape, dt))

        def sem(name):
            return s.enter_context(nc.semaphore(name))

        W1 = sb("w1s", [P, E * KC * 2 * FF], BF16)
        W2 = sb("w2s", [P, E * FC * 2 * D], BF16)
        stage = [sb(f"stage{p}", [P, KC * FF], F32) for p in range(2)]
        b1n = sb("b1n", [E * FC, P], F32)
        b1T = sb("b1T", [P, E * FC], F32)
        b2b = sb("b2b", [P, E * D], F32)
        row = [sb(f"frow{p}", [P, ROW], F32) for p in range(2)]
        hn = [sb(f"fhn{p}", [P, D], F32) for p in range(2)]
        hh = [sb(f"hh{p}", [P, KC, 2, P], BF16) for p in range(2)]
        g = [sb(f"g{p}", [P, FC, P], F32) for p in range(2)]
        gh = [sb(f"gh{p}", [P, FC, P], BF16) for p in range(2)]
        gl = [sb(f"gl{p}", [P, FC, P], BF16) for p in range(2)]
        y = sb("y", [P, D], F32)
        res = [sb(f"res{p}", [P, D], F32) for p in range(2)]
        ids = [sb(f"ids{p}", [P, 1], U32) for p in range(2)]
        psT = [s.enter_context(nc.psum_tensor(f"fT{p}", [P, 512], F32)) for p in range(2)]
        psH = [s.enter_context(nc.psum_tensor(f"fH{p}", [P, 4, P], F32)) for p in range(4)]
        psY = [s.enter_context(nc.psum_tensor(f"fY{p}", [P, 512], F32)) for p in range(2)]
        wst, row_in, stored = ([sem(f"{n}{p}") for p in range(2)] for n in ("wst", "row_in", "stored"))
        (bias_in, hi_done, lo_done, b1_tr, hn_done, tr_done, hi_out, lo_out, h_done, g_done, ghi_done, glo_done,
         y_done, y_sum, res_done, b1_out) = (sem(n) for n in (
             "bias_in", "hi_done", "lo_done", "b1_tr", "hn_done", "tr_done", "hi_out", "lo_out", "h_done",
             "g_done", "ghi_done", "glo_done", "y_done", "y_sum", "res_done", "b1_out"))
        passed_pool = sem("passed_pool3")
        NW = 2 * E

        def split(w):
            e = w // 2
            if w % 2 == 0:
                v = W1[:, e * KC * 2 * FF:(e + 1) * KC * 2 * FF].rearrange("p (k a n) -> p k a n", k=KC, a=2)
                t = stage[w % 2][:].rearrange("p (k n) -> p k n", k=KC)
            else:
                v = W2[:, e * FC * 2 * D:(e + 1) * FC * 2 * D].rearrange("p (k a n) -> p k a n", k=FC, a=2)
                t = stage[w % 2][:].rearrange("p (k n) -> p k n", k=FC)
            return v[:, :, 0, :], v[:, :, 1, :], t

        def tiles(eng, body):
            peel(2, lambda p: body(p, p))
            with eng.Fori(1, TILES // 2) as i:
                for p in range(2):
                    body(2 * i + p, p)

        def expert_of(eng, t):
            return eng.value_load(c["tile_e"][0:1, bass.ds(t, 1)], min_val=0, max_val=E - 1)

        with nc.Block() as block:
            @block.sync
            def _(sp):
                sp.dma_start(b1n[:], b1.rearrange("e (c p) -> (e c) p", p=P)).then_inc(bias_in, 16)
                sp.dma_start(b2b[:], b2.rearrange("(a e) d -> a (e d)", a=1).to_broadcast([P, E * D])).then_inc(bias_in, 16)
                for w in range(NW):
                    if w >= 2:
                        sp.wait_ge(lo_done, w - 1)
                    src = (w1 if w % 2 == 0 else w2)[w // 2].rearrange("(k p) n -> p k n", p=P)
                    sp.dma_start(split(w)[2], src).then_inc(wst[w % 2], 16)

                def body(i, p):
                    t = 2 * i + p
                    if not isinstance(i, int):
                        sp.wait_ge(res_done, t - 1)
                    r = sp.value_load(c["tile_r"][0:1, bass.ds(t, 1)], min_val=0, max_val=DUMMY)
                    sp.dma_start(row[p][:], rows_d[bass.ds(r, P), :]).then_inc(row_in[p], 16)

                for p in range(2):
                    body(0, p)
                with sp.Fori(1, TILES // 2) as i:
                    for p in range(2):
                        body(i, p)

            @block.gpsimd
            def _(pool):
                for w in range(NW):
                    hi, lo, st = split(w)
                    pool.wait_ge(hi_done, w + 1)
                    pool.tensor_tensor(lo, st, hi, ALU.subtract).then_inc(lo_done, 1)

                def body(t, p):
                    pool.wait_ge(res_done, t + 1)
                    pool.sem_inc(passed_pool, 1)
                    pool.indirect_dma_start(out_d, bass.IndirectOffsetOnAxis(ap=ids[p][:, 0:1], axis=0), res[p][:], None,
                                            bounds_check=TOK - 1, oob_is_err=False).then_inc(stored[p], 16)

                tiles(pool, body)
                for p in range(2):
                    wait(pool, stored[p], 16 * (TILES // 2))

            @block.scalar
            def _(act):
                act.wait_ge(b1_tr, 1)
                act.activation(b1T[:], psT[0][:, 0:E * FC], ACT.Copy).then_inc(b1_out, 1)
                for w in range(NW):
                    hi, lo, st = split(w)
                    act.wait_ge(wst[w % 2], 16 * (w // 2 + 1))
                    act.activation(hi, st, ACT.Copy).then_inc(hi_done, 1)
                act.wait_ge(b1_out, 1)

                def body(t, p):
                    e = expert_of(act, t)
                    act.wait_ge(tr_done, t + 1)
                    act.activation(hh[p][:, :, 0, :], psT[p][:, 0:D].rearrange("p (k n) -> p k n", k=KC), ACT.Copy).then_inc(hi_out, 1)
                    for j in range(2):
                        act.wait_ge(h_done, 2 * t + j + 1)
                        for k in range(4):
                            f = 4 * j + k
                            ins = act.activation(g[p][:, f, :], psH[2 * p + j][:, k, :], ACT.Gelu,
                                                 bias=b1T[:, bass.ds(e * FC + f, 1)])
                        ins.then_inc(g_done, 1)

                tiles(act, body)

            @block.vector
            def _(dve):
                dve.wait_ge(bias_in, 32)

                def prepare(i, t, p):
                    dve.wait_ge(row_in[p], 16 * i + 16)
                    dve.tensor_scalar(hn[p][:], row[p][:, 0:D], row[p][:, D:D + 1], row[p][:, D + 1:D + 2],
                                      ALU.mult, ALU.add).then_inc(hn_done, 1)

                def low(t, p):
                    dve.wait_ge(hi_out, t + 1)
                    dve.tensor_tensor(hh[p][:, :, 1, :], psT[p][:, 0:D].rearrange("p (k n) -> p k n", k=KC),
                                      hh[p][:, :, 0, :], ALU.subtract).then_inc(lo_out, 1)

                def body(i, p):
                    t = 2 * i + p
                    prepare(i, t, p)
                    low(t, p)
                    e = expert_of(dve, t)
                    for j in range(2):
                        half = slice(4 * j, 4 * j + 4)
                        dve.wait_ge(g_done, 2 * t + j + 1)
                        dve.tensor_copy(gh[p][:, half, :], g[p][:, half, :]).then_inc(ghi_done, 1)
                        dve.wait_ge(ghi_done, 2 * t + j + 1)
                        dve.tensor_tensor(gl[p][:, half, :], g[p][:, half, :], gh[p][:, half, :], ALU.subtract).then_inc(glo_done, 1)
                    dve.wait_ge(y_done, t + 1)
                    dve.tensor_tensor(y[:], psY[p][:, 0:D], b2b[:, bass.ds(e * D, D)], ALU.add).then_inc(y_sum, 1)
                    dve.wait_ge(y_sum, t + 1)
                    wait(dve, stored[p], 16 * i)
                    dve.tensor_copy(ids[p][:], row[p][:, D + 3:D + 4].bitcast(U32))
                    dve.scalar_tensor_tensor(res[p][:], y[:], row[p][:, D + 2:D + 3], row[p][:, 0:D],
                                             ALU.mult, ALU.add).then_inc(res_done, 1)

                peel(2, lambda p: body(0, p))
                with dve.Fori(1, TILES // 2) as i:
                    for p in range(2):
                        body(i, p)

            @block.tensor
            def _(pe):
                pe.wait_ge(bias_in, 32)
                pe.transpose(psT[0][:, 0:E * FC], b1n[:], c["ident"][0:E * FC, 0:E * FC]).then_inc(b1_tr, 1)
                pe.wait_ge(b1_out, 1)
                pe.wait_ge(lo_done, NW)

                def rows_T(t, p):
                    pe.wait_ge(hn_done, t + 1)
                    for k in range(KC):
                        ins = pe.transpose(psT[p][:, k * P:(k + 1) * P], hn[p][:, k * P:(k + 1) * P], c["ident"][:])
                    ins.then_inc(tr_done, 1)

                def body(t, p):
                    e = expert_of(pe, t)
                    rows_T(t, p)
                    pe.wait_ge(lo_out, t + 1)
                    for j in range(2):
                        for k in range(4):
                            f = 4 * j + k
                            n = 0
                            for kc in range(KC):
                                for a, b in ((0, 0), (0, 1), (1, 0)):
                                    n += 1
                                    ins = pe.matmul(psH[2 * p + j][:, k, :],
                                                    W1[:, bass.ds(e * (KC * 2 * FF) + (kc * 2 + a) * FF + f * P, P)],
                                                    hh[p][:, kc, b, :], start=n == 1, stop=n == 3 * KC)
                        ins.then_inc(h_done, 1)
                    for f in range(FC):
                        if f % 4 == 0:
                            pe.wait_ge(glo_done, 2 * t + f // 4 + 1)
                        for m, (a, b) in enumerate(((0, 0), (0, 1), (1, 0))):
                            ins = pe.matmul(psY[p][:, 0:D], (gl if b else gh)[p][:, f, :],
                                            W2[:, bass.ds(e * (FC * 2 * D) + (f * 2 + a) * D, D)],
                                            start=f == 0 and m == 0, stop=f == FC - 1 and m == 2)
                    ins.then_inc(y_done, 1)

                tiles(pe, body)


def build(nc, x, ctx_1024, g_xattn, g_ffn, wq, wkv, wout, bout, w_red, wg, w1, b1, w2, b2, out):
    parts_d = nc.dram_tensor("qk_parts", (B, HALVES, 3, P, COLS), BF16, kind="Internal").ap()
    v_d = nc.dram_tensor("v_quads", (B, P, QUADS * KB * HQ * 32), F32, kind="Internal").ap()
    rows_d = nc.dram_tensor("sorted_rows", (DUMMY + P, ROW), F32, kind="Internal").ap()
    with ExitStack() as s:
        c = {}
        for name, shape, dt in (("ident", [P, P], F32), ("identb", [P, P], BF16), ("mask_q", [P, P], BF16),
                                ("mask_k", [P, P], BF16), ("before", [P, P], BF16), ("onesb", [P, P], BF16),
                                ("mhalf", [P, NB], F32), ("half", [P, 1], F32), ("eiota", [P, NB, E], F32),
                                ("run", [P, E], F32), ("base", [P, E], F32), ("tokf", [P, NB], F32),
                                ("wred", [P, KC, GD], F32), ("wout", [P, QUADS, D], F32), ("wgT", [GD, E], F32),
                                ("tgf", [P, 1], F32), ("tile_e", [1, TILES], I32), ("tile_r", [1, TILES], I32)):
            c[name] = s.enter_context(nc.sbuf_tensor(name, shape, dt))
        setup(nc, c, g_xattn, g_ffn, wout, bout, w_red, wg)
        project(nc, c, x, ctx_1024, wq, wkv, parts_d, v_d)
        attend(nc, c, x, parts_d, v_d, rows_d)
        close_rows(nc, c, rows_d)
        experts(nc, c, w1, b1, w2, b2, rows_d, out)


_INS = ['x', 'ctx_1024', 'g_xattn', 'g_ffn', 'L0_xattn_Wq', 'L0_xattn_Wkv', 'L0_xattn_Wout', 'L0_xattn_bout',
        'L0_ffn_w_red', 'L0_ffn_wg', 'L0_ffn_w1', 'L0_ffn_b1', 'L0_ffn_w2', 'L0_ffn_b2']


def kernel(**inputs):
    import numpy as _np
    import concourse.bacc as _bacc
    from concourse import mybir as _mybir
    from concourse.bass_utils import run_bass_kernel_spmd as _run

    nc = _bacc.Bacc("TRN2", target_bir_lowering=False, num_devices=1)
    arrays, args = {}, []
    for name in _INS:
        a = _np.ascontiguousarray(inputs[name])
        arrays[f"in_{name}_dram"] = a
        args.append(nc.dram_tensor(f"in_{name}_dram", a.shape, _mybir.dt.from_np(a.dtype), kind="ExternalInput").ap())
    out = nc.dram_tensor("out_0_dram", (B, T, D), _mybir.dt.float32, kind="ExternalOutput").ap()
    build(nc, *args, out)
    r = _run(nc, [arrays], core_ids=[0])
    return r.results[0]["out_0_dram"]
```

```python
from contextlib import ExitStack

import concourse.bass as bass
from concourse import mybir

F32 = mybir.dt.float32
BF16 = mybir.dt.bfloat16
I32 = mybir.dt.int32
U32 = mybir.dt.uint32
ALU = mybir.AluOpType
ACT = mybir.ActivationFunctionType
AX = mybir.AxisListType

P = 128
B, T, D = 8, 512, 256
TM = 512
KEYS = TM + T
HEADS, DH = 16, 16
QUADS = 4
HQ = HEADS // QUADS
NB = T // P
KB = KEYS // P
KC = D // P
HALVES = 2
COLS = T + KEYS
EPS = 1e-5
SCALE = DH ** -0.5
Q_PART = (0, 0, 1, 1, 0, 2)
K_PART = (0, 1, 0, 1, 2, 0)
TERMS = len(Q_PART)
SROWS = TERMS * DH
MROWS = 2 * HQ
E, FF, GD = 8, 1024, 16
FC = FF // P
TOK = B * T
CAP = TOK + P
DUMMY = E * CAP
ROW = D + 4
TILES = 40
NOTOK = 1 << 20
MASKED = -1e30


class Count:

    def __init__(self, sem, base=0):
        self.sem, self.base, self.n = sem, base, 0

    def add(self, ins, k=1):
        ins.then_inc(self.sem, k)
        self.n += k
        return ins

    def wait(self, eng):
        eng.wait_ge(self.sem, self.base + self.n)


def peel(count, body):
    for p in range(count):
        body(p)


def wait(eng, sem, value):
    if not isinstance(value, int) or value > 0:
        eng.wait_ge(sem, value)


def project(nc, c, x, ctx, wq, wkv, parts_d, v_d):
    with ExitStack() as s:
        def sb(name, shape, dt):
            return s.enter_context(nc.sbuf_tensor(name, shape, dt))

        def sem(name):
            return s.enter_context(nc.semaphore(name))

        wq_s = sb("wq_s", [P, KC, D], F32)
        wkv_s = sb("wkv_s", [P, KC, 2 * D], F32)
        xc = [sb(f"xc{p}", [P, KB, D], F32) for p in range(2)]
        st = sb("st1", [P, NB, 6], F32)
        mv = sb("mv1", [P, NB, 2], F32)
        ve = sb("ve1", [P, NB], F32)
        rs = sb("rs1", [P, NB], F32)
        xcT = sb("xcT", [P, KC, KEYS], F32)
        part = [sb(f"part{p}", [P, 3, COLS], BF16) for p in range(HALVES)]
        rest = [sb(f"rest{p}", [P, T], F32) for p in range(2)]
        vs = sb("vs", [P, QUADS, KB, HQ, 32], F32)
        psT = [s.enter_context(nc.psum_tensor(f"psT{p}", [P, 512], F32)) for p in range(2)]
        psQ = [s.enter_context(nc.psum_tensor(f"psQ{p}", [P, 512], F32)) for p in range(3)]
        psV = [s.enter_context(nc.psum_tensor(f"psV{p}", [P, 2, D], F32)) for p in range(2)]

        w_in = sem("w_in")
        x_in = [sem(f"x_in{p}") for p in range(2)]
        stat_done, mean_done, var_done, rstd_done, norm_done = (
            sem(n) for n in ("stat_done", "mean_done", "var_done", "rstd_done", "norm_done"))
        tr_done, tr_out = sem("tr_done"), sem("tr_out")
        qk_done, first_out, rest_out, second_out, third_out = (
            sem(n) for n in ("qk_done", "first_out", "rest_out", "second_out", "third_out"))
        v_done, v_out = sem("v_done"), sem("v_out")
        ones_set = sem("ones_set")
        passed_pool, passed_dve = sem("passed_pool1"), sem("passed_dve1")
        part_st = [sem(f"part_st{h}") for h in range(HALVES)]
        v_st = sem("v_st")
        UN = 3 * HALVES

        with nc.Block() as block:
            @block.sync
            def _(sp):
                sp.dma_start(wq_s[:], wq.rearrange("(c p) n -> p c n", p=P)).then_inc(w_in, 16)
                sp.dma_start(wkv_s[:], wkv.rearrange("(c p) n -> p c n", p=P)).then_inc(w_in, 16)

                def load(b, p):
                    sp.dma_start(xc[p][:, 0:NB, :], ctx[bass.ds(b, 1)].rearrange("a (n p) d -> p (a n) d", p=P)).then_inc(x_in[p], 16)
                    sp.dma_start(xc[p][:, NB:KB, :], x[bass.ds(b, 1)].rearrange("a (n p) d -> p (a n) d", p=P)).then_inc(x_in[p], 16)

                load(0, 0)
                load(1, 1)

                def store(b):
                    for hf in range(HALVES):
                        wait(sp, third_out, UN * b + 3 * (hf + 1))
                        sp.wait_ge(first_out, UN * b + 3 * (hf + 1))
                        sp.dma_start(parts_d[bass.ds(b, 1), hf].rearrange("a c p n -> p (a c) n"), part[hf][:]).then_inc(part_st[hf], 16)
                    wait(sp, v_out, 4 * b + 4)
                    sp.dma_start(v_d[bass.ds(b, 1)].rearrange("a p n -> p (a n)"),
                                 vs[:].rearrange("p a b c d -> p (a b c d)")).then_inc(v_st, 16)

                with sp.Fori(0, B // 2 - 1) as i:
                    for p in range(2):
                        b = 2 * i + p
                        sp.wait_ge(tr_done, 4 * b + 4)
                        load(b + 2, p)
                        store(b)
                for p in range(2):
                    store(B - 2 + p)
                for hf in range(HALVES):
                    wait(sp, part_st[hf], 16 * B)
                wait(sp, v_st, 16 * B)

            @block.gpsimd
            def _(pool):
                pool.memset(vs[:], 1.0).then_inc(ones_set, 1)

                def body(b, p):
                    pool.wait_ge(mean_done, b + 1)
                    pool.sem_inc(passed_pool, 1)
                    pool.tensor_scalar(ve[:], mv[:, :, 1], EPS, None, ALU.add).then_inc(var_done, 1)
                    pool.wait_ge(var_done, b + 1)
                    pool.tensor_tensor(rs[:], ve[:], c["mhalf"][:, 0:NB], ALU.pow).then_inc(rstd_done, 1)
                    for u in range(UN):
                        hf, k = divmod(u, 3)
                        r = rest[u % 2]
                        wait(pool, rest_out, UN * b + u + 1)
                        pool.sem_inc(passed_pool, 1)
                        pool.tensor_copy(part[hf][:, 1, k * 512:(k + 1) * 512], r[:]).then_inc(second_out, 1)
                        pool.wait_ge(second_out, UN * b + u + 1)
                        pool.tensor_tensor(part[hf][:, 2, k * 512:(k + 1) * 512], r[:],
                                           part[hf][:, 1, k * 512:(k + 1) * 512], ALU.subtract).then_inc(third_out, 1)

                peel(2, lambda p: body(p, p))
                with pool.Fori(1, B // 2) as i:
                    for p in range(2):
                        body(2 * i + p, p)

            @block.vector
            def _(dve):
                def body(i, p):
                    b = 2 * i + p
                    X = xc[p][:, NB:KB, :]
                    dve.wait_ge(x_in[p], 32 * i + 32)
                    for n in range(NB):
                        dve.bn_stats(st[:, n, :], X[:, n, :]).then_inc(stat_done, 1)
                    dve.wait_ge(stat_done, NB * b + NB)
                    dve.sem_inc(passed_dve, 1)
                    for n in range(NB):
                        ins = dve.bn_aggr(mv[:, n, :], st[:, n, :])
                    ins.then_inc(mean_done, 1)
                    dve.wait_ge(mean_done, b + 1)
                    dve.wait_ge(rstd_done, b + 1)
                    for n in range(NB):
                        ins = dve.tensor_scalar(X[:, n, :], X[:, n, :], mv[:, n, 0:1], rs[:, n:n + 1], ALU.subtract, ALU.mult)
                    ins.then_inc(norm_done, 1)
                    for u in range(UN):
                        hf, k = divmod(u, 3)
                        dve.wait_ge(first_out, UN * b + u + 1)
                        wait(dve, third_out, UN * b + max(u - 1, 0))
                        dve.scalar_tensor_tensor(rest[u % 2][:], psQ[u % 3][:], SCALE if k == 0 else 1.0,
                                                 part[hf][:, 0, k * 512:(k + 1) * 512], ALU.mult, ALU.subtract).then_inc(rest_out, 1)

                peel(2, lambda p: body(0, p))
                with dve.Fori(1, B // 2) as i:
                    for p in range(2):
                        body(i, p)

            @block.scalar
            def _(act):
                def body(i, p):
                    b = 2 * i + p
                    for t in range(4):
                        act.wait_ge(tr_done, 4 * b + t + 1)
                        k, half = t // 2, t % 2
                        act.activation(xcT[:, k, half * 512:(half + 1) * 512], psT[t % 2][:], ACT.Copy).then_inc(tr_out, 1)
                    for u in range(UN):
                        hf, k = divmod(u, 3)
                        act.wait_ge(qk_done, UN * b + u + 1)
                        if k == 0:
                            wait(act, part_st[hf], 16 * b)
                        act.activation(part[hf][:, 0, k * 512:(k + 1) * 512], psQ[u % 3][:], ACT.Copy,
                                       scale=SCALE if k == 0 else 1.0).then_inc(first_out, 1)
                    wait(act, v_st, 16 * b)
                    for t in range(4):
                        act.wait_ge(v_done, 4 * b + t + 1)
                        for n in range(2):
                            ins = act.activation(vs[:, :, 2 * t + n, :, 0:DH],
                                                 psV[t % 2][:, n, :].rearrange("p (q h d) -> p q h d", q=QUADS, h=HQ), ACT.Copy)
                        ins.then_inc(v_out, 1)
                act.wait_ge(ones_set, 1)
                peel(2, lambda p: body(0, p))
                with act.Fori(1, B // 2) as i:
                    for p in range(2):
                        body(i, p)

            @block.tensor
            def _(pe):
                pe.wait_ge(w_in, 32)

                def body(i, p):
                    b = 2 * i + p
                    for t in range(4):
                        k, half = t // 2, t % 2
                        if t == 0:
                            pe.wait_ge(x_in[p], 32 * i + 32)
                        if t == 1:
                            pe.wait_ge(norm_done, b + 1)
                        wait(pe, tr_out, 4 * b + max(t - 1, 0))
                        for n in range(NB):
                            ins = pe.transpose(psT[t % 2][:, n * P:(n + 1) * P],
                                               xc[p][:, NB * half + n, k * P:(k + 1) * P], c["ident"][:])
                        ins.then_inc(tr_done, 1)
                    wait(pe, tr_out, 4 * b + 4)
                    for u in range(UN):
                        hf, k = divmod(u, 3)
                        wait(pe, rest_out, UN * b + max(u - 2, 0))
                        for kc in range(KC):
                            w = wq_s[:, kc, hf * P:(hf + 1) * P] if k == 0 else wkv_s[:, kc, hf * P:(hf + 1) * P]
                            cols = slice(TM, KEYS) if k == 0 else slice((k - 1) * 512, k * 512)
                            ins = pe.matmul(psQ[u % 3][:], w, xcT[:, kc, cols], start=kc == 0, stop=kc == KC - 1)
                        ins.then_inc(qk_done, 1)
                    for t in range(4):
                        wait(pe, v_out, 4 * b + max(t - 1, 0))
                        for n in range(2):
                            for kc in range(KC):
                                ins = pe.matmul(psV[t % 2][:, n, :], xcT[:, kc, (2 * t + n) * P:(2 * t + n + 1) * P],
                                                wkv_s[:, kc, D:2 * D], start=kc == 0, stop=kc == KC - 1)
                        ins.then_inc(v_done, 1)

                peel(2, lambda p: body(0, p))
                with pe.Fori(1, B // 2) as i:
                    for p in range(2):
                        body(i, p)


def w1_views(c, w):
    n = 2 * KC * 2 * FF
    v = c["W1"][:, w * n:(w + 1) * n].rearrange("p (k a n) -> p k a n", a=2, n=FF)
    return v[:, :, 0, :], v[:, :, 1, :], c[f"wide{w % 2}"][:].rearrange("p (k n) -> p k n", n=FF)


def load_w1(sp, c, w1, w, w1_in):
    sp.dma_start(w1_views(c, w)[2], w1[2 * w:2 * w + 2].rearrange("e (k p) n -> p (e k) n", p=P)).then_inc(w1_in[w % 2], 16)


def high_w1(act, c, w, w1_in, w1_hi):
    hi, lo, t = w1_views(c, w)
    act.wait_ge(w1_in[w % 2], 16)
    act.activation(hi, t, ACT.Copy).then_inc(w1_hi, 1)


def low_w1(eng, c, w, w1_hi):
    hi, lo, t = w1_views(c, w)
    eng.wait_ge(w1_hi, w % 2 + 1)
    return eng.tensor_tensor(lo, t, hi, ALU.subtract)


def attend(nc, c, x, w1, w2, parts_d, v_d, rows_d):
    N_M = 3
    N_T = 18
    N_TL = 7
    with ExitStack() as s:
        def sb(name, shape, dt):
            return s.enter_context(nc.sbuf_tensor(name, shape, dt))

        def sem(name):
            return s.enter_context(nc.semaphore(name))

        NQ, NK, NV = HQ * T, HQ * KEYS, KB * HQ * 32 * 2
        at = lambda q, lo, n: c["W1"][:, q * (NQ + NK + NV) + lo:q * (NQ + NK + NV) + lo + n]
        qs = [at(q, 0, NQ).rearrange("p (h n) -> p h n", h=HQ) for q in range(QUADS)]
        ks = [at(q, NQ, NK).rearrange("p (h n) -> p h n", h=HQ) for q in range(QUADS)]
        vq = [at(q, NQ + NK, NV).bitcast(F32).rearrange("p (k h d) -> p k h d", k=KB, h=HQ) for q in range(QUADS)]
        pr = [c[f"wide{p}"][:].rearrange("p (h n) -> p h n", h=HQ) for p in range(2)]
        stage = [sb(f"stage{p}", [P, FC * D // 2], F32) for p in range(2)]
        mx = sb("mx", [P, NB, HQ, 2], F32)
        nm = sb("nm", [P, NB, HQ], F32)
        mp = sb("mp", [P, NB, 2, HQ], BF16)
        mT = [sb(f"mT{p}", [MROWS, T], BF16) for p in range(2)]
        osb = sb("osb", [P, T], F32)
        lsum = sb("lsum", [P, T], F32)
        ot = [sb(f"ot{q}", [P, T], F32) for q in range(QUADS)]
        xres = sb("xres", [P, NB, D], F32)
        row = sb("row", [P, NB, ROW], F32)
        st = sb("st2", [P, NB, 6], F32)
        mv = sb("mv2", [P, NB, 2], F32)
        ve = sb("ve2", [P, NB], F32)
        rs = sb("rs2", [P, NB], F32)
        hT = sb("hT", [P, KC, T], F32)
        redT = sb("redT", [GD, T], F32)
        lg = sb("lg", [P, NB, E], F32)
        lmax = sb("lmax", [P, NB], F32)
        dif = sb("dif", [P, NB, E], F32)
        ex = sb("ex", [P, NB, E], F32)
        esum = sb("esum", [P, NB], F32)
        einv = sb("einv", [P, NB], F32)
        eq = sb("eq", [P, NB, E], F32)
        cand = sb("cand", [P, NB, E], F32)
        cmin = sb("cmin", [P, NB], F32)
        oh = sb("oh", [P, NB, E], BF16)
        cumr = sb("cumr", [P, NB, E], F32)
        pick = sb("pick", [P, NB, E], F32)
        slot = sb("slot", [P, NB], F32)
        slots = [sb(f"slots{n}", [P, 1], U32) for n in range(NB)]

        psS = [s.enter_context(nc.psum_tensor(f"psS{p}", [P, 1024], F32)) for p in range(2)]
        psA = [s.enter_context(nc.psum_tensor(f"psA{p}", [P, 512], F32)) for p in range(2)]
        psO = s.enter_context(nc.psum_tensor("psO", [P, 512], F32))
        psM = s.enter_context(nc.psum_tensor("psM", [P, 512], F32))

        w2_in, w1_in = ([sem(f"{n}{p}") for p in range(2)] for n in ("w2_in", "w1_in"))
        w2_hi, w2_lo, w1_hi = sem("w2_hi"), sem("w2_lo"), sem("w1_hi")
        stk_in = [sem(f"stk_in{q}") for q in range(QUADS)]
        v_in = [sem(f"v_in{q}") for q in range(QUADS)]
        sel_set, sel_fix = sem("sel_set"), sem("sel_fix")
        s_done, exp_done, pv_done = sem("s_done"), sem("exp_done"), sem("pv_done")
        a_done, max_done = sem("a_done"), sem("max_done")
        shift_made, shift_tr, shift_out, shift_in = (sem(n) for n in ("shift_made", "shift_tr", "shift_out", "shift_in"))
        o_out, l_out, r_out, ot_done = (sem(n) for n in ("o_out", "l_out", "r_out", "ot_done"))
        x_in = sem("xres_in")
        tl_done, tl_out = sem("tl_done"), sem("tl_out")
        chain = sem("chain")
        ve_done, rstd_done = sem("ve_done"), sem("rstd2_done")
        ex_done = sem("ex_done")
        idx_ready, row_out = sem("idx_ready"), sem("row_out")
        passed_pool, passed_dve = sem("passed_pool2"), sem("passed_dve2")
        C_MEAN, C_HN, C_DIF, C_OH = 4, 6, 8, 12

        def spans(g):
            if g < 2:
                return [(2 * g, 0, 0), (2 * g + 1, 0, 512)]
            if g == 2:
                return [(NB, 0, 0), (NB + 1, P, 512)]
            return [(NB + 2, 2 * P, 0), (NB + 3, 3 * P, 2 * P)]

        def width(g):
            kb, q0, at = spans(g)[1]
            return at + T - q0

        def row_units(quad_h):
            for i in range(NB):
                yield i, 0, TM
                yield i, TM, (i + 1) * P

        def ahead(q, u, last):
            k = 2 * u
            d = 1 if k < 16 else 2
            if last and q + d >= QUADS:
                return None
            return d, (2 + k // 8) % HQ, k % 8

        def iterate(eng, body):
            body(0, True, False)
            with eng.Fori(1, B - 1) as b:
                body(b, False, False)
            body(B - 1, False, True)

        with nc.Block() as block:
            @block.sync
            def _(sp):
                def load_stack(b, q):
                    hf, o = divmod(q * HQ * DH, P)
                    for t in range(TERMS):
                        for dst, part, lo, hi in ((qs[q], Q_PART[t], 0, T), (ks[q], K_PART[t], T, COLS)):
                            sp.dma_start(dst[DH * t:DH * (t + 1), :, :],
                                         parts_d[bass.ds(b, 1), hf, part, o:o + HQ * DH, lo:hi]
                                         .rearrange("a (h d) n -> d (a h) n", h=HQ)).then_inc(stk_in[q], 16)

                def load_v(b, q):
                    sp.dma_start(vq[q].rearrange("p k h d -> p (k h d)"),
                                 v_d[bass.ds(b, 1), :, q * 1024:(q + 1) * 1024].rearrange("a p n -> p (a n)")).then_inc(v_in[q], 16)

                def load_x(b):
                    sp.dma_start(xres[:], x[bass.ds(b, 1)].rearrange("a (n p) d -> p (a n) d", p=P)).then_inc(x_in, 16)

                def send_shift(n, q):
                    sp.wait_ge(shift_out, n + 1)
                    src = mT[q % 2]
                    sp.dma_start(qs[q][SROWS:SROWS + MROWS, :, :],
                                 src[:].unsqueeze(1).to_broadcast([MROWS, HQ, T])).then_inc(shift_in, 16)

                for q in range(3):
                    load_stack(0, q)
                    load_v(0, q)
                send_shift(0, 0)

                def body(b, first, last):
                    for q in range(QUADS):
                        n = b * QUADS + q
                        bn, qn = (b, q + 3) if q == 0 else (b + 1, q - 1)
                        if q == 0 or not last:
                            wait(sp, s_done, 16 * n)
                            load_stack(bn, qn)
                            wait(sp, pv_done, 4 * n)
                            load_v(bn, qn)
                        if q == 2:
                            if not first:
                                sp.wait_ge(tl_out, N_TL * (b - 1) + 4)
                            load_x(b)
                        if q < 2:
                            wait(sp, w2_lo, 2 * b + q - 1)
                            sp.dma_start(stage[q][:].rearrange("p (k n) -> p k n", n=D),
                                         w2[bass.ds(b, 1), q * FF // 2:(q + 1) * FF // 2, :]
                                         .rearrange("a (k p) n -> p (a k) n", p=P)).then_inc(w2_in[q], 16)
                        if not (last and q == QUADS - 1):
                            send_shift(n + 1, (q + 1) % QUADS)

                iterate(sp, body)
                sp.wait_ge(pv_done, 4 * B * QUADS)
                for w in range(2):
                    load_w1(sp, c, w1, w, w1_in)

            @block.gpsimd
            def _(pool):
                for q in range(QUADS):
                    pool.memset(ks[q][SROWS:SROWS + MROWS], 0.0).then_inc(sel_set, 1)
                for part in range(2):
                    pool.wait_ge(sel_set, QUADS * (part + 1))
                    for q in range(QUADS):
                        v = ks[q][SROWS:SROWS + MROWS]
                        pool.affine_select(out=v, in_=v, compare_op=ALU.not_equal, fill=1.0, base=-HQ * part,
                                           pattern=[[-1, HQ], [0, KEYS]], channel_multiplier=1).then_inc(sel_set, 1)

                def rstd(tb):
                    pool.wait_ge(chain, N_T * tb + C_MEAN)
                    pool.sem_inc(passed_pool, 1)
                    pool.tensor_scalar(ve[:], mv[:, :, 1], EPS, None, ALU.add).then_inc(ve_done, 1)
                    pool.wait_ge(ve_done, tb + 1)
                    pool.tensor_tensor(rs[:], ve[:], c["mhalf"][:, 0:NB], ALU.pow).then_inc(rstd_done, 1)

                def scatter(tb):
                    pool.wait_ge(idx_ready, tb + 1)
                    pool.sem_inc(passed_pool, 1)
                    for n in range(NB):
                        pool.indirect_dma_start(rows_d[:, :], bass.IndirectOffsetOnAxis(ap=slots[n][:, 0:1], axis=0),
                                                row[:, n, :], None).then_inc(row_out, 16)

                def body(b, first, last):
                    for q in range(QUADS):
                        n = b * QUADS + q
                        if not (first and q == 0):
                            pq = (q - 1) % QUADS
                            pool.wait_ge(r_out, n)
                            if pq == 0:
                                wait(pool, tl_done, 0 if first else N_TL * (b - 1) + 2)
                            pool.tensor_tensor(ot[pq][:], osb[:], lsum[:], ALU.mult).then_inc(ot_done, 1)
                        if q in (1, 3):
                            k = q // 2
                            v = c["W2"][:, bass.ds(b * (FC * 2 * D) + k * FC * D, FC * D)].rearrange("p (k a n) -> p k a n", a=2, n=D)
                            t = stage[k][:].rearrange("p (k n) -> p k n", n=D)
                            pool.wait_ge(w2_in[k], 16 * (b + 1))
                            pool.sem_inc(passed_pool, 1)
                            pool.tensor_copy(v[:, :, 0, :], t).then_inc(w2_hi, 1)
                            pool.wait_ge(w2_hi, 2 * b + k + 1)
                            pool.sem_inc(passed_pool, 1)
                            pool.tensor_tensor(v[:, :, 1, :], t, v[:, :, 0, :], ALU.subtract).then_inc(w2_lo, 1)
                        if not first:
                            if q == 0:
                                rstd(b - 1)
                            if q == 2:
                                scatter(b - 1)
                                pool.wait_ge(row_out, 16 * NB * b)

                iterate(pool, body)
                pool.wait_ge(r_out, B * QUADS)
                pool.tensor_tensor(ot[QUADS - 1][:], osb[:], lsum[:], ALU.mult).then_inc(ot_done, 1)
                rstd(B - 1)
                low_w1(pool, c, 0, w1_hi)
                scatter(B - 1)
                low_w1(pool, c, 1, w1_hi)
                pool.wait_ge(row_out, 16 * NB * B)

            @block.vector
            def _(dve):
                def maxima(w, h, unit):
                    i, lo, nk = list(row_units(h))[unit]
                    dve.wait_ge(a_done, w + 1)
                    dve.tensor_reduce(mx[:, i, h, unit % 2:unit % 2 + 1], psA[unit % 2][:, 0:nk], AX.X, ALU.max).then_inc(max_done, 1)

                def shift(n):
                    dve.wait_ge(max_done, 32 * (n + 1))
                    dve.tensor_reduce(nm[:], mx[:], AX.X, ALU.max, negate=True).then_inc(shift_made, 1)
                    dve.wait_ge(shift_made, N_M * n + 1)
                    wait(dve, shift_tr, n)
                    dve.tensor_copy(mp[:, :, 0, :], nm[:]).then_inc(shift_made, 1)
                    dve.wait_ge(shift_made, N_M * n + 2)
                    dve.tensor_tensor(mp[:, :, 1, :], nm[:], mp[:, :, 0, :], ALU.subtract).then_inc(shift_made, 1)

                def sums(n):
                    dve.wait_ge(o_out, n + 1)
                    wait(dve, ot_done, n)
                    dve.sem_inc(passed_dve, 1)
                    dve.stream_shuffle(lsum[:], osb[:], [DH + k % DH for k in range(32)]).then_inc(l_out, 1)
                    dve.wait_ge(l_out, n + 1)
                    dve.reciprocal(lsum[:], lsum[:]).then_inc(r_out, 1)

                for w in range(48):
                    maxima(w, w // 8 % HQ, w % 8)
                    if w == 31:
                        shift(0)

                def tail(tb):
                    k = Count(chain, N_T * tb)
                    bc = lambda a: a.unsqueeze(2).to_broadcast([P, NB, E])

                    def x1(r):
                        if r == 0:
                            dve.wait_ge(x_in, 16 * tb + 16)
                        dve.wait_ge(tl_done, N_TL * tb + r + 1)
                        ins = dve.tensor_tensor(row[:, 2 * r:2 * r + 2, 0:D], psM[:].rearrange("p (n d) -> p n d", d=D),
                                                xres[:, 2 * r:2 * r + 2, :], ALU.add)
                        ins.then_inc(tl_out, 1)

                    def stats():
                        dve.wait_ge(tl_out, N_TL * tb + 2)
                        k.add(dve.tensor_copy(row[:, :, D + 3:D + 4].bitcast(I32), c["tokf"][:].unsqueeze(2)))
                        k.wait(dve)
                        k.add(dve.tensor_scalar(c["tokf"][:], c["tokf"][:], float(T), None, ALU.add))
                        for n in range(NB):
                            ins = dve.bn_stats(st[:, n, :], row[:, n, 0:D])
                        k.add(ins)
                        k.wait(dve)
                        dve.sem_inc(passed_dve, 1)
                        for n in range(NB):
                            ins = dve.bn_aggr(mv[:, n, :], st[:, n, :])
                        k.add(ins)
                        assert k.n == C_MEAN

                    def norm():
                        dve.wait_ge(rstd_done, tb + 1)
                        k.wait(dve)
                        dve.tensor_copy(row[:, :, D:D + 1], rs[:].unsqueeze(2))
                        k.add(dve.scalar_tensor_tensor(row[:, :, D + 1:D + 2], mv[:, :, 0:1], -1.0, rs[:].unsqueeze(2), ALU.mult, ALU.mult))
                        k.wait(dve)
                        for n in range(NB):
                            ins = dve.tensor_scalar(xres[:, n, :], row[:, n, 0:D], rs[:, n:n + 1], row[:, n, D + 1:D + 2], ALU.mult, ALU.add)
                        k.add(ins)
                        assert k.n == C_HN

                    def route():
                        dve.wait_ge(tl_done, N_TL * tb + 6)
                        dve.tensor_copy(lg[:], psM[:, 0:NB * E].rearrange("p (n e) -> p n e", e=E)).then_inc(tl_out, 1)
                        dve.wait_ge(tl_out, N_TL * tb + 6)
                        k.add(dve.tensor_reduce(lmax[:], lg[:], AX.X, ALU.max))
                        k.wait(dve)
                        k.add(dve.tensor_tensor(dif[:], lg[:], bc(lmax[:]), ALU.subtract))
                        assert k.n == C_DIF
                        k.add(dve.tensor_tensor(eq[:], lg[:], bc(lmax[:]), ALU.is_equal))
                        k.wait(dve)
                        k.add(dve.scalar_tensor_tensor(cand[:], eq[:], -float(E), c["eiota"][:], ALU.mult, ALU.add))
                        k.wait(dve)
                        k.add(dve.tensor_reduce(cmin[:], cand[:], AX.X, ALU.min))
                        k.wait(dve)
                        k.add(dve.tensor_tensor(oh[:], cand[:], bc(cmin[:]), ALU.is_equal))
                        assert k.n == C_OH
                        dve.wait_ge(ex_done, tb + 1)
                        k.add(dve.tensor_reduce(esum[:], ex[:], AX.X, ALU.add))
                        k.wait(dve)
                        k.add(dve.reciprocal(einv[:], esum[:]))
                        k.wait(dve)
                        k.add(dve.tensor_scalar(row[:, :, D + 2:D + 3], einv[:].unsqueeze(2), c["tgf"][:, 0:1], None, ALU.mult))

                    def place():
                        dve.wait_ge(tl_done, N_TL * tb + 7)
                        run = c["run"]
                        k.add(dve.tensor_tensor(cumr[:], psM[:, 0:NB * E].rearrange("p (n e) -> p n e", e=E),
                                                run[:].unsqueeze(1).to_broadcast([P, NB, E]), ALU.add))
                        k.wait(dve)
                        dve.tensor_tensor(run[:], run[:], psM[:, NB * E:NB * E + E], ALU.add).then_inc(tl_out, 1)
                        k.add(dve.tensor_tensor(pick[:], cumr[:], oh[:], ALU.mult))
                        k.wait(dve)
                        k.add(dve.tensor_reduce(slot[:], pick[:], AX.X, ALU.add))
                        k.wait(dve)
                        for n in range(NB):
                            ins = dve.tensor_copy(slots[n][:], slot[:, n:n + 1])
                        ins.then_inc(idx_ready, 1)
                        assert k.n == N_T, k.n

                    return [lambda: x1(0), lambda: x1(1), stats, norm, route, place]

                def body(b, first, last):
                    for q in range(QUADS):
                        n = b * QUADS + q
                        for u in range(16):
                            if u == 8 and not (last and q == QUADS - 1):
                                shift(n + 1)
                            a = ahead(q, u, last)
                            if a:
                                d, h, unit = a
                                for k in range(2):
                                    maxima(32 * n + 48 + 2 * u + k, h, unit + k)
                            if u == 4 and not (first and q == 0):
                                sums(n - 1)
                            if not first and (q, u) in TAIL_DVE:
                                step(b, TAIL_DVE[q, u])

                TAIL_DVE = {(0, 9): 0, (0, 15): 1, (1, 0): 2, (1, 2): 3, (2, 4): 4, (2, 10): 5}
                tails = {}

                def step(b, j):
                    if j == 0:
                        tails["now"] = tail(b - 1)
                    tails["now"][j]()

                iterate(dve, body)
                sums(B * QUADS - 1)
                for f in tail(B - 1):
                    f()

            @block.scalar
            def _(act):
                act.wait_ge(shift_tr, 1)
                act.activation(mT[0][:], psM[0:MROWS, :], ACT.Copy).then_inc(shift_out, 1)

                def tail_copy(tb, j):
                    if j == 0 or j == 1:
                        act.wait_ge(tl_done, N_TL * tb + 3 + j)
                        act.activation(hT[:, j, :], psM[:], ACT.Copy).then_inc(tl_out, 1)
                    if j == 2:
                        act.wait_ge(tl_done, N_TL * tb + 5)
                        act.activation(redT[:], psM[0:GD, :], ACT.Copy).then_inc(tl_out, 1)
                    if j == 3:
                        act.wait_ge(chain, N_T * tb + C_DIF)
                        act.activation(ex[:], dif[:], ACT.Exp).then_inc(ex_done, 1)

                TAIL_ACT = {(1, 5): 0, (1, 8): 1, (1, 14): 2, (2, 4): 3}

                def body(b, first, last):
                    for q in range(QUADS):
                        n = b * QUADS + q
                        for g in range(4):
                            for h in range(HQ):
                                u = 4 * g + h
                                act.wait_ge(s_done, 16 * n + u + 1)
                                if not (first and q == 0 and g < 2):
                                    wait(act, pv_done, 4 * n + g - 1)
                                act.activation(pr[g % 2][:, h, 0:width(g)], psS[u % 2][:, 0:width(g)], ACT.Exp).then_inc(exp_done, 1)
                                if u == 2 and not (first and q == 0):
                                    act.wait_ge(pv_done, 4 * n)
                                    wait(act, ot_done, n - 1)
                                    act.activation(osb[:], psO[:], ACT.Copy).then_inc(o_out, 1)
                                if u == 11 and not (last and q == QUADS - 1):
                                    nn, qq = n + 1, (q + 1) % QUADS
                                    act.wait_ge(shift_tr, nn + 1)
                                    wait(act, shift_in, 16 * n)
                                    act.activation(mT[qq % 2][:], psM[0:MROWS, :], ACT.Copy).then_inc(shift_out, 1)
                                if not first and (q, u) in TAIL_ACT:
                                    tail_copy(b - 1, TAIL_ACT[q, u])

                iterate(act, body)
                act.wait_ge(pv_done, 4 * B * QUADS)
                act.wait_ge(ot_done, B * QUADS - 1)
                act.activation(osb[:], psO[:], ACT.Copy).then_inc(o_out, 1)
                high_w1(act, c, 0, w1_in, w1_hi)
                for j in range(4):
                    tail_copy(B - 1, j)
                high_w1(act, c, 1, w1_in, w1_hi)

            @block.tensor
            def _(pe):
                def row_scores(w, q, h, unit):
                    i, lo, nk = list(row_units(h))[unit]
                    ps = psA[unit % 2]
                    wait(pe, max_done, w - 1)
                    causal = lo > 0
                    ins = pe.matmul(ps[:, 0:nk], qs[q][0:SROWS, h, i * P:(i + 1) * P], ks[q][0:SROWS, h, lo:lo + nk],
                                    start=True, stop=not causal)
                    if causal:
                        ins = pe.matmul(ps[:, nk - P:nk], c["identb"][:], c["mask_q"][:], start=False, stop=True)
                    ins.then_inc(a_done, 1)

                def shift_rows(n):
                    pe.wait_ge(shift_made, N_M * (n + 1))
                    for i in range(NB):
                        ins = pe.matmul(psM[0:MROWS, i * P:(i + 1) * P], mp[:, i].rearrange("p a h -> p (a h)"), c["identb"][:],
                                        start=True, stop=True)
                    ins.then_inc(shift_tr, 1)

                def key_scores(n, q, g, h, tile0):
                    u = 4 * g + h
                    if not (tile0 and u < 2):
                        wait(pe, exp_done, 16 * n + u - 1)
                    ps = psS[u % 2]
                    for kb, q0, at in spans(g):
                        nq = T - q0
                        causal = kb >= NB
                        ins = pe.matmul(ps[:, at:at + nq], ks[q][0:SROWS + MROWS, h, kb * P:(kb + 1) * P],
                                        qs[q][0:SROWS + MROWS, h, q0:T], start=True, stop=not causal)
                        if causal:
                            ins = pe.matmul(ps[:, at:at + P], c["identb"][:], c["mask_k"][:], start=False, stop=True)
                    ins.then_inc(s_done, 1)

                def values(n, q, g):
                    wait(pe, exp_done, 16 * n + 4 * g + 4)
                    for kb, q0, at in spans(g):
                        for h in range(HQ):
                            ins = pe.matmul(psO[32 * h:32 * h + 32, q0:T], vq[q][:, kb, h, :], pr[g % 2][:, h, at:at + T - q0],
                                            start=kb == 0, stop=kb == KB - 1)
                    ins.then_inc(pv_done, 1)

                def tail(tb, j):
                    if j > 0:
                        pe.wait_ge(tl_out, N_TL * tb + j)
                    if j < 2:
                        pe.wait_ge(ot_done, QUADS * tb + QUADS)
                        for n in range(2):
                            for q in range(QUADS):
                                ins = pe.matmul(psM[:, n * D:(n + 1) * D], ot[q][:, (2 * j + n) * P:(2 * j + n + 1) * P],
                                                c["wout"][:, q, :], start=q == 0, stop=q == QUADS - 1)
                    elif j < 4:
                        pe.wait_ge(chain, N_T * tb + C_HN)
                        for n in range(NB):
                            ins = pe.transpose(psM[:, n * P:(n + 1) * P], xres[:, n, (j - 2) * P:(j - 1) * P], c["ident"][:])
                    elif j == 4:
                        for k in range(KC):
                            ins = pe.matmul(psM[0:GD, :], c["wred"][:, k, :], hT[:, k, :], start=k == 0, stop=k == KC - 1)
                    elif j == 5:
                        for n in range(NB):
                            ins = pe.matmul(psM[:, n * E:(n + 1) * E], redT[:, n * P:(n + 1) * P], c["wgT"][:], start=True, stop=True)
                    else:
                        pe.wait_ge(chain, N_T * tb + C_OH)
                        o = oh[:].rearrange("p n e -> p (n e)")
                        pe.matmul(psM[:, 0:NB * E], c["before"][:], o, start=True, stop=False, skip_group_check=True)
                        for m in range(1, NB):
                            pe.matmul(psM[:, m * E:NB * E], c["onesb"][:], o[:, 0:(NB - m) * E], start=False, stop=False,
                                      skip_group_check=True)
                        for m in range(NB):
                            ins = pe.matmul(psM[:, NB * E:NB * E + E], c["onesb"][:], o[:, m * E:(m + 1) * E], start=False,
                                            stop=m == NB - 1, skip_group_check=True)
                    ins.then_inc(tl_done, 1)

                TAIL_PE = {(0, 7): 0, (0, 14): 1, (1, 4): 2, (1, 7): 3, (1, 13): 4, (2, 2): 5, (2, 7): 6}

                for w in range(48):
                    if w == 0:
                        pe.wait_ge(stk_in[0], 16 * 2 * TERMS)
                    if w == 32:
                        pe.wait_ge(stk_in[1], 16 * 2 * TERMS)
                    row_scores(w, w // 32, w // 8 % HQ, w % 8)
                shift_rows(0)
                pe.wait_ge(sel_set, 3 * QUADS)

                def body(b, first, last):
                    done = 0
                    for q in range(QUADS):
                        n = b * QUADS + q
                        tile0 = first and q == 0
                        pe.wait_ge(shift_in, 16 * (n + 1))
                        for g in range(4):
                            for h in range(HQ):
                                u = 4 * g + h
                                key_scores(n, q, g, h, tile0)
                                if h == 1:
                                    if g == 0 and not tile0:
                                        values(n - 1, (q - 1) % QUADS, 3)
                                    if g == 1:
                                        pe.wait_ge(v_in[q], 16 * (b + 1))
                                        wait(pe, o_out, n)
                                    if g > 0:
                                        values(n, q, g - 1)
                                a = ahead(q, u, last)
                                if a:
                                    d, hh, unit = a
                                    qq = (q + d) % QUADS
                                    if u == 8:
                                        pe.wait_ge(stk_in[qq], 16 * 2 * TERMS * (b + 1 + (q + d) // QUADS))
                                    for k in range(2):
                                        row_scores(32 * n + 48 + 2 * u + k, qq, hh, unit + k)
                                if u == 11 and not (last and q == QUADS - 1):
                                    pe.wait_ge(shift_out, n + 1)
                                    if not first:
                                        pe.wait_ge(tl_out, N_TL * (b - 1) + done)
                                    shift_rows(n + 1)
                                if not first and (q, u) in TAIL_PE:
                                    pe.wait_ge(shift_out, n + 2 if u > 11 else n + 1)
                                    tail(b - 1, TAIL_PE[q, u])
                                    done += 1

                iterate(pe, body)
                values(B * QUADS - 1, QUADS - 1, 3)
                for j in range(N_TL):
                    tail(B - 1, j)


def setup(nc, c, g_x, g_f, wout, bout, w_red, wg):
    with ExitStack() as s:
        def sb(name, shape, dt):
            return s.enter_context(nc.sbuf_tensor(name, shape, dt))

        def sem(name):
            return s.enter_context(nc.semaphore(name))

        gates = sb("gates", [P, 2], F32)
        wg_s = sb("wg_s", [E, GD], F32)
        wsq = sb("wsq", [E, GD], F32)
        wn = sb("wn", [E, 1], F32)
        wn2 = sb("wn2", [E, 1], F32)
        wn3 = sb("wn3", [E, 1], F32)
        wgn = sb("wgn", [E, GD], F32)
        ints = sb("ints", [P, 64], I32)
        tg = sb("tg", [P, 2], F32)
        ps = s.enter_context(nc.psum_tensor("ps_setup", [P, 512], F32))
        load, wload, cleared, built, ints_set, tanh_done, step, norm_done, scaled, tr = (
            sem(n) for n in ("g_load", "w_load", "cleared", "built", "ints_set", "tanh_done", "step", "wg_norm", "scaled", "wg_tr"))
        with nc.Block() as block:
            @block.sync
            def _(sp):
                sp.dma_start(gates[:, 0:1], g_x.rearrange("(a n) -> a n", a=1).to_broadcast([P, 1])).then_inc(load, 16)
                sp.dma_start(gates[:, 1:2], g_f.rearrange("(a n) -> a n", a=1).to_broadcast([P, 1])).then_inc(load, 16)
                sp.dma_start(wg_s[:], wg).then_inc(load, 16)
                sp.dma_start(c["wred"][:], w_red.rearrange("(k p) n -> p k n", p=P)).then_inc(load, 16)
                sp.wait_ge(cleared, 1)
                for h in range(HQ):
                    sp.dma_start(c["wout"][32 * h:32 * h + DH, :, :],
                                 wout.rearrange("(q h d) n -> h d q n", q=QUADS, h=HQ)[h]).then_inc(wload, 16)
                sp.dma_start(c["wout"][DH:DH + 1, 0, :], bout.rearrange("(a n) -> a n", a=1)).then_inc(wload, 16)
                sp.wait_ge(wload, 16 * (HQ + 1))
                sp.wait_ge(load, 64)

            @block.gpsimd
            def _(pool):
                pool.memset(c["ident"][:], 0.0).then_inc(built, 1)
                pool.memset(c["identb"][:], 0.0).then_inc(built, 1)
                pool.memset(c["mask_q"][:], 0.0).then_inc(built, 1)
                pool.memset(c["mask_k"][:], 0.0).then_inc(built, 1)
                pool.memset(c["before"][:], 1.0).then_inc(built, 1)
                pool.memset(c["onesb"][:], 1.0)
                pool.memset(c["mhalf"][:], -0.5).then_inc(built, 1)
                pool.wait_ge(built, 6)
                for m in (c["ident"], c["identb"]):
                    pool.affine_select(out=m[:], in_=m[:], compare_op=ALU.not_equal, fill=1.0, base=0,
                                       pattern=[[-1, P]], channel_multiplier=1).then_inc(built, 1)
                pool.affine_select(out=c["mask_q"][:], in_=c["mask_q"][:], compare_op=ALU.is_ge, fill=MASKED, base=0,
                                   pattern=[[-1, P]], channel_multiplier=1)
                pool.affine_select(out=c["mask_k"][:], in_=c["mask_k"][:], compare_op=ALU.is_ge, fill=MASKED, base=0,
                                   pattern=[[1, P]], channel_multiplier=-1)
                pool.affine_select(out=c["before"][:], in_=c["before"][:], compare_op=ALU.is_gt, fill=0.0, base=0,
                                   pattern=[[1, P]], channel_multiplier=-1)
                pool.iota(ints[:, 0:NB * E], pattern=[[0, NB], [1, E]], base=0, channel_multiplier=0).then_inc(ints_set, 1)
                pool.iota(ints[:, 32:40], pattern=[[CAP, E]], base=0, channel_multiplier=0).then_inc(ints_set, 1)
                pool.iota(ints[:, 40:40 + NB], pattern=[[P, NB]], base=0, channel_multiplier=1).then_inc(ints_set, 1)
                pool.wait_ge(norm_done, 1)
                pool.tensor_tensor(wn2[:], wn[:], c["half"][0:E, 0:1], ALU.pow).then_inc(norm_done, 1)

            @block.vector
            def _(dve):
                dve.memset(c["half"][:], 0.5)
                dve.memset(c["wout"][:], 0.0).then_inc(cleared, 1)
                dve.wait_ge(ints_set, 3)
                dve.tensor_copy(c["eiota"][:].rearrange("p n e -> p (n e)"), ints[:, 0:NB * E])
                dve.tensor_copy(c["run"][:], ints[:, 32:40])
                dve.tensor_copy(c["base"][:], ints[:, 32:40])
                dve.tensor_copy(c["tokf"][:], ints[:, 40:40 + NB])
                dve.wait_ge(load, 64)
                dve.tensor_tensor(wsq[:], wg_s[:], wg_s[:], ALU.mult).then_inc(step, 1)
                dve.wait_ge(step, 1)
                dve.tensor_reduce(wn[:], wsq[:], AX.X, ALU.add).then_inc(norm_done, 1)
                dve.wait_ge(norm_done, 2)
                dve.tensor_scalar(wn3[:], wn2[:], 1e-4, None, ALU.max).then_inc(step, 1)
                dve.wait_ge(step, 2)
                dve.reciprocal(wn[:], wn3[:]).then_inc(step, 1)
                dve.wait_ge(step, 3)
                dve.tensor_scalar(wgn[:], wg_s[:], wn[:, 0:1], None, ALU.mult).then_inc(scaled, 1)
                dve.wait_ge(tanh_done, 1)
                dve.tensor_copy(c["tgf"][:], tg[:, 1:2])
                dve.wait_ge(wload, 16 * (HQ + 1))
                dve.tensor_scalar(c["wout"][:].rearrange("p q n -> p (q n)"), c["wout"][:].rearrange("p q n -> p (q n)"),
                                  tg[:, 0:1], None, ALU.mult)
                dve.wait_ge(tr, 1)
                dve.tensor_copy(c["wgT"][:], ps[0:GD, 0:E])

            @block.scalar
            def _(act):
                act.wait_ge(load, 64)
                act.activation(tg[:], gates[:], ACT.Tanh).then_inc(tanh_done, 1)

            @block.tensor
            def _(pe):
                pe.wait_ge(scaled, 1)
                pe.wait_ge(built, 8)
                pe.transpose(ps[0:GD, 0:E], wgn[:], c["ident"][0:E, 0:E]).then_inc(tr, 1)


def close_rows(nc, c, w1, b1, b2, rows_d):
    with ExitStack() as s:
        def sb(name, shape, dt):
            return s.enter_context(nc.sbuf_tensor(name, shape, dt))

        def sem(name):
            return s.enter_context(nc.semaphore(name))

        pad = sb("pad", [P, ROW], F32)
        padf = sb("padf", [P, E], F32)
        padi = [sb(f"padi{e}", [P, 1], U32) for e in range(E)]
        pi = sb("pi", [P, E], I32)
        pf = sb("pf", [P, E], F32)
        ti = sb("ti", [1, TILES], I32)
        tf = sb("tf", [1, TILES], F32)
        cf = sb("cf", [1, E], F32)
        ci = sb("ci", [1, E], I32)
        nt = sb("nt", [1, E], F32)
        ones = sb("ones8", [1, E], F32)
        end = sb("end", [1, E], F32)
        skip = sb("skip", [1, E], F32)
        ge = sb("ge", [1, TILES, E], F32)
        gs = sb("gsk", [1, TILES, E], F32)
        te = sb("te", [1, TILES], F32)
        tr = sb("tr", [1, TILES], F32)
        tr2 = sb("tr2", [1, TILES], F32)
        b1n = sb("b1n", [E * FC, P], F32)
        psB = s.enter_context(nc.psum_tensor("psB", [P, 512], F32))
        w1_in = [sem(f"w1_in_late{p}") for p in range(2)]
        w1_hi, bias_in, b1_tr = sem("w1_hi_late"), sem("bias_in"), sem("b1_tr")
        ints_set, step, pad_ready, pad_out, dummy_out = (sem(n) for n in ("ints2", "step2", "pad_ready", "pad_out", "dummy_out"))
        with nc.Block() as block:
            @block.gpsimd
            def _(pool):
                pool.iota(pi[:], pattern=[[0, E]], base=0, channel_multiplier=1).then_inc(ints_set, 1)
                pool.iota(ti[:], pattern=[[P, TILES]], base=0, channel_multiplier=0).then_inc(ints_set, 1)
                pool.wait_ge(pad_ready, 1)
                for e in range(E):
                    pool.indirect_dma_start(rows_d[:, :], bass.IndirectOffsetOnAxis(ap=padi[e][:, 0:1], axis=0),
                                            pad[:], None).then_inc(pad_out, 16)
                low_w1(pool, c, 2, w1_hi)
                pool.wait_ge(pad_out, 16 * E)

            @block.sync
            def _(sp):
                for w in range(2, 4):
                    load_w1(sp, c, w1, w, w1_in)
                sp.dma_start(b1n[:], b1.rearrange("e (c p) -> (e c) p", p=P)).then_inc(bias_in, 16)
                sp.dma_start(c["b2b"][:], b2.rearrange("(a e) d -> a (e d)", a=1).to_broadcast([P, E * D])).then_inc(bias_in, 16)
                sp.wait_ge(pad_ready, 1)
                sp.dma_start(rows_d[DUMMY:DUMMY + P, :], pad[:]).then_inc(dummy_out, 16)
                sp.wait_ge(dummy_out, 16)
                sp.wait_ge(bias_in, 32)

            @block.scalar
            def _(act):
                act.wait_ge(b1_tr, 1)
                act.activation(c["b1T"][:], psB[:, 0:E * FC], ACT.Copy)
                for w in range(2, 4):
                    high_w1(act, c, w, w1_in, w1_hi)

            @block.tensor
            def _(pe):
                pe.wait_ge(bias_in, 32)
                pe.transpose(psB[:, 0:E * FC], b1n[:], c["ident"][0:E * FC, 0:E * FC]).then_inc(b1_tr, 1)

            @block.vector
            def _(dve):
                k = Count(step)
                dve.memset(ones[:], 1.0)
                k.add(dve.memset(pad[:], 0.0))
                k.wait(dve)
                k.add(dve.memset(pad[:, D + 3:D + 4].bitcast(I32), NOTOK))
                dve.wait_ge(ints_set, 2)
                k.add(dve.tensor_copy(pf[:], pi[:]))
                k.add(dve.tensor_copy(tf[:], ti[:]))
                k.wait(dve)
                k.add(dve.tensor_tensor(padf[:], pf[:], c["run"][:], ALU.add))
                k.wait(dve)
                for e in range(E):
                    ins = dve.tensor_copy(padi[e][:], padf[:, e:e + 1])
                ins.then_inc(pad_ready, 1)
                k.add(dve.tensor_tensor(cf[:], c["run"][0:1, :], c["base"][0:1, :], ALU.subtract))
                k.wait(dve)
                k.add(dve.tensor_scalar(nt[:], cf[:], float(P - 1), None, ALU.add))
                k.wait(dve)
                k.add(dve.tensor_copy(ci[:], nt[:]))
                k.wait(dve)
                k.add(dve.tensor_scalar(ci[:], ci[:], 7, None, ALU.arith_shift_right))
                k.wait(dve)
                k.add(dve.tensor_copy(nt[:], ci[:]))
                k.wait(dve)
                k.add(dve.tensor_tensor_scan(end[:], ones[:], nt[:], 0.0, ALU.mult, ALU.add))
                k.add(dve.tensor_scalar(skip[:], nt[:], -float(P), float(CAP), ALU.mult, ALU.add))
                k.wait(dve)
                k.add(dve.tensor_scalar(end[:], end[:], float(P), None, ALU.mult))
                k.wait(dve)
                k.add(dve.tensor_tensor(ge[:], tf[:].unsqueeze(2).to_broadcast([1, TILES, E]),
                                        end[:].unsqueeze(1).to_broadcast([1, TILES, E]), ALU.is_ge))
                k.wait(dve)
                k.add(dve.tensor_reduce(te[:], ge[:], AX.X, ALU.add))
                k.add(dve.tensor_tensor(gs[:], ge[:], skip[:].unsqueeze(1).to_broadcast([1, TILES, E]), ALU.mult))
                k.wait(dve)
                k.add(dve.tensor_scalar(te[:], te[:], float(E - 1), None, ALU.min))
                k.add(dve.tensor_reduce(tr[:], gs[:], AX.X, ALU.add))
                k.wait(dve)
                k.add(dve.tensor_tensor(tr2[:], tr[:], tf[:], ALU.add))
                k.wait(dve)
                k.add(dve.tensor_scalar(tr2[:], tr2[:], float(DUMMY), None, ALU.min))
                k.wait(dve)
                dve.tensor_copy(c["tile_e"][:], te[:])
                dve.tensor_copy(c["tile_r"][:], tr2[:])
                low_w1(dve, c, 3, w1_hi)


def experts(nc, c, rows_d, out):
    out_d = out.rearrange("b t d -> (b t) d")
    U = 4
    with ExitStack() as s:
        def sb(name, shape, dt):
            return s.enter_context(nc.sbuf_tensor(name, shape, dt))

        def sem(name):
            return s.enter_context(nc.semaphore(name))

        W1, W2, b1T, b2b = c["W1"], c["W2"], c["b1T"], c["b2b"]
        row = [sb(f"frow{r}", [P, ROW], F32) for r in range(U)]
        res = [sb(f"res{r}", [P, D], F32) for r in range(U)]
        ids = [sb(f"ids{r}", [P, 1], U32) for r in range(U)]
        hn = [sb(f"fhn{p}", [P, D], F32) for p in range(2)]
        hh = [sb(f"hh{p}", [P, KC, 2, P], BF16) for p in range(2)]
        g = [sb(f"g{p}", [P, FC, P], F32) for p in range(2)]
        gh = [sb(f"gh{p}", [P, FC, P], BF16) for p in range(2)]
        gl = [sb(f"gl{p}", [P, FC, P], BF16) for p in range(2)]
        y = sb("y", [P, D], F32)
        psT = [s.enter_context(nc.psum_tensor(f"fT{p}", [P, 512], F32)) for p in range(2)]
        psH = [s.enter_context(nc.psum_tensor(f"fH{p}", [P, 4, P], F32)) for p in range(4)]
        psY = [s.enter_context(nc.psum_tensor(f"fY{p}", [P, 512], F32)) for p in range(2)]
        row_in, stored = ([sem(f"{n}{r}") for r in range(U)] for n in ("row_in", "stored"))
        (hn_done, tr_done, hi_out, lo_out, h_done, g_done, ghi_done, glo_done, y_done, y_sum, res_done, passed_pool) = (
            sem(n) for n in ("hn_done", "tr_done", "hi_out", "lo_out", "h_done", "g_done", "ghi_done", "glo_done",
                             "y_done", "y_sum", "res_done", "passed_pool3"))

        def tiles(eng, body):
            for r in range(U):
                body(0, r)
            with eng.Fori(1, TILES // U - 1) as i:
                for r in range(U):
                    body(i, r)
            for r in range(U):
                body(TILES // U - 1, r)

        def ahead(i, r, k):
            i, r = (i + 1, r + k - U) if r + k >= U else (i, r + k)
            return None if isinstance(i, int) and i >= TILES // U else (i, r)

        def expert_of(eng, t):
            return eng.value_load(c["tile_e"][0:1, bass.ds(t, 1)], min_val=0, max_val=E - 1)

        with nc.Block() as block:
            @block.sync
            def _(sp):
                def body(i, r):
                    t = U * i + r
                    wait(sp, res_done, t - U + 1)
                    first_row = sp.value_load(c["tile_r"][0:1, bass.ds(t, 1)], min_val=0, max_val=DUMMY)
                    sp.dma_start(row[r][:], rows_d[bass.ds(first_row, P), :]).then_inc(row_in[r], 16)

                tiles(sp, body)

            @block.gpsimd
            def _(pool):
                def body(i, r):
                    pool.wait_ge(res_done, U * i + r + 1)
                    pool.sem_inc(passed_pool, 1)
                    pool.indirect_dma_start(out_d, bass.IndirectOffsetOnAxis(ap=ids[r][:, 0:1], axis=0), res[r][:], None,
                                            bounds_check=TOK - 1, oob_is_err=False).then_inc(stored[r], 16)

                tiles(pool, body)
                for r in range(U):
                    pool.wait_ge(stored[r], 16 * (TILES // U))

            @block.scalar
            def _(act):
                def high(i, r):
                    act.wait_ge(tr_done, U * i + r + 1)
                    act.activation(hh[r % 2][:, :, 0, :], psT[r % 2][:, 0:D].rearrange("p (k n) -> p k n", k=KC),
                                   ACT.Copy).then_inc(hi_out, 1)

                def gelu(e, i, r, j):
                    act.wait_ge(h_done, 2 * (U * i + r) + j + 1)
                    for k in range(4):
                        f = 4 * j + k
                        ins = act.activation(g[r % 2][:, f, :], psH[2 * (r % 2) + j][:, k, :], ACT.Gelu,
                                             bias=b1T[:, bass.ds(e * FC + f, 1)])
                    ins.then_inc(g_done, 1)

                def body(i, r):
                    e = expert_of(act, U * i + r)
                    gelu(e, i, r, 0)
                    after = ahead(i, r, 1)
                    if after:
                        high(*after)
                    gelu(e, i, r, 1)

                high(0, 0)
                tiles(act, body)

            @block.vector
            def _(dve):
                def norm(i, r):
                    dve.wait_ge(row_in[r], 16 * (i + 1))
                    dve.tensor_scalar(hn[r % 2][:], row[r][:, 0:D], row[r][:, D:D + 1], row[r][:, D + 1:D + 2],
                                      ALU.mult, ALU.add).then_inc(hn_done, 1)

                def low(i, r):
                    dve.wait_ge(hi_out, U * i + r + 1)
                    dve.tensor_tensor(hh[r % 2][:, :, 1, :], psT[r % 2][:, 0:D].rearrange("p (k n) -> p k n", k=KC),
                                      hh[r % 2][:, :, 0, :], ALU.subtract).then_inc(lo_out, 1)

                def split_g(i, r, j):
                    half, p = slice(4 * j, 4 * j + 4), r % 2
                    n = 2 * (U * i + r) + j + 1
                    dve.wait_ge(g_done, n)
                    dve.tensor_copy(gh[p][:, half, :], g[p][:, half, :]).then_inc(ghi_done, 1)
                    dve.wait_ge(ghi_done, n)
                    dve.tensor_tensor(gl[p][:, half, :], g[p][:, half, :], gh[p][:, half, :], ALU.subtract).then_inc(glo_done, 1)

                def result(i, r):
                    t = U * i + r
                    e = expert_of(dve, t)
                    dve.wait_ge(y_done, t + 1)
                    wait(dve, res_done, t)
                    dve.tensor_tensor(y[:], psY[r % 2][:, 0:D], b2b[:, bass.ds(e * D, D)], ALU.add).then_inc(y_sum, 1)
                    dve.wait_ge(y_sum, t + 1)
                    wait(dve, stored[r], 16 * i)
                    dve.tensor_copy(ids[r][:], row[r][:, D + 3:D + 4].bitcast(U32))
                    dve.scalar_tensor_tensor(res[r][:], y[:], row[r][:, D + 2:D + 3], row[r][:, 0:D],
                                             ALU.mult, ALU.add).then_inc(res_done, 1)

                def body(i, r):
                    after = ahead(i, r, 1)
                    if after:
                        low(*after)
                    split_g(i, r, 0)
                    split_g(i, r, 1)
                    if r > 0:
                        result(i, r - 1)
                    elif not isinstance(i, int) or i > 0:
                        result(i - 1, U - 1)
                    after = ahead(i, r, 2)
                    if after:
                        norm(*after)

                norm(0, 0)
                norm(0, 1)
                low(0, 0)
                tiles(dve, body)
                result(TILES // U - 1, U - 1)

            @block.tensor
            def _(pe):
                def rows_T(i, r):
                    pe.wait_ge(hn_done, U * i + r + 1)
                    for k in range(KC):
                        ins = pe.transpose(psT[r % 2][:, k * P:(k + 1) * P], hn[r % 2][:, k * P:(k + 1) * P], c["ident"][:])
                    ins.then_inc(tr_done, 1)

                def hidden(e, r, j):
                    p = r % 2
                    for k in range(4):
                        f, n = 4 * j + k, 0
                        for kc in range(KC):
                            for a, b in ((0, 0), (0, 1), (1, 0)):
                                n += 1
                                ins = pe.matmul(psH[2 * p + j][:, k, :],
                                                W1[:, bass.ds(e * (KC * 2 * FF) + (kc * 2 + a) * FF + f * P, P)],
                                                hh[p][:, kc, b, :], start=n == 1, stop=n == 3 * KC)
                    ins.then_inc(h_done, 1)

                def model(i, r):
                    t, p = U * i + r, r % 2
                    e = expert_of(pe, t)
                    for f in range(FC):
                        if f % 4 == 0:
                            pe.wait_ge(glo_done, 2 * t + f // 4 + 1)
                        for m, (a, b) in enumerate(((0, 0), (0, 1), (1, 0))):
                            ins = pe.matmul(psY[p][:, 0:D], (gl if b else gh)[p][:, f, :],
                                            W2[:, bass.ds(e * (FC * 2 * D) + (f * 2 + a) * D, D)],
                                            start=f == 0 and m == 0, stop=f == FC - 1 and m == 2)
                    ins.then_inc(y_done, 1)

                def body(i, r):
                    e = expert_of(pe, U * i + r)
                    pe.wait_ge(lo_out, U * i + r + 1)
                    hidden(e, r, 0)
                    after = ahead(i, r, 1)
                    if after:
                        rows_T(*after)
                    hidden(e, r, 1)
                    if r > 0:
                        model(i, r - 1)
                    elif not isinstance(i, int) or i > 0:
                        model(i - 1, U - 1)

                rows_T(0, 0)
                tiles(pe, body)
                model(TILES // U - 1, U - 1)


def build(nc, x, ctx_1024, g_xattn, g_ffn, wq, wkv, wout, bout, w_red, wg, w1, b1, w2, b2, out):
    parts_d = nc.dram_tensor("qk_parts", (B, HALVES, 3, P, COLS), BF16, kind="Internal").ap()
    v_d = nc.dram_tensor("v_quads", (B, P, QUADS * KB * HQ * 32), F32, kind="Internal").ap()
    rows_d = nc.dram_tensor("sorted_rows", (DUMMY + P, ROW), F32, kind="Internal").ap()
    with ExitStack() as s:
        c = {}
        for name, shape, dt in (("ident", [P, P], F32), ("identb", [P, P], BF16), ("mask_q", [P, P], BF16),
                                ("mask_k", [P, P], BF16), ("before", [P, P], BF16), ("onesb", [P, P], BF16),
                                ("mhalf", [P, NB], F32), ("half", [P, 1], F32), ("eiota", [P, NB, E], F32),
                                ("run", [P, E], F32), ("base", [P, E], F32), ("tokf", [P, NB], F32),
                                ("wred", [P, KC, GD], F32), ("wout", [P, QUADS, D], F32), ("wgT", [GD, E], F32),
                                ("tgf", [P, 1], F32), ("b1T", [P, E * FC], F32), ("tile_e", [1, TILES], I32), ("tile_r", [1, TILES], I32)):
            c[name] = s.enter_context(nc.sbuf_tensor(name, shape, dt))
        c["W1"] = s.enter_context(nc.sbuf_tensor("W1", [P, E * KC * 2 * FF], BF16))
        setup(nc, c, g_xattn, g_ffn, wout, bout, w_red, wg)
        project(nc, c, x, ctx_1024, wq, wkv, parts_d, v_d)
        c["W2"] = s.enter_context(nc.sbuf_tensor("W2", [P, E * FC * 2 * D], BF16))
        for p in range(2):
            c[f"wide{p}"] = s.enter_context(nc.sbuf_tensor(f"wide{p}", [P, HQ * 1024], F32))
        attend(nc, c, x, w1, w2, parts_d, v_d, rows_d)
        c["b2b"] = s.enter_context(nc.sbuf_tensor("b2b", [P, E * D], F32))
        close_rows(nc, c, w1, b1, b2, rows_d)
        experts(nc, c, rows_d, out)


_INS = ['x', 'ctx_1024', 'g_xattn', 'g_ffn', 'L0_xattn_Wq', 'L0_xattn_Wkv', 'L0_xattn_Wout', 'L0_xattn_bout',
        'L0_ffn_w_red', 'L0_ffn_wg', 'L0_ffn_w1', 'L0_ffn_b1', 'L0_ffn_w2', 'L0_ffn_b2']


def kernel(**inputs):
    import numpy as _np
    import concourse.bacc as _bacc
    from concourse import mybir as _mybir
    from concourse.bass_utils import run_bass_kernel_spmd as _run

    nc = _bacc.Bacc("TRN2", target_bir_lowering=False, num_devices=1)
    arrays, args = {}, []
    for name in _INS:
        a = _np.ascontiguousarray(inputs[name])
        arrays[f"in_{name}_dram"] = a
        args.append(nc.dram_tensor(f"in_{name}_dram", a.shape, _mybir.dt.from_np(a.dtype), kind="ExternalInput").ap())
    out = nc.dram_tensor("out_0_dram", (B, T, D), _mybir.dt.float32, kind="ExternalOutput").ap()
    build(nc, *args, out)
    r = _run(nc, [arrays], core_ids=[0])
    return r.results[0]["out_0_dram"]
```

```python
from contextlib import ExitStack

import concourse.bass as bass
from concourse import mybir

F32 = mybir.dt.float32
BF16 = mybir.dt.bfloat16
I32 = mybir.dt.int32
U32 = mybir.dt.uint32
ALU = mybir.AluOpType
ACT = mybir.ActivationFunctionType
AX = mybir.AxisListType

P = 128
B, T, D = 8, 512, 256
TM = 512
KEYS = TM + T
HEADS, DH = 16, 16
QUADS = 4
HQ = HEADS // QUADS
SN = DH // QUADS
NB = T // P
KB = KEYS // P
KC = D // P
HALVES = 2
COLS = T + KEYS
EPS = 1e-5
SCALE = DH ** -0.5
Q_PART = (0, 0, 1, 1, 0, 2)
K_PART = (0, 1, 0, 1, 2, 0)
TERMS = len(Q_PART)
SROWS = TERMS * DH
MROWS = 2 * HQ
E, FF, GD = 8, 1024, 16
FC = FF // P
TOK = B * T
WIDE = KC * 2 * FF
assert WIDE == FC * 2 * D
CAP = TOK + P
DUMMY = E * CAP
ROW = D + 4
TILES = 40
NOTOK = 1 << 20
MASKED = -1e30


class Count:

    def __init__(self, sem, base=0):
        self.sem, self.base, self.n = sem, base, 0

    def add(self, ins, k=1):
        ins.then_inc(self.sem, k)
        self.n += k
        return ins

    def wait(self, eng):
        eng.wait_ge(self.sem, self.base + self.n)


def peel(count, body):
    for p in range(count):
        body(p)


def wait(eng, sem, value):
    if not isinstance(value, int) or value > 0:
        eng.wait_ge(sem, value)


class Arena:

    def __init__(self, s, nc, c):
        NQ, NK, NV = HQ * T, HQ * KEYS, KB * HQ * 32 * 2
        at = lambda q, lo, n: c["W1"][:, q * (NQ + NK + NV) + lo:q * (NQ + NK + NV) + lo + n]
        self.qs = [at(q, 0, NQ).rearrange("p (h n) -> p h n", h=HQ) for q in range(QUADS)]
        self.ks = [at(q, NQ, NK).rearrange("p (h n) -> p h n", h=HQ) for q in range(QUADS)]
        self.vq = [at(q, NQ + NK, NV).bitcast(F32).rearrange("p (k h d) -> p k h d", k=KB, h=HQ) for q in range(QUADS)]
        self.stk_in = [s.enter_context(nc.semaphore(f"stk_in{q}")) for q in range(QUADS)]
        self.v_in = [s.enter_context(nc.semaphore(f"v_in{q}")) for q in range(QUADS)]


def load_stack(sp, ar, parts_d, b, q):
    hf, o = divmod(q * HQ * DH, P)
    for t in range(TERMS):
        for dst, part, lo, hi in ((ar.qs[q], Q_PART[t], 0, T), (ar.ks[q], K_PART[t], T, COLS)):
            sp.dma_start(dst[DH * t:DH * (t + 1), :, :],
                         parts_d[bass.ds(b, 1), hf, part, o:o + HQ * DH, lo:hi]
                         .rearrange("a (h d) n -> d (a h) n", h=HQ)).then_inc(ar.stk_in[q], 16)


def load_v(sp, ar, v_d, b, q):
    sp.dma_start(ar.vq[q].rearrange("p k h d -> p (k h d)"),
                 v_d[bass.ds(b, 1), :, q * 1024:(q + 1) * 1024].rearrange("a p n -> p (a n)")).then_inc(ar.v_in[q], 16)


def project(nc, c, ar, x, ctx, wq, wkv, parts_d, v_d):
    with ExitStack() as s:
        def sb(name, shape, dt):
            return s.enter_context(nc.sbuf_tensor(name, shape, dt))

        def sem(name):
            return s.enter_context(nc.semaphore(name))

        wq_s = sb("wq_s", [P, KC, D], F32)
        wkv_s = sb("wkv_s", [P, KC, 2 * D], F32)
        xc = [sb(f"xc{p}", [P, KB, D], F32) for p in range(2)]
        st = sb("st1", [P, NB, 6], F32)
        mv = sb("mv1", [P, NB, 2], F32)
        ve = sb("ve1", [P, NB], F32)
        rs = sb("rs1", [P, NB], F32)
        xcT = sb("xcT", [P, KC, KEYS], F32)
        part = [sb(f"part{p}", [P, 3, COLS], BF16) for p in range(HALVES)]
        rest = [sb(f"rest{p}", [P, T], F32) for p in range(2)]
        vs = sb("vs", [P, QUADS, KB, HQ, 32], F32)
        psT = [s.enter_context(nc.psum_tensor(f"psT{p}", [P, 512], F32)) for p in range(2)]
        psQ = [s.enter_context(nc.psum_tensor(f"psQ{p}", [P, 512], F32)) for p in range(3)]
        psV = [s.enter_context(nc.psum_tensor(f"psV{p}", [P, 2, D], F32)) for p in range(2)]

        w_in = sem("w_in")
        x_in = [sem(f"x_in{p}") for p in range(2)]
        stat_done, mean_done, var_done, rstd_done, norm_done = (
            sem(n) for n in ("stat_done", "mean_done", "var_done", "rstd_done", "norm_done"))
        tr_done, tr_out = sem("tr_done"), sem("tr_out")
        qk_done, first_out, rest_out, second_out, third_out = (
            sem(n) for n in ("qk_done", "first_out", "rest_out", "second_out", "third_out"))
        v_done, v_out = sem("v_done"), sem("v_out")
        ones_set = sem("ones_set")
        passed_pool, passed_dve = sem("passed_pool1"), sem("passed_dve1")
        part_st = [sem(f"part_st{h}") for h in range(HALVES)]
        v_st = sem("v_st")
        UN = 3 * HALVES

        def batches(eng, body):
            for p in range(2):
                body(0, p, False)
            with eng.Fori(1, B // 2 - 1) as i:
                for p in range(2):
                    body(i, p, False)
            for p in range(2):
                body(B // 2 - 1, p, p == 1)

        with nc.Block() as block:
            @block.sync
            def _(sp):
                def load(b, p):
                    sp.dma_start(xc[p][:, 0:NB, :], ctx[bass.ds(b, 1)].rearrange("a (n p) d -> p (a n) d", p=P)).then_inc(x_in[p], 16)
                    sp.dma_start(xc[p][:, NB:KB, :], x[bass.ds(b, 1)].rearrange("a (n p) d -> p (a n) d", p=P)).then_inc(x_in[p], 16)

                load(0, 0)
                sp.dma_start(wq_s[:], wq.rearrange("(c p) n -> p c n", p=P)).then_inc(w_in, 16)
                sp.dma_start(wkv_s[:], wkv.rearrange("(c p) n -> p c n", p=P)).then_inc(w_in, 16)
                load(1, 1)

                def store(b):
                    for hf in range(HALVES):
                        wait(sp, third_out, UN * b + 3 * (hf + 1))
                        sp.wait_ge(first_out, UN * b + 3 * (hf + 1))
                        sp.dma_start(parts_d[bass.ds(b, 1), hf].rearrange("a c p n -> p (a c) n"), part[hf][:]).then_inc(part_st[hf], 16)
                    wait(sp, v_out, 4 * b + 4)
                    sp.dma_start(v_d[bass.ds(b, 1)].rearrange("a p n -> p (a n)"),
                                 vs[:].rearrange("p a b c d -> p (a b c d)")).then_inc(v_st, 16)

                with sp.Fori(0, B // 2 - 1) as i:
                    for p in range(2):
                        b = 2 * i + p
                        sp.wait_ge(tr_done, 4 * b + 4)
                        load(b + 2, p)
                        store(b)
                for hf in range(HALVES):
                    sp.wait_ge(part_st[hf], 16)
                sp.wait_ge(v_st, 16)
                for q in range(3):
                    load_stack(sp, ar, parts_d, 0, q)
                    load_v(sp, ar, v_d, 0, q)
                for p in range(2):
                    store(B - 2 + p)
                for hf in range(HALVES):
                    wait(sp, part_st[hf], 16 * B)
                wait(sp, v_st, 16 * B)

            @block.gpsimd
            def _(pool):
                pool.memset(vs[:], 0.0).then_inc(ones_set, 1)
                pool.wait_ge(ones_set, 1)
                for q in range(QUADS):
                    pool.memset(vs[:, q, :, :, DH + SN * q:DH + SN * (q + 1)], 1.0).then_inc(ones_set, 1)
                    pool.wait_ge(ones_set, q + 2)

                def rstd(b):
                    pool.wait_ge(mean_done, b + 1)
                    pool.sem_inc(passed_pool, 1)
                    pool.tensor_scalar(ve[:], mv[:, :, 1], EPS, None, ALU.add).then_inc(var_done, 1)
                    pool.wait_ge(var_done, b + 1)
                    pool.tensor_tensor(rs[:], ve[:], c["mhalf"][:, 0:NB], ALU.pow).then_inc(rstd_done, 1)

                def body(b, last):
                    for u in range(UN):
                        hf, k = divmod(u, 3)
                        pool.wait_ge(second_out, UN * b + u + 1)
                        pool.tensor_tensor(part[hf][:, 2, k * 512:(k + 1) * 512], rest[u % 2][:],
                                           part[hf][:, 1, k * 512:(k + 1) * 512], ALU.subtract).then_inc(third_out, 1)
                        if u == 1 and not last:
                            rstd(b + 1)

                rstd(0)
                batches(pool, lambda i, p, last: body(2 * i + p, last))

            @block.vector
            def _(dve):
                def moments(i, p):
                    b = 2 * i + p
                    dve.wait_ge(x_in[p], 32 * i + 32)
                    for n in range(NB):
                        dve.bn_stats(st[:, n, :], xc[p][:, NB + n, :]).then_inc(stat_done, 1)
                    dve.wait_ge(stat_done, NB * b + NB)
                    dve.sem_inc(passed_dve, 1)
                    for n in range(NB):
                        ins = dve.bn_aggr(mv[:, n, :], st[:, n, :])
                    ins.then_inc(mean_done, 1)

                def normalise(i, p):
                    b = 2 * i + p
                    X = xc[p][:, NB:KB, :]
                    dve.wait_ge(mean_done, b + 1)
                    dve.wait_ge(rstd_done, b + 1)
                    for n in range(NB):
                        ins = dve.tensor_scalar(X[:, n, :], X[:, n, :], mv[:, n, 0:1], rs[:, n:n + 1], ALU.subtract, ALU.mult)
                    ins.then_inc(norm_done, 1)

                def body(i, p, last):
                    b = 2 * i + p
                    after = (i + p, 1 - p)
                    for u in range(UN):
                        hf, k = divmod(u, 3)
                        dve.wait_ge(first_out, UN * b + u + 1)
                        wait(dve, third_out, UN * b + u - 1)
                        dve.scalar_tensor_tensor(rest[u % 2][:], psQ[u % 3][:], SCALE if k == 0 else 1.0,
                                                 part[hf][:, 0, k * 512:(k + 1) * 512], ALU.mult, ALU.subtract).then_inc(rest_out, 1)
                        if u == 0 and not last:
                            moments(*after)
                        if u == 4 and not last:
                            normalise(*after)

                def select(q):
                    dve.tensor_copy(ar.ks[q][SROWS:SROWS + MROWS], c["sel"][SROWS:SROWS + MROWS, :].unsqueeze(2).to_broadcast([MROWS, HQ, KEYS]))

                select(0)
                select(1)
                moments(0, 0)
                normalise(0, 0)
                select(2)
                select(3)
                batches(dve, body)

            @block.scalar
            def _(act):
                def second(b, u):
                    hf, k = divmod(u, 3)
                    act.wait_ge(rest_out, UN * b + u + 1)
                    act.activation(part[hf][:, 1, k * 512:(k + 1) * 512], rest[u % 2][:], ACT.Copy).then_inc(second_out, 1)

                def body(i, p):
                    b = 2 * i + p
                    for t in range(4):
                        act.wait_ge(tr_done, 4 * b + t + 1)
                        half, k = t // 2, t % 2
                        act.activation(xcT[:, k, half * 512:(half + 1) * 512], psT[t % 2][:], ACT.Copy).then_inc(tr_out, 1)
                    for u in range(UN):
                        hf, k = divmod(u, 3)
                        act.wait_ge(qk_done, UN * b + u + 1)
                        if k == 0:
                            wait(act, part_st[hf], 16 * b)
                        act.activation(part[hf][:, 0, k * 512:(k + 1) * 512], psQ[u % 3][:], ACT.Copy,
                                       scale=SCALE if k == 0 else 1.0).then_inc(first_out, 1)
                        if u > 0:
                            second(b, u - 1)
                    second(b, UN - 1)
                    wait(act, v_st, 16 * b)
                    for t in range(4):
                        act.wait_ge(v_done, 4 * b + t + 1)
                        for n in range(2):
                            ins = act.activation(vs[:, :, 2 * t + n, :, 0:DH],
                                                 psV[t % 2][:, n, :].rearrange("p (q h d) -> p q h d", q=QUADS, h=HQ), ACT.Copy)
                        ins.then_inc(v_out, 1)
                act.wait_ge(ones_set, 1 + QUADS)
                peel(2, lambda p: body(0, p))
                with act.Fori(1, B // 2) as i:
                    for p in range(2):
                        body(i, p)

            @block.tensor
            def _(pe):
                def body(i, p):
                    b = 2 * i + p
                    for t in range(4):
                        half, k = t // 2, t % 2
                        if t == 0:
                            pe.wait_ge(x_in[p], 32 * i + 32)
                        if t == 2:
                            pe.wait_ge(norm_done, b + 1)
                        wait(pe, tr_out, 4 * b + max(t - 1, 0))
                        for n in range(NB):
                            ins = pe.transpose(psT[t % 2][:, n * P:(n + 1) * P],
                                               xc[p][:, NB * half + n, k * P:(k + 1) * P], c["ident"][:])
                        ins.then_inc(tr_done, 1)
                    if isinstance(b, int) and b == 0:
                        pe.wait_ge(w_in, 32)
                    wait(pe, tr_out, 4 * b + 4)
                    for u in range(UN):
                        hf, k = divmod(u, 3)
                        wait(pe, rest_out, UN * b + max(u - 2, 0))
                        for kc in range(KC):
                            w = wq_s[:, kc, hf * P:(hf + 1) * P] if k == 0 else wkv_s[:, kc, hf * P:(hf + 1) * P]
                            cols = slice(TM, KEYS) if k == 0 else slice((k - 1) * 512, k * 512)
                            ins = pe.matmul(psQ[u % 3][:], w, xcT[:, kc, cols], start=kc == 0, stop=kc == KC - 1)
                        ins.then_inc(qk_done, 1)
                    for t in range(4):
                        wait(pe, v_out, 4 * b + max(t - 1, 0))
                        for n in range(2):
                            for kc in range(KC):
                                ins = pe.matmul(psV[t % 2][:, n, :], xcT[:, kc, (2 * t + n) * P:(2 * t + n + 1) * P],
                                                wkv_s[:, kc, D:2 * D], start=kc == 0, stop=kc == KC - 1)
                        ins.then_inc(v_done, 1)

                peel(2, lambda p: body(0, p))
                with pe.Fori(1, B // 2) as i:
                    for p in range(2):
                        body(i, p)


def w1_views(c, w):
    n = 2 * KC * 2 * FF
    v = c["W1"][:, w * n:(w + 1) * n].rearrange("p (k a n) -> p k a n", a=2, n=FF)
    return v[:, :, 0, :], v[:, :, 1, :], c[f"wide{w % 2}"][:].rearrange("p (k n) -> p k n", n=FF)


def load_w1(sp, c, w1, w, w1_in):
    sp.dma_start(w1_views(c, w)[2], w1[2 * w:2 * w + 2].rearrange("e (k p) n -> p (e k) n", p=P)).then_inc(w1_in[w % 2], 16)


def high_w1(act, c, w, w1_in, w1_hi):
    hi, lo, t = w1_views(c, w)
    act.wait_ge(w1_in[w % 2], 16 * (w // 2) + 16)
    act.activation(hi, t, ACT.Copy).then_inc(w1_hi, 1)


def low_w1(eng, c, w, w1_hi):
    hi, lo, t = w1_views(c, w)
    eng.wait_ge(w1_hi, w + 1)
    return eng.tensor_tensor(lo, t, hi, ALU.subtract)


def attend(nc, c, ar, x, w1, b1, w2, parts_d, v_d, rows_d):
    N_M = 3
    N_T = 17
    PRO = 12 * HQ
    N_TL = 7
    with ExitStack() as s:
        def sb(name, shape, dt):
            return s.enter_context(nc.sbuf_tensor(name, shape, dt))

        def sem(name):
            return s.enter_context(nc.semaphore(name))

        qs, ks, vq, stk_in, v_in = ar.qs, ar.ks, ar.vq, ar.stk_in, ar.v_in
        pr = [c[f"wide{p}"][:].rearrange("p (h n) -> p h n", h=HQ) for p in range(2)]
        stage = [sb(f"stage{p}", [P, FC * D // 2], F32) for p in range(2)]
        mx = sb("mx", [P, NB, HQ, 2], F32)
        nm = sb("nm", [P, NB, HQ], F32)
        mp = sb("mp", [P, NB, 2, HQ], BF16)
        mT = [sb(f"mT{p}", [MROWS, T], BF16) for p in range(2)]
        osb = sb("osb", [P, T], F32)
        lsum = sb("lsum", [P, T], F32)
        ot = [sb(f"ot{q}", [P, T], F32) for q in range(QUADS)]
        xres = sb("xres", [P, NB, D], F32)
        row = sb("row", [P, NB, ROW], F32)
        st = sb("st2", [P, NB, 6], F32)
        mv = sb("mv2", [P, NB, 2], F32)
        ve = sb("ve2", [P, NB], F32)
        rs = sb("rs2", [P, NB], F32)
        hT = sb("hT", [P, KC, T], F32)
        redT = sb("redT", [GD, T], F32)
        lg = sb("lg", [P, NB, E], F32)
        lmax = sb("lmax", [P, NB], F32)
        dif = sb("dif", [P, NB, E], F32)
        ex = sb("ex", [P, NB, E], F32)
        esum = sb("esum", [P, NB], F32)
        einv = sb("einv", [P, NB], F32)
        eq = sb("eq", [P, NB, E], F32)
        cand = sb("cand", [P, NB, E], F32)
        cmin = sb("cmin", [P, NB], F32)
        oh = sb("oh", [P, NB, E], BF16)
        cumr = sb("cumr", [P, NB, E], F32)
        pick = sb("pick", [P, NB, E], F32)
        slot = sb("slot", [P, NB], F32)
        slots = [sb(f"slots{n}", [P, 1], U32) for n in range(NB)]
        pad = sb("pad", [P, ROW], F32)
        padi = sb("padi", [1, E], I32)
        cf = sb("cf", [1, E], F32)
        ci = sb("ci", [1, E], I32)
        nt = sb("nt", [1, E], F32)
        ones = sb("ones8", [1, E], F32)
        end = sb("end", [1, E], F32)
        skip = sb("skip", [1, E], F32)
        ge, gs = (a[0:1, 0:TILES * E].rearrange("p (t e) -> p t e", e=E) for a in (lsum, osb))
        b1n = osb[0:E * FC, 0:P]
        te = sb("te", [1, TILES], F32)
        tr = sb("tr", [1, TILES], F32)
        tr2 = sb("tr2", [1, TILES], F32)

        psS = [s.enter_context(nc.psum_tensor(f"psS{p}", [P, 1024], F32)) for p in range(2)]
        psA = [s.enter_context(nc.psum_tensor(f"psA{p}", [P, 512], F32)) for p in range(2)]
        psO = s.enter_context(nc.psum_tensor("psO", [P, 512], F32))
        psM = s.enter_context(nc.psum_tensor("psM", [P, 512], F32))

        w2_in, w1_in = ([sem(f"{n}{p}") for p in range(2)] for n in ("w2_in", "w1_in"))
        w2_hi, w2_lo, w1_hi = sem("w2_hi"), sem("w2_lo"), sem("w1_hi")
        w1_lo = [sem(f"w1_lo{p}") for p in range(2)]
        bias_in, b1_tr, b1_out = sem("bias_in"), sem("b1_tr"), sem("b1_out")
        step, pad_set, pad_ready, pad_out, dummy_out = (sem(n) for n in ("step2", "pad_set", "pad_ready", "pad_out", "dummy_out"))
        s_done, exp_done, pv_done = sem("s_done"), sem("exp_done"), sem("pv_done")
        a_done, max_done = sem("a_done"), sem("max_done")
        shift_made, shift_tr, shift_out, shift_in = (sem(n) for n in ("shift_made", "shift_tr", "shift_out", "shift_in"))
        o_out, l_out, l_inv, r_out, ot_done = (sem(n) for n in ("o_out", "l_out", "l_inv", "r_out", "ot_done"))
        raw = [osb] + ot[1:]
        x_in = sem("xres_in")
        tl_done, tl_out = sem("tl_done"), sem("tl_out")
        chain = sem("chain")
        ve_done, rstd_done = sem("ve_done"), sem("rstd2_done")
        ex_done, hn_done = sem("ex_done"), sem("hn2_done")
        idx_ready, row_out = sem("idx_ready"), sem("row_out")
        passed_pool, passed_dve = sem("passed_pool2"), sem("passed_dve2")
        C_MEAN, C_SCAL, C_DIF, C_OH = 4, 5, 7, 11

        def spans(g):
            if g < 2:
                return [(2 * g, 0, 0), (2 * g + 1, 0, 512)]
            if g == 2:
                return [(NB, 0, 0), (NB + 1, P, 512)]
            return [(NB + 2, 2 * P, 0), (NB + 3, 3 * P, 2 * P)]

        def width(g):
            kb, q0, at = spans(g)[1]
            return at + T - q0

        def max_bank(w, unit):
            if isinstance(w, int) and w < PRO:
                return (psA + psS)[w % 4]
            return psA[unit % 2]

        def row_units(quad_h):
            for i in range(NB):
                yield i, 0, TM
                yield i, TM, (i + 1) * P

        def ahead(q, u, last):
            k = 2 * u
            d = 1 if k < 16 else 2
            if last and q + d >= QUADS:
                return None
            return d, (2 + k // 8) % HQ, k % 8

        def iterate(eng, body):
            body(0, True, False)
            with eng.Fori(1, B - 1) as b:
                body(b, False, False)
            body(B - 1, False, True)

        with nc.Block() as block:
            @block.sync
            def _(sp):
                def load_x(b):
                    sp.dma_start(xres[:], x[bass.ds(b, 1)].rearrange("a (n p) d -> p (a n) d", p=P)).then_inc(x_in, 16)

                def send_shift(n, q):
                    sp.wait_ge(shift_out, n + 1)
                    src = mT[q % 2]
                    sp.dma_start(qs[q][SROWS:SROWS + MROWS, :, :],
                                 src[:].unsqueeze(1).to_broadcast([MROWS, HQ, T])).then_inc(shift_in, 16)

                sp.dma_start(b1n, b1.rearrange("e (c p) -> (e c) p", p=P)).then_inc(bias_in, 16)
                send_shift(0, 0)
                sp.wait_ge(pad_set, 2)
                sp.dma_start(rows_d[DUMMY:DUMMY + P, :], pad[:]).then_inc(dummy_out, 16)

                def body(b, first, last):
                    for q in range(QUADS):
                        n = b * QUADS + q
                        bn, qn = (b, q + 3) if q == 0 else (b + 1, q - 1)
                        if q == 0 or not last:
                            wait(sp, s_done, 16 * n)
                            load_stack(sp, ar, parts_d, bn, qn)
                            wait(sp, pv_done, 4 * n)
                            load_v(sp, ar, v_d, bn, qn)
                        if q == 2:
                            if not first:
                                sp.wait_ge(tl_out, N_TL * (b - 1) + 4)
                            load_x(b)
                        if q < 2:
                            wait(sp, w2_lo, 2 * b + q - 1)
                            sp.dma_start(stage[q][:].rearrange("p (k n) -> p k n", n=D),
                                         w2[bass.ds(b, 1), q * FF // 2:(q + 1) * FF // 2, :]
                                         .rearrange("a (k p) n -> p (a k) n", p=P)).then_inc(w2_in[q], 16)
                        if not (last and q == QUADS - 1):
                            send_shift(n + 1, (q + 1) % QUADS)

                iterate(sp, body)
                sp.wait_ge(pv_done, 4 * B * QUADS)
                sp.wait_ge(row_out, 16 * NB * (B - 1))
                for w in range(4):
                    if w >= 2:
                        sp.wait_ge(w1_lo[w - 2], 1)
                    load_w1(sp, c, w1, w, w1_in)
                sp.wait_ge(pad_ready, 1)
                for e in range(E):
                    behind = sp.value_load(padi[0:1, e:e + 1], min_val=0, max_val=DUMMY - P)
                    sp.dma_start(rows_d[bass.ds(behind, P), :], pad[:]).then_inc(pad_out, 16)
                sp.wait_ge(pad_out, 16 * E)
                sp.wait_ge(dummy_out, 16)
                
            @block.gpsimd
            def _(pool):
                def rstd(tb):
                    pool.wait_ge(chain, N_T * tb + C_MEAN)
                    pool.sem_inc(passed_pool, 1)
                    pool.tensor_scalar(ve[:], mv[:, :, 1], EPS, None, ALU.add).then_inc(ve_done, 1)
                    pool.wait_ge(ve_done, tb + 1)
                    pool.tensor_tensor(rs[:], ve[:], c["mhalf"][:, 0:NB], ALU.pow).then_inc(rstd_done, 1)

                def gather(b, q):
                    pool.wait_ge(o_out, QUADS * b + q + 1)
                    if q > 1:
                        pool.wait_ge(l_out, (QUADS - 1) * b + q - 1)
                    pool.tensor_tensor(lsum[:], osb[:] if q == 1 else lsum[:], raw[q][:], ALU.add).then_inc(l_out, 1)

                def divide(tb):
                    for q in range(QUADS):
                        pool.wait_ge(r_out, QUADS * tb + q + 1)
                        pool.tensor_tensor(ot[q][:], raw[q][:], hT[:, q % 2, :], ALU.mult).then_inc(ot_done, 1)

                def scatter(tb):
                    pool.wait_ge(idx_ready, tb + 1)
                    pool.sem_inc(passed_pool, 1)
                    for n in range(NB):
                        pool.indirect_dma_start(rows_d[:, :], bass.IndirectOffsetOnAxis(ap=slots[n][:, 0:1], axis=0),
                                                row[:, n, :], None).then_inc(row_out, 16)

                def body(b, first, last):
                    for q in range(QUADS):
                        n = b * QUADS + q
                        if q >= 2:
                            gather(b, q - 1)
                        if q == 0 and not first:
                            gather(b - 1, QUADS - 1)
                            divide(b - 1)
                        if q == 1 and not first:
                            rstd(b - 1)
                        if q in (1, 3):
                            k = q // 2
                            v = c["W2"][:, bass.ds(b * (FC * 2 * D) + k * FC * D, FC * D)].rearrange("p (k a n) -> p k a n", a=2, n=D)
                            t = stage[k][:].rearrange("p (k n) -> p k n", n=D)
                            pool.wait_ge(w2_in[k], 16 * (b + 1))
                            pool.sem_inc(passed_pool, 1)
                            pool.tensor_copy(v[:, :, 0, :], t).then_inc(w2_hi, 1)
                            pool.wait_ge(w2_hi, 2 * b + k + 1)
                            pool.sem_inc(passed_pool, 1)
                            pool.tensor_tensor(v[:, :, 1, :], t, v[:, :, 0, :], ALU.subtract).then_inc(w2_lo, 1)
                        if not first:
                            if q == 3:
                                scatter(b - 1)
                                pool.wait_ge(row_out, 16 * NB * b)

                iterate(pool, body)
                gather(B - 1, QUADS - 1)
                divide(B - 1)
                low_w1(pool, c, 1, w1_hi).then_inc(w1_lo[1], 1)
                rstd(B - 1)
                scatter(B - 1)
                pool.wait_ge(row_out, 16 * NB * B)

            @block.vector
            def _(dve):
                def maxima(w, h, unit):
                    i, lo, nk = list(row_units(h))[unit]
                    dve.wait_ge(a_done, w + 1)
                    dve.tensor_reduce(mx[:, i, h, unit % 2:unit % 2 + 1], max_bank(w, unit)[:, 0:nk], AX.X, ALU.max).then_inc(max_done, 1)

                def shift(n):
                    dve.wait_ge(max_done, 32 * (n + 1))
                    dve.tensor_reduce(nm[:], mx[:], AX.X, ALU.max, negate=True).then_inc(shift_made, 1)
                    dve.wait_ge(shift_made, N_M * n + 1)
                    wait(dve, shift_tr, n)
                    dve.tensor_copy(mp[:, :, 0, :], nm[:]).then_inc(shift_made, 1)
                    dve.wait_ge(shift_made, N_M * n + 2)
                    dve.tensor_tensor(mp[:, :, 1, :], nm[:], mp[:, :, 0, :], ALU.subtract).then_inc(shift_made, 1)

                def sums(tb, part):
                    if part < 4:
                        dve.wait_ge(l_out, (QUADS - 1) * (tb + 1))
                        piece = lsum[:, part * P:(part + 1) * P]
                        ins = dve.reciprocal(piece, piece)
                        if part == 3:
                            ins.then_inc(l_inv, 1)
                    else:
                        q = part - 4
                        dve.wait_ge(l_inv, tb + 1)
                        if q >= 2:
                            dve.wait_ge(ot_done, QUADS * tb + q - 1)
                        dve.sem_inc(passed_dve, 1)
                        dve.stream_shuffle(hT[:, q % 2, :], lsum[:],
                                           [DH + SN * q + k % SN for k in range(32)]).then_inc(r_out, 1)

                dve.memset(ones[:], 1.0)
                dve.memset(pad[:], 0.0).then_inc(pad_set, 1)
                dve.wait_ge(pad_set, 1)
                dve.memset(pad[:, D + 3:D + 4].bitcast(I32), NOTOK).then_inc(pad_set, 1)

                for w in range(PRO):
                    maxima(w, w // 8 % HQ, w % 8)
                    if w == 31:
                        shift(0)

                def tail(tb):
                    k = Count(chain, N_T * tb)
                    bc = lambda a: a.unsqueeze(2).to_broadcast([P, NB, E])
                    bank = lambda: psM[:, 0:NB * E].rearrange("p (n e) -> p n e", e=E)

                    def x1(r):
                        if r == 0:
                            dve.wait_ge(x_in, 16 * tb + 16)
                        dve.wait_ge(tl_done, N_TL * tb + r + 1)
                        dve.tensor_tensor(row[:, 2 * r:2 * r + 2, 0:D], psM[:].rearrange("p (n d) -> p n d", d=D),
                                          xres[:, 2 * r:2 * r + 2, :], ALU.add).then_inc(tl_out, 1)

                    def token():
                        dve.wait_ge(tl_out, N_TL * tb + 2)
                        k.add(dve.tensor_copy(row[:, :, D + 3:D + 4].bitcast(I32), c["tokf"][:].unsqueeze(2)))
                        k.wait(dve)
                        k.add(dve.tensor_scalar(c["tokf"][:], c["tokf"][:], float(T), None, ALU.add))

                    def stats(n):
                        ins = dve.bn_stats(st[:, n, :], row[:, n, 0:D])
                        if n == NB - 1:
                            k.add(ins)

                    def mean():
                        k.wait(dve)
                        dve.sem_inc(passed_dve, 1)
                        for n in range(NB):
                            ins = dve.bn_aggr(mv[:, n, :], st[:, n, :])
                        k.add(ins)
                        assert k.n == C_MEAN

                    def scalars():
                        dve.wait_ge(rstd_done, tb + 1)
                        k.wait(dve)
                        dve.tensor_copy(row[:, :, D:D + 1], rs[:].unsqueeze(2))
                        k.add(dve.scalar_tensor_tensor(row[:, :, D + 1:D + 2], mv[:, :, 0:1], -1.0, rs[:].unsqueeze(2), ALU.mult, ALU.mult))
                        assert k.n == C_SCAL

                    def logits():
                        dve.wait_ge(tl_done, N_TL * tb + 6)
                        dve.tensor_copy(lg[:], bank()).then_inc(tl_out, 1)
                        dve.wait_ge(tl_out, N_TL * tb + 6)
                        k.add(dve.tensor_reduce(lmax[:], lg[:], AX.X, ALU.max))

                    def differ():
                        k.wait(dve)
                        k.add(dve.tensor_tensor(dif[:], lg[:], bc(lmax[:]), ALU.subtract))
                        assert k.n == C_DIF
                        k.add(dve.tensor_tensor(eq[:], lg[:], bc(lmax[:]), ALU.is_equal))

                    def candidates():
                        k.wait(dve)
                        k.add(dve.scalar_tensor_tensor(cand[:], eq[:], -float(E), c["eiota"][:], ALU.mult, ALU.add))

                    def least():
                        k.wait(dve)
                        k.add(dve.tensor_reduce(cmin[:], cand[:], AX.X, ALU.min))

                    def one_hot():
                        k.wait(dve)
                        k.add(dve.tensor_tensor(oh[:], cand[:], bc(cmin[:]), ALU.is_equal))
                        assert k.n == C_OH

                    def total():
                        dve.wait_ge(ex_done, tb + 1)
                        k.add(dve.tensor_reduce(esum[:], ex[:], AX.X, ALU.add))

                    def inverse():
                        k.wait(dve)
                        k.add(dve.reciprocal(einv[:], esum[:]))

                    def score():
                        k.wait(dve)
                        k.add(dve.tensor_scalar(row[:, :, D + 2:D + 3], einv[:].unsqueeze(2), c["tgf"][:, 0:1], None, ALU.mult))

                    def ranks():
                        dve.wait_ge(tl_done, N_TL * tb + 7)
                        run = c["run"]
                        k.add(dve.tensor_tensor(cumr[:], bank(), run[:].unsqueeze(1).to_broadcast([P, NB, E]), ALU.add))
                        k.wait(dve)
                        dve.tensor_tensor(run[:], run[:], psM[:, NB * E:NB * E + E], ALU.add).then_inc(tl_out, 1)
                        k.add(dve.tensor_tensor(pick[:], cumr[:], oh[:], ALU.mult))

                    def slot_sum():
                        k.wait(dve)
                        k.add(dve.tensor_reduce(slot[:], pick[:], AX.X, ALU.add))

                    def slot_ints():
                        k.wait(dve)
                        for n in range(NB):
                            ins = dve.tensor_copy(slots[n][:], slot[:, n:n + 1])
                        ins.then_inc(idx_ready, 1)
                        assert k.n == N_T, k.n

                    return [lambda: x1(0), lambda: x1(1), token, lambda: stats(0), lambda: stats(1), lambda: stats(2),
                            lambda: stats(3), mean, scalars, logits, differ, candidates, least, one_hot, total, inverse,
                            score, ranks, slot_sum, slot_ints]

                TAIL_DVE = ((1, 1), (1, 5), (1, 5), (1, 7), (1, 7), (1, 9), (1, 9), (1, 11), (1, 13), (2, 8), (2, 9), (2, 10),
                            (2, 10), (2, 11), (2, 14), (2, 14), (2, 15), (3, 3), (3, 4), (3, 5))
                SUMS = {4: 0, 5: 1, 6: 2, 7: 3, 8: 4, 9: 5, 10: 6, 11: 7}

                def body(b, first, last):
                    parts = None if first else tail(b - 1)
                    assert first or len(parts) == len(TAIL_DVE)
                    for q in range(QUADS):
                        n = b * QUADS + q
                        for u in range(16):
                            if u == 8 and not (last and q == QUADS - 1):
                                shift(n + 1)
                            a = ahead(q, u, last)
                            if a:
                                d, h, unit = a
                                for k in range(2):
                                    maxima(32 * n + 48 + 2 * u + k, h, unit + k)
                            if q == 0 and u in SUMS and not first:
                                sums(b - 1, SUMS[u])
                            if not first:
                                for part, place in zip(parts, TAIL_DVE):
                                    if place == (q, u):
                                        part()

                def pad_rows():
                    dve.wait_ge(tl_out, N_TL * B)
                    dve.tensor_copy(padi[:], c["run"][0:1, :]).then_inc(pad_ready, 1)

                def tile_tables():
                    k = Count(step)
                    k.add(dve.tensor_tensor(cf[:], c["run"][0:1, :], c["base"][0:1, :], ALU.subtract))
                    k.wait(dve)
                    k.add(dve.tensor_scalar(nt[:], cf[:], float(P - 1), None, ALU.add))
                    k.wait(dve)
                    k.add(dve.tensor_copy(ci[:], nt[:]))
                    k.wait(dve)
                    k.add(dve.tensor_scalar(ci[:], ci[:], 7, None, ALU.arith_shift_right))
                    k.wait(dve)
                    k.add(dve.tensor_copy(nt[:], ci[:]))
                    k.wait(dve)
                    k.add(dve.tensor_tensor_scan(end[:], ones[:], nt[:], 0.0, ALU.mult, ALU.add))
                    k.add(dve.tensor_scalar(skip[:], nt[:], -float(P), float(CAP), ALU.mult, ALU.add))
                    k.wait(dve)
                    k.add(dve.tensor_scalar(end[:], end[:], float(P), None, ALU.mult))
                    k.wait(dve)
                    k.add(dve.tensor_tensor(ge, c["tf"][:].unsqueeze(2).to_broadcast([1, TILES, E]),
                                            end[:].unsqueeze(1).to_broadcast([1, TILES, E]), ALU.is_ge))
                    k.wait(dve)
                    k.add(dve.tensor_reduce(te[:], ge, AX.X, ALU.add))
                    k.add(dve.tensor_tensor(gs, ge, skip[:].unsqueeze(1).to_broadcast([1, TILES, E]), ALU.mult))
                    k.wait(dve)
                    k.add(dve.tensor_scalar(te[:], te[:], float(E - 1), None, ALU.min))
                    k.add(dve.tensor_reduce(tr[:], gs, AX.X, ALU.add))
                    k.wait(dve)
                    k.add(dve.tensor_tensor(tr2[:], tr[:], c["tf"][:], ALU.add))
                    k.wait(dve)
                    k.add(dve.tensor_scalar(tr2[:], tr2[:], float(DUMMY), None, ALU.min))
                    k.wait(dve)
                    dve.tensor_copy(c["tile_e"][:], te[:])
                    dve.tensor_scalar(c["tile_w"][:], te[:], float(WIDE), None, ALU.mult)
                    dve.tensor_copy(c["tile_r"][:], tr2[:])

                iterate(dve, body)
                for part in range(8):
                    sums(B - 1, part)
                parts = tail(B - 1)
                for k, f in enumerate(parts):
                    if k == 0:
                        low_w1(dve, c, 0, w1_hi).then_inc(w1_lo[0], 1)
                    if k == 9:
                        low_w1(dve, c, 2, w1_hi)
                    f()
                    if k == len(parts) - 3:
                        pad_rows()
                tile_tables()
                low_w1(dve, c, 3, w1_hi)

            @block.scalar
            def _(act):
                act.wait_ge(shift_tr, 1)
                act.activation(mT[0][:], psM[0:MROWS, :], ACT.Copy).then_inc(shift_out, 1)
                act.wait_ge(b1_tr, 1)
                act.activation(c["b1T"][:], psM[:, 0:E * FC], ACT.Copy).then_inc(b1_out, 1)

                def tail_copy(tb, j):
                    if j in (4, 5):
                        act.wait_ge(chain, N_T * tb + C_SCAL)
                        for n in range(2 * (j - 4), 2 * (j - 4) + 2):
                            ins = act.activation(xres[:, n, :], row[:, n, 0:D], ACT.Identity, bias=row[:, n, D + 1:D + 2],
                                                 scale=row[:, n, D:D + 1])
                        ins.then_inc(hn_done, 1)
                    if j == 0 or j == 1:
                        act.wait_ge(tl_done, N_TL * tb + 3 + j)
                        act.activation(hT[:, j, :], psM[:], ACT.Copy).then_inc(tl_out, 1)
                    if j == 2:
                        act.wait_ge(tl_done, N_TL * tb + 5)
                        act.activation(redT[:], psM[0:GD, :], ACT.Copy).then_inc(tl_out, 1)
                    if j == 3:
                        act.wait_ge(chain, N_T * tb + C_DIF)
                        act.activation(ex[:], dif[:], ACT.Exp).then_inc(ex_done, 1)

                TAIL_ACT = {(1, 14): 4, (1, 15): 5, (2, 2): 0, (2, 4): 1, (2, 6): 2, (2, 12): 3}

                def body(b, first, last):
                    for q in range(QUADS):
                        n = b * QUADS + q
                        for g in range(4):
                            for h in range(HQ):
                                u = 4 * g + h
                                act.wait_ge(s_done, 16 * n + u + 1)
                                if not (first and q == 0 and g < 2):
                                    wait(act, pv_done, 4 * n + g - 1)
                                act.activation(pr[g % 2][:, h, 0:width(g)], psS[u % 2][:, 0:width(g)], ACT.Exp).then_inc(exp_done, 1)
                                if u == 2 and not (first and q == 0):
                                    act.wait_ge(pv_done, 4 * n)
                                    if q == 1 and not first:
                                        act.wait_ge(ot_done, QUADS * b)
                                    if q >= 2 and not first:
                                        act.wait_ge(tl_done, N_TL * (b - 1) + 2)
                                    act.activation(raw[(q - 1) % QUADS][:], psO[:], ACT.Copy).then_inc(o_out, 1)
                                if u == 11 and not (last and q == QUADS - 1):
                                    nn, qq = n + 1, (q + 1) % QUADS
                                    act.wait_ge(shift_tr, nn + 1)
                                    wait(act, shift_in, 16 * n)
                                    act.activation(mT[qq % 2][:], psM[0:MROWS, :], ACT.Copy).then_inc(shift_out, 1)
                                if not first and (q, u) in TAIL_ACT:
                                    tail_copy(b - 1, TAIL_ACT[q, u])

                iterate(act, body)
                act.wait_ge(pv_done, 4 * B * QUADS)
                act.activation(raw[QUADS - 1][:], psO[:], ACT.Copy).then_inc(o_out, 1)
                for w in range(2):
                    high_w1(act, c, w, w1_in, w1_hi)
                high_w1(act, c, 2, w1_in, w1_hi)
                for j in (4, 5, 0, 1):
                    tail_copy(B - 1, j)
                high_w1(act, c, 3, w1_in, w1_hi)
                for j in (2, 3):
                    tail_copy(B - 1, j)

            @block.tensor
            def _(pe):
                def row_scores(w, q, h, unit):
                    i, lo, nk = list(row_units(h))[unit]
                    ps = max_bank(w, unit)
                    wait(pe, max_done, w - 3 if isinstance(w, int) and w < PRO else w - 1)
                    causal = lo > 0
                    ins = pe.matmul(ps[:, 0:nk], qs[q][0:SROWS, h, i * P:(i + 1) * P], ks[q][0:SROWS, h, lo:lo + nk],
                                    start=True, stop=not causal)
                    if causal:
                        ins = pe.matmul(ps[:, nk - P:nk], c["identb"][:], c["mask_q"][:], start=False, stop=True)
                    ins.then_inc(a_done, 1)

                def shift_rows(n):
                    pe.wait_ge(shift_made, N_M * (n + 1))
                    for i in range(NB):
                        ins = pe.matmul(psM[0:MROWS, i * P:(i + 1) * P], mp[:, i].rearrange("p a h -> p (a h)"), c["identb"][:],
                                        start=True, stop=True)
                    ins.then_inc(shift_tr, 1)

                def key_scores(n, q, g, h, tile0):
                    u = 4 * g + h
                    if not (tile0 and u < 2):
                        wait(pe, exp_done, 16 * n + u - 1)
                    ps = psS[u % 2]
                    for kb, q0, at in spans(g):
                        nq = T - q0
                        causal = kb >= NB
                        ins = pe.matmul(ps[:, at:at + nq], ks[q][0:SROWS + MROWS, h, kb * P:(kb + 1) * P],
                                        qs[q][0:SROWS + MROWS, h, q0:T], start=True, stop=not causal)
                        if causal:
                            ins = pe.matmul(ps[:, at:at + P], c["identb"][:], c["mask_k"][:], start=False, stop=True)
                    ins.then_inc(s_done, 1)

                def values(n, q, g, parts=(0, 1)):
                    pe.wait_ge(exp_done, 16 * n + 4 * g + 4)
                    for kb, q0, at in [spans(g)[k] for k in parts]:
                        for h in range(HQ):
                            ins = pe.matmul(psO[32 * h:32 * h + 32, q0:T], vq[q][:, kb, h, :], pr[g % 2][:, h, at:at + T - q0],
                                            start=kb == 0, stop=kb == KB - 1)
                    if parts[-1] == 1:
                        ins.then_inc(pv_done, 1)

                def tail(tb, j, part=None):
                    if j > 0 and part != 1:
                        pe.wait_ge(tl_out, N_TL * tb + j)
                    if j < 2:
                        pe.wait_ge(ot_done, QUADS * tb + QUADS)
                        for n in range(2) if part is None else [part]:
                            for q in range(QUADS):
                                ins = pe.matmul(psM[:, n * D:(n + 1) * D], ot[q][:, (2 * j + n) * P:(2 * j + n + 1) * P],
                                                c["wout"][:, q, :], start=q == 0, stop=q == QUADS - 1)
                    elif j < 4:
                        pe.wait_ge(hn_done, 2 * tb + 2)
                        for n in range(NB):
                            ins = pe.transpose(psM[:, n * P:(n + 1) * P], xres[:, n, (j - 2) * P:(j - 1) * P], c["ident"][:])
                    elif j == 4:
                        for k in range(KC):
                            ins = pe.matmul(psM[0:GD, :], c["wred"][:, k, :], hT[:, k, :], start=k == 0, stop=k == KC - 1)
                    elif j == 5:
                        for n in range(NB):
                            ins = pe.matmul(psM[:, n * E:(n + 1) * E], redT[:, n * P:(n + 1) * P], c["wgT"][:], start=True, stop=True)
                    else:
                        pe.wait_ge(chain, N_T * tb + C_OH)
                        o = oh[:].rearrange("p n e -> p (n e)")
                        pe.matmul(psM[:, 0:NB * E], c["before"][:], o, start=True, stop=False, skip_group_check=True)
                        for m in range(1, NB):
                            pe.matmul(psM[:, m * E:NB * E], c["onesb"][:], o[:, 0:(NB - m) * E], start=False, stop=False,
                                      skip_group_check=True)
                        for m in range(NB):
                            ins = pe.matmul(psM[:, NB * E:NB * E + E], c["onesb"][:], o[:, m * E:(m + 1) * E], start=False,
                                            stop=m == NB - 1, skip_group_check=True)
                    if part != 0:
                        ins.then_inc(tl_done, 1)

                TAIL_PE = {(0, 14): (0, 0), (1, 0): (0, 1), (1, 2): (1, 0), (1, 4): (1, 1), (2, 1): (2,), (2, 3): (3,), (2, 5): (4,),
                           (2, 7): (5,), (3, 1): (6,)}

                for w in range(PRO):
                    if w == 0:
                        pe.wait_ge(stk_in[0], 16 * 2 * TERMS)
                    if w == 32:
                        pe.wait_ge(stk_in[1], 16 * 2 * TERMS)
                    row_scores(w, w // 32, w // 8 % HQ, w % 8)
                shift_rows(0)
                pe.wait_ge(bias_in, 16)
                pe.wait_ge(shift_out, 1)
                pe.transpose(psM[:, 0:E * FC], b1n, c["ident"][0:E * FC, 0:E * FC]).then_inc(b1_tr, 1)
                pe.wait_ge(b1_out, 1)

                def rows(n, q, u, k, b, last):
                    a = ahead(q, u, last)
                    if a:
                        d, h, unit = a
                        ahead_q = (q + d) % QUADS
                        if u == 8 and k == 0:
                            pe.wait_ge(stk_in[ahead_q], 16 * 2 * TERMS * (b + 1 + (q + d) // QUADS))
                        row_scores(32 * n + 48 + 2 * u + k, ahead_q, h, unit + k)

                def body(b, first, last):
                    done = 0
                    for q in range(QUADS):
                        n = b * QUADS + q
                        tile0 = first and q == 0
                        pe.wait_ge(shift_in, 16 * (n + 1))
                        for g in range(4):
                            for h in range(HQ):
                                u = 4 * g + h
                                if h % 2 and (g > 0 or h == 1):
                                    key_scores(n, q, g, h, tile0)
                                    rows(n, q, u, 0, b, last)
                                    rows(n, q, u, 1, b, last)
                                else:
                                    rows(n, q, u, 0, b, last)
                                    key_scores(n, q, g, h, tile0)
                                    rows(n, q, u, 1, b, last)
                                if h == 1:
                                    if g == 0 and not tile0:
                                        values(n - 1, (q - 1) % QUADS, 3)
                                    if g == 1:
                                        pe.wait_ge(v_in[q], 16 * (b + 1))
                                        wait(pe, o_out, n)
                                if g > 0 and h in (1, 3):
                                    values(n, q, g - 1, (h // 2,))
                                if u == 11 and not (last and q == QUADS - 1):
                                    pe.wait_ge(shift_out, n + 1)
                                    if not first:
                                        pe.wait_ge(tl_out, N_TL * (b - 1) + done)
                                    shift_rows(n + 1)
                                if not first and (q, u) in TAIL_PE:
                                    pe.wait_ge(shift_out, n + 2 if u > 11 else n + 1)
                                    tail(b - 1, *TAIL_PE[q, u])
                                    done = TAIL_PE[q, u][0] + 1

                iterate(pe, body)
                values(B * QUADS - 1, QUADS - 1, 3)
                for j in range(N_TL):
                    tail(B - 1, j)


def setup(nc, c, g_x, g_f, wout, bout, w_red, wg):
    with ExitStack() as s:
        def sb(name, shape, dt):
            return s.enter_context(nc.sbuf_tensor(name, shape, dt))

        def sem(name):
            return s.enter_context(nc.semaphore(name))

        gates = sb("gates", [P, 2], F32)
        wg_s = sb("wg_s", [E, GD], F32)
        wsq = sb("wsq", [E, GD], F32)
        wn = sb("wn", [E, 1], F32)
        wn2 = sb("wn2", [E, 1], F32)
        wn3 = sb("wn3", [E, 1], F32)
        wgn = sb("wgn", [E, GD], F32)
        ints = sb("ints", [P, 64], I32)
        ints_t = sb("ints_t", [1, TILES], I32)
        tg = sb("tg", [P, 2], F32)
        ps = s.enter_context(nc.psum_tensor("ps_setup", [P, 512], F32))
        sel_set = sem("sel_set")
        load, wload, cleared, built, ints_set, tanh_done, step, norm_done, scaled, tr = (
            sem(n) for n in ("g_load", "w_load", "cleared", "built", "ints_set", "tanh_done", "step", "wg_norm", "scaled", "wg_tr"))
        with nc.Block() as block:
            @block.sync
            def _(sp):
                sp.dma_start(gates[:, 0:1], g_x.rearrange("(a n) -> a n", a=1).to_broadcast([P, 1])).then_inc(load, 16)
                sp.dma_start(gates[:, 1:2], g_f.rearrange("(a n) -> a n", a=1).to_broadcast([P, 1])).then_inc(load, 16)
                sp.dma_start(wg_s[:], wg).then_inc(load, 16)
                sp.dma_start(c["wred"][:], w_red.rearrange("(k p) n -> p k n", p=P)).then_inc(load, 16)
                sp.wait_ge(cleared, 1)
                for h in range(HQ):
                    sp.dma_start(c["wout"][32 * h:32 * h + DH, :, :],
                                 wout.rearrange("(q h d) n -> h d q n", q=QUADS, h=HQ)[h]).then_inc(wload, 16)
                sp.dma_start(c["wout"][DH:DH + 1, 0, :], bout.rearrange("(a n) -> a n", a=1)).then_inc(wload, 16)
                sp.wait_ge(wload, 16 * (HQ + 1))
                sp.wait_ge(load, 64)

            @block.gpsimd
            def _(pool):
                pool.memset(c["ident"][:], 0.0).then_inc(built, 1)
                pool.memset(c["identb"][:], 0.0).then_inc(built, 1)
                pool.memset(c["mask_q"][:], 0.0).then_inc(built, 1)
                pool.memset(c["mask_k"][:], 0.0).then_inc(built, 1)
                pool.memset(c["before"][:], 1.0).then_inc(built, 1)
                pool.memset(c["onesb"][:], 1.0)
                pool.memset(c["mhalf"][:], -0.5).then_inc(built, 1)
                pool.wait_ge(built, 6)
                for m in (c["ident"], c["identb"]):
                    pool.affine_select(out=m[:], in_=m[:], compare_op=ALU.not_equal, fill=1.0, base=0,
                                       pattern=[[-1, P]], channel_multiplier=1).then_inc(built, 1)
                pool.affine_select(out=c["mask_q"][:], in_=c["mask_q"][:], compare_op=ALU.is_ge, fill=MASKED, base=0,
                                   pattern=[[-1, P]], channel_multiplier=1)
                pool.affine_select(out=c["mask_k"][:], in_=c["mask_k"][:], compare_op=ALU.is_ge, fill=MASKED, base=0,
                                   pattern=[[1, P]], channel_multiplier=-1)
                pool.affine_select(out=c["before"][:], in_=c["before"][:], compare_op=ALU.is_gt, fill=0.0, base=0,
                                   pattern=[[1, P]], channel_multiplier=-1)
                pool.iota(ints[:, 0:NB * E], pattern=[[0, NB], [1, E]], base=0, channel_multiplier=0).then_inc(ints_set, 1)
                pool.iota(ints[:, 32:40], pattern=[[CAP, E]], base=0, channel_multiplier=0).then_inc(ints_set, 1)
                pool.iota(ints[:, 40:40 + NB], pattern=[[P, NB]], base=0, channel_multiplier=1).then_inc(ints_set, 1)
                pool.iota(ints_t[:], pattern=[[P, TILES]], base=0, channel_multiplier=0).then_inc(ints_set, 1)
                v = c["sel"][:]
                pool.memset(v, 0.0).then_inc(sel_set, 1)
                for m in range(2):
                    pool.wait_ge(sel_set, m + 1)
                    pool.affine_select(out=v, in_=v, compare_op=ALU.not_equal, fill=1.0, base=-SROWS - HQ * m,
                                       pattern=[[-1, HQ]], channel_multiplier=1).then_inc(sel_set, 1)
                pool.wait_ge(sel_set, 3)
                pool.wait_ge(norm_done, 1)
                pool.tensor_tensor(wn2[:], wn[:], c["half"][0:E, 0:1], ALU.pow).then_inc(norm_done, 1)

            @block.vector
            def _(dve):
                dve.memset(c["half"][:], 0.5)
                dve.memset(c["wout"][:], 0.0).then_inc(cleared, 1)
                dve.wait_ge(ints_set, 4)
                dve.tensor_copy(c["tf"][:], ints_t[:])
                dve.tensor_copy(c["eiota"][:].rearrange("p n e -> p (n e)"), ints[:, 0:NB * E])
                dve.tensor_copy(c["run"][:], ints[:, 32:40])
                dve.tensor_copy(c["base"][:], ints[:, 32:40])
                dve.tensor_copy(c["tokf"][:], ints[:, 40:40 + NB])
                dve.wait_ge(load, 64)
                dve.tensor_tensor(wsq[:], wg_s[:], wg_s[:], ALU.mult).then_inc(step, 1)
                dve.wait_ge(step, 1)
                dve.tensor_reduce(wn[:], wsq[:], AX.X, ALU.add).then_inc(norm_done, 1)
                dve.wait_ge(norm_done, 2)
                dve.tensor_scalar(wn3[:], wn2[:], 1e-4, None, ALU.max).then_inc(step, 1)
                dve.wait_ge(step, 2)
                dve.reciprocal(wn[:], wn3[:]).then_inc(step, 1)
                dve.wait_ge(step, 3)
                dve.tensor_scalar(wgn[:], wg_s[:], wn[:, 0:1], None, ALU.mult).then_inc(scaled, 1)
                dve.wait_ge(tanh_done, 1)
                dve.tensor_copy(c["tgf"][:], tg[:, 1:2])
                dve.wait_ge(wload, 16 * (HQ + 1))
                dve.tensor_scalar(c["wout"][:].rearrange("p q n -> p (q n)"), c["wout"][:].rearrange("p q n -> p (q n)"),
                                  tg[:, 0:1], None, ALU.mult)
                dve.wait_ge(tr, 1)
                dve.tensor_copy(c["wgT"][:], ps[0:GD, 0:E])

            @block.scalar
            def _(act):
                act.wait_ge(load, 64)
                act.activation(tg[:], gates[:], ACT.Tanh).then_inc(tanh_done, 1)

            @block.tensor
            def _(pe):
                pe.wait_ge(scaled, 1)
                pe.wait_ge(built, 8)
                pe.transpose(ps[0:GD, 0:E], wgn[:], c["ident"][0:E, 0:E]).then_inc(tr, 1)


def experts(nc, c, b2, rows_d, out):
    out_d = out.rearrange("b t d -> (b t) d")
    U = 4
    with ExitStack() as s:
        def sb(name, shape, dt):
            return s.enter_context(nc.sbuf_tensor(name, shape, dt))

        def sem(name):
            return s.enter_context(nc.semaphore(name))

        W1, W2, b1T = c["W1"], c["W2"], c["b1T"]
        b2b = sb("b2b", [P, E * D], F32)
        row = [sb(f"frow{r}", [P, ROW], F32) for r in range(U)]
        res = [sb(f"res{r}", [P, D], F32) for r in range(U)]
        ids = [sb(f"ids{r}", [P, 1], U32) for r in range(U)]
        hn = [sb(f"fhn{p}", [P, D], F32) for p in range(2)]
        hh = [sb(f"hh{p}", [P, KC, 2, P], BF16) for p in range(2)]
        g = [sb(f"g{p}", [P, FC, P], F32) for p in range(2)]
        gh = [sb(f"gh{p}", [P, FC, P], BF16) for p in range(2)]
        gl = [sb(f"gl{p}", [P, FC, P], BF16) for p in range(2)]
        y = sb("y", [P, D], F32)
        psT = [s.enter_context(nc.psum_tensor(f"fT{p}", [P, 512], F32)) for p in range(2)]
        psH = [s.enter_context(nc.psum_tensor(f"fH{p}", [P, 4, P], F32)) for p in range(4)]
        psY = [s.enter_context(nc.psum_tensor(f"fY{p}", [P, 512], F32)) for p in range(2)]
        row_in, stored = ([sem(f"{n}{r}") for r in range(U)] for n in ("row_in", "stored"))
        bias_in = sem("b2_in")
        (hn_done, tr_done, hi_out, lo_out, h_done, g_done, ghi_done, glo_done, y_done, y_sum, res_done, passed_pool) = (
            sem(n) for n in ("hn_done", "tr_done", "hi_out", "lo_out", "h_done", "g_done", "ghi_done", "glo_done",
                             "y_done", "y_sum", "res_done", "passed_pool3"))

        def tiles(eng, body):
            for r in range(U):
                body(0, r)
            with eng.Fori(1, TILES // U - 1) as i:
                for r in range(U):
                    body(i, r)
            for r in range(U):
                body(TILES // U - 1, r)

        def ahead(i, r, k):
            i, r = (i + 1, r + k - U) if r + k >= U else (i, r + k)
            return None if isinstance(i, int) and i >= TILES // U else (i, r)

        def expert_of(eng, t):
            return eng.value_load(c["tile_e"][0:1, bass.ds(t, 1)], min_val=0, max_val=E - 1)

        with nc.Block() as block:
            @block.sync
            def _(sp):
                def body(i, r):
                    t = U * i + r
                    wait(sp, res_done, t - U + 1)
                    first_row = sp.value_load(c["tile_r"][0:1, bass.ds(t, 1)], min_val=0, max_val=DUMMY)
                    sp.dma_start(row[r][:], rows_d[bass.ds(first_row, P), :]).then_inc(row_in[r], 16)
                    if isinstance(i, int) and (i, r) == (0, 1):
                        sp.dma_start(b2b[:], b2.rearrange("(a e) d -> a (e d)", a=1).to_broadcast([P, E * D])).then_inc(bias_in, 16)

                tiles(sp, body)

            @block.gpsimd
            def _(pool):
                def body(i, r):
                    pool.wait_ge(res_done, U * i + r + 1)
                    pool.sem_inc(passed_pool, 1)
                    pool.indirect_dma_start(out_d, bass.IndirectOffsetOnAxis(ap=ids[r][:, 0:1], axis=0), res[r][:], None,
                                            bounds_check=TOK - 1, oob_is_err=False).then_inc(stored[r], 16)

                tiles(pool, body)
                for r in range(U):
                    pool.wait_ge(stored[r], 16 * (TILES // U))

            @block.scalar
            def _(act):
                def high(i, r):
                    act.wait_ge(tr_done, U * i + r + 1)
                    act.activation(hh[r % 2][:, :, 0, :], psT[r % 2][:, 0:D].rearrange("p (k n) -> p k n", k=KC),
                                   ACT.Copy).then_inc(hi_out, 1)

                def gelu(e, i, r, j):
                    act.wait_ge(h_done, 2 * (U * i + r) + j + 1)
                    for k in range(4):
                        f = 4 * j + k
                        ins = act.activation(g[r % 2][:, f, :], psH[2 * (r % 2) + j][:, k, :], ACT.Gelu,
                                             bias=b1T[:, bass.ds(e * FC + f, 1)])
                    ins.then_inc(g_done, 1)

                def body(i, r):
                    e = expert_of(act, U * i + r)
                    gelu(e, i, r, 0)
                    after = ahead(i, r, 1)
                    if after:
                        high(*after)
                    gelu(e, i, r, 1)

                high(0, 0)
                tiles(act, body)

            @block.vector
            def _(dve):
                def norm(i, r):
                    dve.wait_ge(row_in[r], 16 * (i + 1))
                    dve.tensor_scalar(hn[r % 2][:], row[r][:, 0:D], row[r][:, D:D + 1], row[r][:, D + 1:D + 2],
                                      ALU.mult, ALU.add).then_inc(hn_done, 1)

                def low(i, r):
                    dve.wait_ge(hi_out, U * i + r + 1)
                    dve.tensor_tensor(hh[r % 2][:, :, 1, :], psT[r % 2][:, 0:D].rearrange("p (k n) -> p k n", k=KC),
                                      hh[r % 2][:, :, 0, :], ALU.subtract).then_inc(lo_out, 1)

                def split_g(i, r, j):
                    half, p = slice(4 * j, 4 * j + 4), r % 2
                    n = 2 * (U * i + r) + j + 1
                    dve.wait_ge(g_done, n)
                    dve.tensor_copy(gh[p][:, half, :], g[p][:, half, :]).then_inc(ghi_done, 1)
                    dve.wait_ge(ghi_done, n)
                    dve.tensor_tensor(gl[p][:, half, :], g[p][:, half, :], gh[p][:, half, :], ALU.subtract).then_inc(glo_done, 1)

                def result(i, r):
                    t = U * i + r
                    e = expert_of(dve, t)
                    if isinstance(t, int) and t == 0:
                        dve.wait_ge(bias_in, 16)
                    dve.wait_ge(y_done, t + 1)
                    wait(dve, res_done, t)
                    dve.tensor_tensor(y[:], psY[r % 2][:, 0:D], b2b[:, bass.ds(e * D, D)], ALU.add).then_inc(y_sum, 1)
                    dve.wait_ge(y_sum, t + 1)
                    wait(dve, stored[r], 16 * i)
                    dve.tensor_copy(ids[r][:], row[r][:, D + 3:D + 4].bitcast(U32))
                    dve.scalar_tensor_tensor(res[r][:], y[:], row[r][:, D + 2:D + 3], row[r][:, 0:D],
                                             ALU.mult, ALU.add).then_inc(res_done, 1)

                def body(i, r):
                    after = ahead(i, r, 1)
                    if after:
                        low(*after)
                    split_g(i, r, 0)
                    split_g(i, r, 1)
                    after = ahead(i, r, 2)
                    if after:
                        norm(*after)
                    if r > 0:
                        result(i, r - 1)
                    elif not isinstance(i, int) or i > 0:
                        result(i - 1, U - 1)

                norm(0, 0)
                norm(0, 1)
                low(0, 0)
                tiles(dve, body)
                result(TILES // U - 1, U - 1)

            @block.tensor
            def _(pe):
                def rows_T(i, r):
                    pe.wait_ge(hn_done, U * i + r + 1)
                    for k in range(KC):
                        ins = pe.transpose(psT[r % 2][:, k * P:(k + 1) * P], hn[r % 2][:, k * P:(k + 1) * P], c["ident"][:])
                    ins.then_inc(tr_done, 1)

                def hidden(at, r, j):
                    p = r % 2
                    for k in range(4):
                        f, n = 4 * j + k, 0
                        for kc in range(KC):
                            for a, b in ((0, 0), (0, 1), (1, 0)):
                                n += 1
                                ins = pe.matmul(psH[2 * p + j][:, k, :],
                                                W1[:, bass.ds(at + (kc * 2 + a) * FF + f * P, P)],
                                                hh[p][:, kc, b, :], start=n == 1, stop=n == 3 * KC)
                    ins.then_inc(h_done, 1)

                def model(at, i, r):
                    t, p = U * i + r, r % 2
                    for f in range(FC):
                        if f % 4 == 0:
                            pe.wait_ge(glo_done, 2 * t + f // 4 + 1)
                        for m, (a, b) in enumerate(((0, 0), (0, 1), (1, 0))):
                            ins = pe.matmul(psY[p][:, 0:D], (gl if b else gh)[p][:, f, :],
                                            W2[:, bass.ds(at + (f * 2 + a) * D, D)],
                                            start=f == 0 and m == 0, stop=f == FC - 1 and m == 2)
                    ins.then_inc(y_done, 1)

                def body(i, r):
                    last_at = None
                    if r == 0:
                        before = 0 if isinstance(i, int) and i == 0 else 1
                        _, found = nc.values_load_multi_w_load_instructions(
                            c["tile_w"][0:1, bass.ds(U * i - before, U + before)], [mybir.EngineType.PE],
                            min_val=0, max_val=(E - 1) * WIDE)
                        places[:] = found[before:]
                        if before:
                            last_at = found[0]
                    else:
                        last_at = places[r - 1]
                    at = places[r]
                    pe.wait_ge(lo_out, U * i + r + 1)
                    hidden(at, r, 0)
                    after = ahead(i, r, 1)
                    if after:
                        rows_T(*after)
                    hidden(at, r, 1)
                    if r > 0:
                        model(last_at, i, r - 1)
                    elif last_at is not None:
                        model(last_at, i - 1, U - 1)

                places = [None] * U
                rows_T(0, 0)
                tiles(pe, body)
                model(places[U - 1], TILES // U - 1, U - 1)


def build(nc, x, ctx_1024, g_xattn, g_ffn, wq, wkv, wout, bout, w_red, wg, w1, b1, w2, b2, out):
    parts_d = nc.dram_tensor("qk_parts", (B, HALVES, 3, P, COLS), BF16, kind="Internal").ap()
    v_d = nc.dram_tensor("v_quads", (B, P, QUADS * KB * HQ * 32), F32, kind="Internal").ap()
    rows_d = nc.dram_tensor("sorted_rows", (DUMMY + P, ROW), F32, kind="Internal").ap()
    with ExitStack() as s:
        c = {}
        for name, shape, dt in (("ident", [P, P], F32), ("identb", [P, P], BF16), ("mask_q", [P, P], BF16),
                                ("mask_k", [P, P], BF16), ("before", [P, P], BF16), ("onesb", [P, P], BF16),
                                ("mhalf", [P, NB], F32), ("half", [P, 1], F32), ("eiota", [P, NB, E], F32),
                                ("run", [P, E], F32), ("base", [P, E], F32), ("tokf", [P, NB], F32),
                                ("wred", [P, KC, GD], F32), ("wout", [P, QUADS, D], F32), ("wgT", [GD, E], F32),
                                ("tgf", [P, 1], F32), ("tf", [1, TILES], F32), ("b1T", [P, E * FC], F32), ("tile_e", [1, TILES], I32), ("tile_w", [1, TILES], I32), ("tile_r", [1, TILES], I32)):
            c[name] = s.enter_context(nc.sbuf_tensor(name, shape, dt))
        c["W1"] = s.enter_context(nc.sbuf_tensor("W1", [P, E * KC * 2 * FF], BF16))
        ar = Arena(s, nc, c)
        c["sel"] = s.enter_context(nc.sbuf_tensor("sel", [P, HQ], BF16))
        setup(nc, c, g_xattn, g_ffn, wout, bout, w_red, wg)
        project(nc, c, ar, x, ctx_1024, wq, wkv, parts_d, v_d)
        c["W2"] = s.enter_context(nc.sbuf_tensor("W2", [P, E * FC * 2 * D], BF16))
        for p in range(2):
            c[f"wide{p}"] = s.enter_context(nc.sbuf_tensor(f"wide{p}", [P, HQ * 1024], F32))
        attend(nc, c, ar, x, w1, b1, w2, parts_d, v_d, rows_d)
        experts(nc, c, b2, rows_d, out)


_INS = ['x', 'ctx_1024', 'g_xattn', 'g_ffn', 'L0_xattn_Wq', 'L0_xattn_Wkv', 'L0_xattn_Wout', 'L0_xattn_bout',
        'L0_ffn_w_red', 'L0_ffn_wg', 'L0_ffn_w1', 'L0_ffn_b1', 'L0_ffn_w2', 'L0_ffn_b2']


def kernel(**inputs):
    import numpy as _np
    import concourse.bacc as _bacc
    from concourse import mybir as _mybir
    from concourse.bass_utils import run_bass_kernel_spmd as _run

    nc = _bacc.Bacc("TRN2", target_bir_lowering=False, num_devices=1)
    arrays, args = {}, []
    for name in _INS:
        a = _np.ascontiguousarray(inputs[name])
        arrays[f"in_{name}_dram"] = a
        args.append(nc.dram_tensor(f"in_{name}_dram", a.shape, _mybir.dt.from_np(a.dtype), kind="ExternalInput").ap())
    out = nc.dram_tensor("out_0_dram", (B, T, D), _mybir.dt.float32, kind="ExternalOutput").ap()
    build(nc, *args, out)
    r = _run(nc, [arrays], core_ids=[0])
    return r.results[0]["out_0_dram"]
```
